# Optimizing a Trainium2 kernel written in Bass

```python
import numpy as np
import jax
import jax.numpy as jnp

def _softmax(x, axis=-1):
    return jax.nn.softmax(x, axis=axis)

def _gelu(x):
    return jax.nn.gelu(x, approximate=True)

def _silu(x):
    return jax.nn.silu(x)

def _sigmoid(x):
    return jax.nn.sigmoid(x)

def _layernorm(x, axis=-1, eps=1e-05):
    m = jnp.mean(x, axis=axis, keepdims=True)
    v = jnp.var(x, axis=axis, keepdims=True)
    return (x - m) / jnp.sqrt(v + eps)

def _scatter_add(tgt, idx, src, axis=0):
    return tgt.at[idx].add(src)

def _segment_sum(src, seg, n):
    return jax.ops.segment_sum(src, seg, n)
kernel_name = 'mk_vit_tower_cls_d1_tok_img768_r4_37ea9d'

def setup_inputs(seed: int=0):
    np.random.seed(seed)
    _w = jnp.asarray

    def _rec_inputs():
        import jax
        import jax.numpy as jnp
        _rk = jax.random.key(seed)
        x = -0.00040386 + 0.999972 * jax.random.normal(jax.random.fold_in(_rk, 1), (8, 3, 128, 128), jnp.float32)
        cls_tok = 0.02 * jax.random.normal(jax.random.fold_in(_rk, 5), (1, 1, 192), jnp.float32)
        return (x, cls_tok)
    x, cls_tok = _rec_inputs()

    def _L0_tok_setup():
        import jax, jax.numpy as jnp
        import numpy as np
        P = 16
        WIN = 64
        NH = 12

        def _layernorm(x, g, b, eps=1e-05):
            m = x.mean(-1, keepdims=True)
            v = ((x - m) ** 2).mean(-1, keepdims=True)
            return (x - m) * jax.lax.rsqrt(v + eps) * g + b

        def _sinusoidal_pe(n, d):
            pos = jnp.arange(n, dtype=jnp.float32)[:, None]
            i = jnp.arange(d // 2, dtype=jnp.float32)[None, :]
            ang = pos / jnp.power(10000.0, 2.0 * i / d)
            pe = jnp.zeros((n, d), jnp.float32)
            pe = pe.at[:, 0::2].set(jnp.sin(ang)).at[:, 1::2].set(jnp.cos(ang))
            return pe
        key = jax.random.key(seed)
        ks = jax.random.split(key, 8)
        B, C, H, W, D, F = (16, 3, 128, 128, 192, 768)
        s = lambda k, shape: jax.random.normal(k, shape, jnp.float32) * 0.02
        return {'input': jax.random.normal(ks[0], (B, C, H, W), jnp.float32), 'patch_w': s(ks[1], (D, C, P, P)), 'patch_b': jnp.zeros((D,), jnp.float32), 'ln_g': jnp.ones((D,), jnp.float32), 'ln_b': jnp.zeros((D,), jnp.float32), 'qkv_w': s(ks[2], (D, 3 * D)), 'qkv_b': jnp.zeros((3 * D,), jnp.float32), 'proj_w': s(ks[3], (D, D)), 'proj_b': jnp.zeros((D,), jnp.float32), 'ff1_w': s(ks[4], (D, F)), 'ff1_b': jnp.zeros((F,), jnp.float32), 'ff2_w': s(ks[5], (F, D)), 'ff2_b': jnp.zeros((D,), jnp.float32)}
    _L0_tok_all = _L0_tok_setup()
    _L0_tok_in = {k: v for k, v in _L0_tok_all.items() if k in ('patch_w', 'patch_b', 'ln_g', 'ln_b', 'qkv_w', 'qkv_b', 'proj_w', 'proj_b', 'ff1_w', 'ff1_b', 'ff2_w', 'ff2_b')}
    del _L0_tok_all

    def _L0_attn_setup():
        import jax, jax.numpy as jnp
        import numpy as np
        B, N, C, H = (8, 256, 192, 12)
        D = C // H
        M = 2 * D
        SCALE = D ** (-0.5)
        EPS = 1e-12

        def _feature_map(z, rand_matrix):
            logits = jnp.einsum('bhnd,hdm->bhnm', z, rand_matrix)
            sqnorm = 0.5 * jnp.sum(z * z, axis=-1, keepdims=True)
            return jnp.exp(logits - sqnorm) * M ** (-0.5)
        key = jax.random.key(seed)
        k1, k2, k3, k4, k5 = jax.random.split(key, 5)
        x = jax.random.normal(k1, (B, N, C), dtype=jnp.float32)
        qkv_w = jax.random.normal(k2, (3 * C, C), dtype=jnp.float32) * 0.02
        proj_w = jax.random.normal(k3, (C, C), dtype=jnp.float32) * 0.02
        proj_b = jax.random.normal(k4, (C,), dtype=jnp.float32) * 0.02
        rand_matrix = jax.random.normal(k5, (H, D, M), dtype=jnp.float32)
        return {'x': x, 'qkv_w': qkv_w, 'proj_w': proj_w, 'proj_b': proj_b, 'rand_matrix': rand_matrix}
    _L0_attn_all = _L0_attn_setup()
    _L0_attn_in = {k: v for k, v in _L0_attn_all.items() if k in ('qkv_w', 'proj_w', 'proj_b', 'rand_matrix')}
    del _L0_attn_all

    def _L0_ffn_setup():
        import jax, jax.numpy as jnp
        import numpy as np
        B, N, D, H, E, HID, TOPK = (8, 197, 192, 12, 8, 768, 2)

        def _layernorm(x, w, b, eps=1e-05):
            mu = jnp.mean(x, axis=-1, keepdims=True)
            var = jnp.mean((x - mu) ** 2, axis=-1, keepdims=True)
            return (x - mu) * jax.lax.rsqrt(var + eps) * w + b
        key = jax.random.key(seed)
        ks = jax.random.split(key, 8)
        s = 0.02
        return {'x': jax.random.normal(ks[0], (B, N, D), jnp.float32), 'norm1_w': jnp.ones((D,), jnp.float32), 'norm1_b': jnp.zeros((D,), jnp.float32), 'qkv_w': jax.random.normal(ks[1], (3 * D, D), jnp.float32) * s, 'qkv_b': jnp.zeros((3 * D,), jnp.float32), 'proj_w': jax.random.normal(ks[2], (D, D), jnp.float32) * s, 'proj_b': jnp.zeros((D,), jnp.float32), 'norm2_w': jnp.ones((D,), jnp.float32), 'norm2_b': jnp.zeros((D,), jnp.float32), 'w_gate': jax.random.normal(ks[3], (D, E), jnp.float32) * s, 'W1': jax.random.normal(ks[4], (E, D, HID), jnp.float32) * s, 'b1': jnp.zeros((E, HID), jnp.float32), 'W2': jax.random.normal(ks[5], (E, HID, D), jnp.float32) * s, 'b2': jnp.zeros((E, D), jnp.float32)}
    _L0_ffn_all = _L0_ffn_setup()
    _L0_ffn_in = {k: v for k, v in _L0_ffn_all.items() if k in ('norm1_w', 'norm1_b', 'qkv_w', 'qkv_b', 'proj_w', 'proj_b', 'norm2_w', 'norm2_b', 'w_gate', 'W1', 'b1', 'W2', 'b2')}
    del _L0_ffn_all
    return {'x': x, 'cls_tok': cls_tok, 'L0_tok_patch_w': _L0_tok_in['patch_w'], 'L0_tok_patch_b': _L0_tok_in['patch_b'], 'L0_tok_ln_g': _L0_tok_in['ln_g'], 'L0_tok_ln_b': _L0_tok_in['ln_b'], 'L0_tok_qkv_w': _L0_tok_in['qkv_w'], 'L0_tok_qkv_b': _L0_tok_in['qkv_b'], 'L0_tok_proj_w': _L0_tok_in['proj_w'], 'L0_tok_proj_b': _L0_tok_in['proj_b'], 'L0_tok_ff1_w': _L0_tok_in['ff1_w'], 'L0_tok_ff1_b': _L0_tok_in['ff1_b'], 'L0_tok_ff2_w': _L0_tok_in['ff2_w'], 'L0_tok_ff2_b': _L0_tok_in['ff2_b'], 'L0_attn_qkv_w': _L0_attn_in['qkv_w'], 'L0_attn_proj_w': _L0_attn_in['proj_w'], 'L0_attn_proj_b': _L0_attn_in['proj_b'], 'L0_attn_rand_matrix': _L0_attn_in['rand_matrix'], 'L0_ffn_norm1_w': _L0_ffn_in['norm1_w'], 'L0_ffn_norm1_b': _L0_ffn_in['norm1_b'], 'L0_ffn_qkv_w': _L0_ffn_in['qkv_w'], 'L0_ffn_qkv_b': _L0_ffn_in['qkv_b'], 'L0_ffn_proj_w': _L0_ffn_in['proj_w'], 'L0_ffn_proj_b': _L0_ffn_in['proj_b'], 'L0_ffn_norm2_w': _L0_ffn_in['norm2_w'], 'L0_ffn_norm2_b': _L0_ffn_in['norm2_b'], 'L0_ffn_w_gate': _L0_ffn_in['w_gate'], 'L0_ffn_W1': _L0_ffn_in['W1'], 'L0_ffn_b1': _L0_ffn_in['b1'], 'L0_ffn_W2': _L0_ffn_in['W2'], 'L0_ffn_b2': _L0_ffn_in['b2']}

def reference(x, cls_tok, L0_tok_patch_w, L0_tok_patch_b, L0_tok_ln_g, L0_tok_ln_b, L0_tok_qkv_w, L0_tok_qkv_b, L0_tok_proj_w, L0_tok_proj_b, L0_tok_ff1_w, L0_tok_ff1_b, L0_tok_ff2_w, L0_tok_ff2_b, L0_attn_qkv_w, L0_attn_proj_w, L0_attn_proj_b, L0_attn_rand_matrix, L0_ffn_norm1_w, L0_ffn_norm1_b, L0_ffn_qkv_w, L0_ffn_qkv_b, L0_ffn_proj_w, L0_ffn_proj_b, L0_ffn_norm2_w, L0_ffn_norm2_b, L0_ffn_w_gate, L0_ffn_W1, L0_ffn_b1, L0_ffn_W2, L0_ffn_b2):
    import jax
    import jax.numpy as jnp

    def _L0_tok_ref(input, patch_w, patch_b, ln_g, ln_b, qkv_w, qkv_b, proj_w, proj_b, ff1_w, ff1_b, ff2_w, ff2_b):
        import jax, jax.numpy as jnp
        import numpy as np
        P = 16
        WIN = 64
        NH = 12

        def _layernorm(x, g, b, eps=1e-05):
            m = x.mean(-1, keepdims=True)
            v = ((x - m) ** 2).mean(-1, keepdims=True)
            return (x - m) * jax.lax.rsqrt(v + eps) * g + b

        def _sinusoidal_pe(n, d):
            pos = jnp.arange(n, dtype=jnp.float32)[:, None]
            i = jnp.arange(d // 2, dtype=jnp.float32)[None, :]
            ang = pos / jnp.power(10000.0, 2.0 * i / d)
            pe = jnp.zeros((n, d), jnp.float32)
            pe = pe.at[:, 0::2].set(jnp.sin(ang)).at[:, 1::2].set(jnp.cos(ang))
            return pe
        B, C, H, W = input.shape
        D = patch_w.shape[0]
        dh = D // NH
        xp = input.reshape(B, C, H // P, P, W // P, P)
        x = jnp.einsum('bchpwq,dcpq->bhwd', xp, patch_w) + patch_b
        x = x.reshape(B, -1, D)
        x = _layernorm(x, ln_g, ln_b)
        N = x.shape[1]
        x = x + _sinusoidal_pe(N, D)

        def ff(y):
            return jax.nn.gelu(y @ ff1_w + ff1_b) @ ff2_w + ff2_b

        def sparse_attn(y):
            nW = N // WIN
            qkv = (y @ qkv_w + qkv_b).reshape(B, nW, WIN, 3, NH, dh)
            q, k, v = (qkv[:, :, :, 0], qkv[:, :, :, 1], qkv[:, :, :, 2])
            scores = jnp.einsum('bwqhd,bwkhd->bwhqk', q, k) * dh ** (-0.5)
            a = jax.nn.softmax(scores, axis=-1)
            o = jnp.einsum('bwhqk,bwkhd->bwqhd', a, v).reshape(B, N, D)
            return o @ proj_w + proj_b
        identity = x
        x = ff(x)
        x = sparse_attn(x)
        x = x + identity
        identity = x
        x = ff(x)
        x = x + identity
        return x

    def _L0_attn_ref(x, qkv_w, proj_w, proj_b, rand_matrix):
        import jax, jax.numpy as jnp
        import numpy as np
        B, N, C, H = (8, 256, 192, 12)
        D = C // H
        M = 2 * D
        SCALE = D ** (-0.5)
        EPS = 1e-12

        def _feature_map(z, rand_matrix):
            logits = jnp.einsum('bhnd,hdm->bhnm', z, rand_matrix)
            sqnorm = 0.5 * jnp.sum(z * z, axis=-1, keepdims=True)
            return jnp.exp(logits - sqnorm) * M ** (-0.5)
        b, n, c = x.shape
        qkv = (x @ qkv_w.T).reshape(b, n, 3, H, D).transpose(2, 0, 3, 1, 4)
        q, k, v = (qkv[0], qkv[1], qkv[2])
        sq = SCALE ** 0.5
        qf = _feature_map(q * sq, rand_matrix)
        kf = _feature_map(k * sq, rand_matrix)
        attn = jnp.einsum('bhnm,bhkm->bhnk', qf, kf)
        denom = jnp.maximum(jnp.sum(jnp.abs(attn), axis=-1, keepdims=True), EPS)
        attn = attn / denom
        out = jnp.einsum('bhnk,bhkd->bhnd', attn, v)
        out = out.transpose(0, 2, 1, 3).reshape(b, n, c)
        return out @ proj_w.T + proj_b

    def _L0_ffn_ref(x, norm1_w, norm1_b, qkv_w, qkv_b, proj_w, proj_b, norm2_w, norm2_b, w_gate, W1, b1, W2, b2):
        import jax, jax.numpy as jnp
        import numpy as np
        B, N, D, H, E, HID, TOPK = (8, 197, 192, 12, 8, 768, 2)

        def _layernorm(x, w, b, eps=1e-05):
            mu = jnp.mean(x, axis=-1, keepdims=True)
            var = jnp.mean((x - mu) ** 2, axis=-1, keepdims=True)
            return (x - mu) * jax.lax.rsqrt(var + eps) * w + b
        Bx, Nx, C = x.shape
        hd = C // H
        scale = hd ** (-0.5)
        xn = _layernorm(x, norm1_w, norm1_b)
        qkv = (xn @ qkv_w.T + qkv_b).reshape(Bx, Nx, 3, H, hd).transpose(2, 0, 3, 1, 4)
        q, k, v = (qkv[0], qkv[1], qkv[2])
        attn = jax.nn.softmax(jnp.einsum('bhqd,bhkd->bhqk', q, k) * scale, axis=-1)
        o = jnp.einsum('bhqk,bhkd->bqhd', attn, v).reshape(Bx, Nx, C)
        x = x + (o @ proj_w.T + proj_b)
        xn2 = _layernorm(x, norm2_w, norm2_b).reshape(-1, C)
        T = xn2.shape[0]
        logits = xn2 @ w_gate
        top_vals, top_idx = jax.lax.top_k(logits, TOPK)
        gates = jax.nn.softmax(top_vals, axis=-1)
        gates_full = jnp.zeros((T, E), xn2.dtype).at[jnp.arange(T)[:, None], top_idx].add(gates)

        def body(acc, p):
            w1, bb1, w2, bb2, g = p
            h = jax.nn.gelu(xn2 @ w1 + bb1, approximate=False)
            return (acc + g[:, None] * (h @ w2 + bb2), None)
        moe_out, _ = jax.lax.scan(body, jnp.zeros_like(xn2), (W1, b1, W2, b2, gates_full.T))
        return x + moe_out.reshape(Bx, Nx, C)
    h = _L0_tok_ref(x, L0_tok_patch_w, L0_tok_patch_b, L0_tok_ln_g, L0_tok_ln_b, L0_tok_qkv_w, L0_tok_qkv_b, L0_tok_proj_w, L0_tok_proj_b, L0_tok_ff1_w, L0_tok_ff1_b, L0_tok_ff2_w, L0_tok_ff2_b)
    h = jnp.concatenate([jnp.broadcast_to(cls_tok, (h.shape[0], 1, h.shape[2])), h], axis=1)
    h = h + _L0_attn_ref(_layernorm(h, axis=-1), L0_attn_qkv_w, L0_attn_proj_w, L0_attn_proj_b, L0_attn_rand_matrix)
    h = h + _L0_ffn_ref(_layernorm(h, axis=-1), L0_ffn_norm1_w, L0_ffn_norm1_b, L0_ffn_qkv_w, L0_ffn_qkv_b, L0_ffn_proj_w, L0_ffn_proj_b, L0_ffn_norm2_w, L0_ffn_norm2_b, L0_ffn_w_gate, L0_ffn_W1, L0_ffn_b1, L0_ffn_W2, L0_ffn_b2)
    return h

_drawn_inputs = setup_inputs


def setup_inputs(seed=0):
    import zlib

    import numpy as np

    out = dict(_drawn_inputs(seed))
    spreads = {'L0_tok_patch_b': (0.0, 0.1),
     'L0_tok_ln_g': (1.0, 0.2),
     'L0_tok_ln_b': (0.0, 0.1),
     'L0_tok_qkv_b': (0.0, 0.356),
     'L0_tok_proj_b': (0.0, 0.1),
     'L0_tok_ff1_b': (0.0, 0.307),
     'L0_tok_ff2_b': (0.0, 0.1),
     'L0_ffn_norm1_w': (1.0, 0.6),
     'L0_ffn_norm1_b': (0.0, 0.8),
     'L0_ffn_qkv_b': (0.0, 0.544),
     'L0_ffn_proj_b': (0.0, 0.1),
     'L0_ffn_norm2_w': (1.0, 0.6),
     'L0_ffn_norm2_b': (0.0, 0.62),
     'L0_ffn_b1': (0.0, 0.8),
     'L0_ffn_b2': (0.0, 0.1)}
    factors = {'L0_tok_qkv_w': 6.545, 'L0_attn_rand_matrix': 8.0, 'L0_ffn_qkv_w': 3.464}
    for name, (base, spread) in spreads.items():
        noise = np.random.default_rng([zlib.crc32(name.encode()), seed]).standard_normal(out[name].shape)
        drawn = base * np.exp(spread * noise) if base else spread * noise
        out[name] = jnp.asarray(drawn.astype(out[name].dtype))
    for name, factor in factors.items():
        out[name] = (out[name] * factor).astype(out[name].dtype)
    return out
```

```python
from contextlib import ExitStack

import numpy as np

import concourse.bass as bass
from concourse import mybir

F32 = mybir.dt.float32
F32R = mybir.dt.float32r
ALU = mybir.AluOpType
ACT = mybir.ActivationFunctionType
AXX = mybir.AxisListType.X

IMAGES = 8
PATCHES = 64
TOKENS = PATCHES + 1
D = 192
CH = 96
KC = D // CH
HEADS = 12
HD = D // HEADS
PAD = 32
HPC = 128 // PAD
HC = HEADS // HPC
HIDDEN = 768
FC = HIDDEN // 128
EXPERTS = 8
GROUPS = 2
GI = IMAGES // GROUPS
ALL = IMAGES * TOKENS
NG = GI * TOKENS
GATE_ROWS = 104
GATE_TILES = ALL // GATE_ROWS
EPS = 1e-5
DENOM_EPS = 1e-12
FEATURES = 2 * HD
SCALE = float(HD) ** -0.5

COLS96 = ["patch_b", "tok_ln_g", "tok_ln_b", "tok_ff2_b", "tok_proj_b", "perf_proj_b",
          "n1_w", "n1_b", "ffn_proj_b", "n2_w", "n2_b", "cls"]
COLS128 = [("tok_ff1_b", FC), ("tok_q_b", HC), ("tok_k_b", HC), ("tok_v_b", HC),
           ("ffn_q_b", HC), ("ffn_k_b", HC), ("ffn_v_b", HC), ("b1", EXPERTS * FC),
           ("feat_add", 1), ("feat_mul", 1)]


def build_tower(nc, dram, out):
    ctx = ExitStack()
    with ctx:
        def sem(name):
            return ctx.enter_context(nc.semaphore(name))

        cursor = [-(-nc.sbuf_base // 64) * 64]

        def reserve(nbytes):
            at = cursor[0]
            cursor[0] += -(-nbytes // 64) * 64
            return at

        def place(name, shape, at, dt=F32):
            return nc.alloc_sbuf_tensor_at(name, shape, dt, offset=at)

        def own(name, shape, dt=F32):
            return place(name, shape, reserve(4 * int(np.prod(shape[1:]))), dt)

        ident = own("ident", [128, 128])
        headmask = own("headmask", [128, HPC])
        blockmask = own("blockmask", [128, 128])
        earlier = own("earlier", [128, EXPERTS, EXPERTS])
        pos = own("pos", [CH, KC, PATCHES])
        pos_b = own("pos_b", [CH, KC, PATCHES])
        mean_w = own("mean_w", [CH, CH])
        cols96 = own("cols96", [CH, 2 * len(COLS96)])
        cols128 = own("cols128", [128, sum(w for _, w in COLS128)])
        w_gate = own("w_gate", [CH, KC, EXPERTS])
        b2 = own("b2", [EXPERTS, D])
        proj_b_eff = own("proj_b_eff", [CH, 2, KC])
        eps_col = own("eps_col", [CH, 1])

        def vec(name, c=None):
            i = 2 * COLS96.index(name)
            return cols96[:, i:i + KC] if c is None else cols96[:, i + c:i + c + 1]

        def col(name, j):
            i = 0
            for n, w in COLS128:
                if n == name:
                    return cols128[:, i + j:i + j + 1]
                i += w

        h = own("h", [CH, KC, ALL])
        x2 = own("x2", [CH, KC, ALL])
        xp = own("xp", [CH, KC, ALL])
        nrm = own("nrm", [CH, KC, ALL])
        at_xc = reserve(4 * KC * ALL)
        at_sq = reserve(4 * KC * ALL)
        at_z = reserve(4 * KC * ALL)
        xc = place("xc", [CH, KC, ALL], at_xc)
        sq = place("sq", [CH, KC, ALL], at_sq)
        z = place("z", [CH, KC, ALL], at_z)
        rstd = own("rstd", [CH, ALL])
        tokx = place("tokx", [CH, KC, IMAGES * PATCHES], at_z)
        id0 = x2
        ffo = nrm
        x1 = xp

        at_s1 = reserve(4 * (2 * KC * HIDDEN + 2 * FC * D))
        tok_off = [at_s1]

        def tok_place(name, shape):
            t = place(name, shape, tok_off[0])
            tok_off[0] += 4 * int(np.prod(shape[1:]))
            return t

        ff1_w = tok_place("ff1_w", [CH, KC, HIDDEN])
        ff2_w = tok_place("ff2_w", [128, FC, D])
        wq = {"tok": tok_place("tok_wq", [CH, KC, HC * 128])}
        wk = {"tok": tok_place("tok_wk", [CH, KC, HC * 128])}
        wv = {"tok": tok_place("tok_wv", [CH, KC, D])}
        wo = {"tok": tok_place("tok_wo", [128, HC, D])}
        for blk in ("perf", "ffn"):
            wq[blk] = own(f"{blk}_wq", [CH, KC, HC * 128])
            wk[blk] = own(f"{blk}_wk", [CH, KC, HC * 128])
            wv[blk] = own(f"{blk}_wv", [CH, KC, D])
            wo[blk] = own(f"{blk}_wo", [128, HC, D])
        rand_w = own("rand_w", [128, HC, 128])

        at_u = reserve(4 * 4 * FC * ALL)
        patches = place("patches", [128, FC, IMAGES * PATCHES], at_u + 4 * FC * ALL)
        patch_w = place("patch_w", [128, FC, D], at_u + 4 * 2 * FC * ALL)
        hid = place("hid", [128, FC, IMAGES * PATCHES], at_u)
        kbd = place("kbd", [128, HC, HPC, ALL], at_u + 4 * FC * ALL)
        qT = place("qT", [128, HC, ALL], at_u + 4 * 3 * FC * ALL)
        oT = place("oT", [128, HC, ALL], at_u + 4 * 3 * FC * ALL + 4 * HC * ALL)
        prob = place("prob", [TOKENS, HEADS, TOKENS], at_u)
        eprob = place("eprob", [TOKENS, HEADS, TOKENS], at_u + 3136)
        probT = place("probT", [TOKENS, HEADS, TOKENS], at_u + 6272)
        fq = place("fq", [128, HC, ALL], at_u + 4 * FC * ALL)
        fk = place("fk", [128, HC, ALL], at_u + 4 * FC * ALL + 4 * HC * ALL)
        flin = place("flin", [128, 2, NG], at_u + 4 * FC * ALL + 8 * HC * ALL)
        hh = [place(f"hh{s}", [128, FC, ALL], at_u + 4 * s * FC * ALL, F32R) for s in range(2)]
        hl = [place(f"hl{s}", [128, FC, ALL], at_u + 4 * (2 + s) * FC * ALL, F32R) for s in range(2)]

        q_img = own("q_img", [128, HC, TOKENS])
        x_img = own("x_img", [CH, KC, TOKENS])
        vpad = own("vpad", [TOKENS, HEADS, PAD])
        rowmax = own("rowmax", [TOKENS, HEADS])
        den = own("den", [128, HC, TOKENS])
        rden = own("rden", [128, HC, TOKENS])
        lden = own("lden", [128, HC, TOKENS])
        kfeat = own("kfeat", [TOKENS, HC * 128])
        kvbd = own("kvbd", [128, HC, 128])

        w1f = own("w1f", [CH, KC, HIDDEN])
        w2f = own("w2f", [128, FC, D])
        n1, n2 = 4 * KC * HIDDEN, 4 * FC * D
        at_s = [reserve(2 * n1 + 2 * n2), at_s1]
        w1h = [place(f"w1h{s}", [CH, KC, HIDDEN], at_s[s], F32R) for s in range(2)]
        w1l = [place(f"w1l{s}", [CH, KC, HIDDEN], at_s[s] + n1, F32R) for s in range(2)]
        w2h = [place(f"w2h{s}", [128, FC, D], at_s[s] + 2 * n1, F32R) for s in range(2)]
        w2l = [place(f"w2l{s}", [128, FC, D], at_s[s] + 2 * n1 + n2, F32R) for s in range(2)]
        gate_b = [own(f"gate_b{s}", [128, ALL]) for s in range(2)]
        hg = place("hg", [128, ALL], at_xc)
        gh = place("gh", [128, ALL], at_xc + 4 * ALL)
        gates_T = place("gates_T", [EXPERTS, ALL], at_sq)
        outbuf = z
        xh = own("xh", [CH, KC, ALL], F32R)
        xl = own("xl", [CH, KC, ALL], F32R)
        logit = own("logit", [GATE_ROWS, GATE_TILES, EXPERTS])
        cmp_gt = own("cmp_gt", [GATE_ROWS, GATE_TILES, EXPERTS, EXPERTS])
        cmp_eq = own("cmp_eq", [GATE_ROWS, GATE_TILES, EXPERTS, EXPERTS])
        rank = own("rank", [GATE_ROWS, GATE_TILES * EXPERTS])
        gsum = own("gsum", [GATE_ROWS, GATE_TILES])
        gates = own("gates", [GATE_ROWS, GATE_TILES, EXPERTS])

        ps = ctx.enter_context(nc.psum_tensor("ps", [128, 8, 512], F32))

        gates_dram = nc.dram_tensor("gates_by_expert", [EXPERTS, ALL], F32, kind="Internal").ap()

        loads = [("patches", patches), ("patch_w", patch_w), ("cols96", cols96), ("mean_w", mean_w),
                 ("pos", pos), ("ff1_w", ff1_w), ("cols128", cols128), ("ff2_w", ff2_w),
                 ("tok_wq", wq["tok"]), ("tok_wk", wk["tok"]), ("headmask", headmask), ("ident", ident),
                 ("tok_wv", wv["tok"]), ("tok_wo", wo["tok"]),
                 ("perf_wq", wq["perf"]), ("perf_wk", wk["perf"]), ("rand_w", rand_w),
                 ("perf_wv", wv["perf"]), ("blockmask", blockmask), ("perf_wo", wo["perf"]),
                 ("ffn_wq", wq["ffn"]), ("ffn_wk", wk["ffn"]), ("ffn_wv", wv["ffn"]),
                 ("ffn_wo", wo["ffn"]), ("w_gate", w_gate), ("earlier", earlier), ("b2", b2)]
        loaded = {name: sem(f"loaded_{name}") for name, _ in loads}
        patch_ready = sem("patch_ready")
        tokx_ready = sem("tokx_ready")
        posb_ready = sem("posb_ready")
        id0_ready = sem("id0_ready")
        consts_set = sem("consts_set")
        ln_mean = sem("ln_mean")
        ln_xc = sem("ln_xc")
        ln_sq = sem("ln_sq")
        ln_var = sem("ln_var")
        ln_log = sem("ln_log")
        ln_rstd = sem("ln_rstd")
        ln_z = sem("ln_z")
        aff = sem("aff")
        ff1_ready = sem("ff1_ready")
        ff1_gelu = sem("ff1_gelu")
        ff2_ready = sem("ff2_ready")
        ff2_taken = sem("ff2_taken")
        cls_set = sem("cls_set")
        q_ready = sem("q_ready")
        q_taken = sem("q_taken")
        k_ready = sem("k_ready")
        k_taken = sem("k_taken")
        q_copied = sem("q_copied")
        x_copied = sem("x_copied")
        s_ready = sem("s_ready")
        max_ready = sem("max_ready")
        sub_done = sem("sub_done")
        exp_done = sem("exp_done")
        pt_ready = sem("pt_ready")
        pt_taken = sem("pt_taken")
        v_ready = sem("v_ready")
        v_taken = sem("v_taken")
        o_ready = sem("o_ready")
        den_ready = sem("den_ready")
        den_log = sem("den_log")
        rden_ready = sem("rden_ready")
        o_done = sem("o_done")
        pbe_ready = sem("pbe_ready")
        pbe_done = sem("pbe_done")
        proj_ready = sem("proj_ready")
        proj_taken = sem("proj_taken")
        f_ready = sem("f_ready")
        f_lin = sem("f_lin")
        f_done = sem("f_done")
        qf_ready = sem("qf_ready")
        qf_done = sem("qf_done")
        kl_ready = sem("kl_ready")
        kf_done = sem("kf_done")
        kv_ready = sem("kv_ready")
        kv_taken = sem("kv_taken")
        clamp_done = sem("clamp_done")
        perf_vready = sem("perf_vready")
        perf_vtaken = sem("perf_vtaken")
        perf_oready = sem("perf_oready")
        perf_den = sem("perf_den")
        perf_rden = sem("perf_rden")
        perf_odone = sem("perf_odone")
        xh_ready = sem("xh_ready")
        xl_ready = sem("xl_ready")
        gl_ready = sem("gl_ready")
        gchain = sem("gchain")
        gexp = sem("gexp")
        gt_ready = sem("gt_ready")
        gt_taken = sem("gt_taken")
        g_stored = sem("g_stored")
        g_loaded = [sem(f"g_loaded{s}") for s in range(2)]
        w1_loaded = sem("w1_loaded")
        w2_loaded = sem("w2_loaded")
        w1_hi = sem("w1_hi")
        w1_lo = sem("w1_lo")
        w2_hi = sem("w2_hi")
        w2_lo = sem("w2_lo")
        e1_ready = sem("e1_ready")
        e1_gelu = sem("e1_gelu")
        gated = sem("gated")
        h_hi = sem("h_hi")
        h_lo = sem("h_lo")
        y_ready = sem("y_ready")
        base_ready = sem("base_ready")
        out_ready = sem("out_ready")
        stored = sem("stored")

        block = ctx.enter_context(nc.Block())

        def cols(g, tokens):
            return slice(g * GI * tokens, (g + 1) * GI * tokens)

        MEAN, VAR, PT0, VB, OB = (4, 5), (6, 7), 3, 5, 6
        KLB, PVB, KVB, POB = 0, 1, 2, 3

        @block.sync
        def _(sp):
            for name, dst in loads:
                sp.dma_start(dst[:], dram[name]).then_inc(loaded[name], 16)
                if name == "tok_wo":
                    sp.dma_start(w1f[:], dram["w1"][0]).then_inc(w1_loaded, 16)
                    sp.dma_start(w2f[:], dram["w2"][0]).then_inc(w2_loaded, 16)

            sp.wait_ge(gt_taken, 2)
            sp.dma_start(gates_dram, gates_T[:]).then_inc(g_stored, 16)
            sp.wait_ge(g_stored, 16)
            sp.dma_start(gate_b[0][:], gates_dram[0:1, :].partition_broadcast(128)).then_inc(g_loaded[0], 16)

            def next_expert(u, s, row):
                sp.wait_ge(w1_lo, u)
                sp.dma_start(w1f[:], row(dram["w1"])).then_inc(w1_loaded, 16)
                sp.wait_ge(w2_lo, u)
                sp.dma_start(w2f[:], row(dram["w2"])).then_inc(w2_loaded, 16)

            def next_gates(u, s):
                sp.dma_start(gate_b[s][:], gates_dram[bass.ds(u, 1), :].partition_broadcast(128)
                             ).then_inc(g_loaded[s], 16)

            sp.dma_start(gate_b[1][:], gates_dram[1:2, :].partition_broadcast(128)).then_inc(g_loaded[1], 16)
            next_expert(1, 1, lambda w: w[1])
            with sp.Fori(0, (EXPERTS - 2) // 2) as i:
                for s in range(2):
                    u = 2 * i + (2 + s)
                    sp.wait_ge(gated, FC * (u - 1))
                    next_gates(u, s)
                    next_expert(u, s, lambda w: w[bass.ds(u, 1)].rearrange("o p k n -> (o p) k n"))

            for g in range(GROUPS):
                sp.wait_ge(out_ready, g + 1)
                sp.dma_start(out[:, :, cols(g, TOKENS)], outbuf[:, :, cols(g, TOKENS)]).then_inc(stored, 16)
            sp.wait_ge(stored, 16 * GROUPS)

        @block.gpsimd
        def _(pool):
            def copies(T, q_src, x_src, q_read, x_read, before):
                def one(b):
                    n = before + b
                    if not (isinstance(n, int) and n == 0):
                        pool.wait_ge(q_read, n)
                    nc.gpsimd.tensor_copy(q_img[:, :, 0:T], q_src[:, :, bass.ds(b * T, T)]).then_inc(q_copied, 1)
                    if not (isinstance(n, int) and n == 0):
                        pool.wait_ge(x_read, n)
                    nc.gpsimd.tensor_copy(x_img[:, :, 0:T], x_src[:, :, bass.ds(b * T, T)]).then_inc(x_copied, 1)
                one(0)
                with pool.Fori(1, IMAGES) as b:
                    one(b)

            def lo1(s, u):
                pool.wait_ge(w1_hi, u + 1)
                nc.gpsimd.tensor_tensor(w1l[s][:], w1f[:], w1h[s][:].bitcast(F32), ALU.subtract).then_inc(w1_lo, 1)

            def lo2(s, u):
                pool.wait_ge(w2_hi, u + 1)
                nc.gpsimd.tensor_tensor(w2l[s][:], w2f[:], w2h[s][:].bitcast(F32), ALU.subtract).then_inc(w2_lo, 1)

            pool.wait_ge(q_taken, GROUPS * HC)
            copies(PATCHES, qT, ffo, s_ready, v_ready, 0)
            lo1(0, 0)
            pool.wait_ge(f_done, 2 * GROUPS * HC)
            copies(TOKENS, fk, nrm, kl_ready, perf_vready, 0)
            pool.wait_ge(q_taken, 2 * GROUPS * HC)
            copies(TOKENS, qT, nrm, s_ready, v_ready, IMAGES)

            def iteration(u, s, last=False):
                if not last:
                    lo1(1 - s, u + 1)
                lo2(s, u)

            iteration(0, 0)
            with pool.Fori(0, (EXPERTS - 2) // 2) as i:
                iteration(2 * i + 1, 1)
                iteration(2 * i + 2, 0)
            iteration(EXPERTS - 1, 1, last=True)

        @block.scalar
        def _(act):
            def layernorm(n, T):
                for g in range(GROUPS):
                    c = cols(g, T)
                    act.wait_ge(ln_xc, GROUPS * n + g + 1)
                    if n:
                        act.wait_ge(ln_var, GROUPS * n)
                    nc.scalar.activation(sq[:, :, c], xc[:, :, c], ACT.Square).then_inc(ln_sq, 1)
                for g in range(GROUPS):
                    c = cols(g, T)
                    v = GROUPS * n + g + 1
                    act.wait_ge(ln_var, v)
                    nc.scalar.activation(rstd[:, c], ps[0:CH, VAR[g], 0:GI * T], ACT.Ln,
                                         bias=eps_col[:, 0:1]).then_inc(ln_log, 1)
                    act.wait_ge(ln_log, v)
                    nc.scalar.activation(rstd[:, c], rstd[:, c], ACT.Exp, scale=-0.5).then_inc(ln_rstd, 1)

            def affine(n, i, w, b):
                for g in range(GROUPS):
                    act.wait_ge(ln_z, GROUPS * n + g + 1)
                    for c in range(KC):
                        last = nc.scalar.activation(nrm[:, c, cols(g, TOKENS)], z[:, c, cols(g, TOKENS)],
                                                    ACT.Identity, scale=vec(w, c), bias=vec(b, c))
                    last.then_inc(aff, 1)

            def gelus(f):
                for g in range(GROUPS):
                    for m in range(FC):
                        t = (f * GROUPS + g) * FC + m
                        act.wait_ge(ff1_ready, t + 1)
                        nc.scalar.activation(hid[:, m, cols(g, PATCHES)], ps[:, t % 4, 0:GI * PATCHES],
                                             ACT.Gelu_apprx_tanh, bias=col("tok_ff1_b", m)).then_inc(ff1_gelu, 1)

            def take_q(a, T, bias):
                for g in range(GROUPS):
                    for c in range(HC):
                        t = (a * GROUPS + g) * HC + c
                        act.wait_ge(q_ready, t + 1)
                        nc.scalar.activation(qT[:, c, cols(g, T)], ps[:, t % 2, 0:GI * T], ACT.Identity,
                                             bias=col(bias, c)).then_inc(q_taken, 1)

            def attention(a, T):
                def exp(b):
                    n = IMAGES * a + b
                    act.wait_ge(sub_done, n + 1)
                    act.wait_ge(pt_ready, n)
                    nc.scalar.activation(eprob[0:T, :, 0:T], prob[0:T, :, 0:T], ACT.Exp,
                                         scale=SCALE).then_inc(exp_done, 1)

                def take_v(b):
                    n = IMAGES * a + b
                    act.wait_ge(v_ready, n + 1)
                    nc.scalar.copy(vpad[0:T, :, 0:HD],
                                   ps[0:T, VB, 0:D].rearrange("p (h d) -> p h d", d=HD)).then_inc(v_taken, 1)

                def take_pt(b):
                    n = IMAGES * a + b
                    act.wait_ge(pt_ready, n + 1)
                    half = HEADS // 2
                    for j in range(2):
                        last = nc.scalar.copy(
                            probT[0:T, half * j:half * (j + 1), 0:T],
                            ps[0:T, PT0 + j, 0:half * T].rearrange("p (h t) -> p h t", t=T))
                    last.then_inc(pt_taken, 1)

                def reciprocal(b):
                    n = IMAGES * a + b
                    act.wait_ge(den_ready, n + 1)
                    nc.scalar.activation(lden[:, :, 0:T], den[:, :, 0:T], ACT.Ln).then_inc(den_log, 1)
                    act.wait_ge(den_log, n + 1)
                    nc.scalar.activation(rden[:, :, 0:T], lden[:, :, 0:T], ACT.Exp,
                                         scale=-1.0).then_inc(rden_ready, 1)

                exp(0)
                take_v(0)
                with act.Fori(0, IMAGES - 1) as b:
                    take_pt(b)
                    exp(b + 1)
                    reciprocal(b)
                    take_v(b + 1)
                take_pt(IMAGES - 1)
                reciprocal(IMAGES - 1)

            def exp_and_log():
                nc.scalar.preload_act_table_set("natural_log_exp_and_others")

            exp_and_log()
            act.wait_ge(loaded["cols96"], 16)
            for g in range(GROUPS):
                for m in range(KC):
                    act.wait_ge(patch_ready, 2 * g + m + 1)
                    last = nc.scalar.activation(tokx[:, m, cols(g, PATCHES)],
                                                ps[0:CH, 2 * g + m, 0:GI * PATCHES], ACT.Identity,
                                                bias=vec("patch_b", m))
                last.then_inc(tokx_ready, 1)
            act.wait_ge(consts_set, 2)
            layernorm(0, PATCHES)
            act.wait_ge(loaded["cols128"], 16)
            gelus(0)
            exp_and_log()
            take_q(0, PATCHES, "tok_q_b")
            attention(0, PATCHES)
            gelus(1)
            exp_and_log()
            act.wait_ge(w1_loaded, 16)
            nc.scalar.copy(w1h[0][:], w1f[:]).then_inc(w1_hi, 1)
            layernorm(1, TOKENS)

            for g in range(GROUPS):
                for c in range(2 * HC):
                    t = 2 * HC * g + c
                    act.wait_ge(f_ready, t + 1)
                    if t >= 2:
                        act.wait_ge(f_done, t - 1)
                    nc.scalar.activation(flin[:, t % 2, :], ps[:, t % 4, 0:NG], ACT.Identity,
                                         scale=col("feat_mul", 0), bias=col("feat_add", 0)).then_inc(f_lin, 1)
            for g in range(GROUPS):
                for c in range(HC):
                    t = HC * g + c
                    act.wait_ge(qf_ready, t + 1)
                    nc.scalar.activation(qT[:, c, cols(g, TOKENS)], ps[:, 4 + t % 2, 0:NG],
                                         ACT.Exp).then_inc(qf_done, 1)

            def key_features(b):
                act.wait_ge(kl_ready, b + 1)
                nc.scalar.activation(kfeat[:], ps[0:TOKENS, KLB, 0:HC * 128], ACT.Exp).then_inc(kf_done, 1)
                act.wait_ge(perf_vready, b + 1)
                nc.scalar.copy(vpad[:, :, 0:HD],
                               ps[0:TOKENS, PVB, 0:D].rearrange("p (h d) -> p h d", d=HD)
                               ).then_inc(perf_vtaken, 1)

            with act.Fori(0, IMAGES) as b:
                key_features(b)

            layernorm(2, TOKENS)
            layernorm(3, TOKENS)
            affine(3, 0, "n1_w", "n1_b")
            take_q(1, TOKENS, "ffn_q_b")
            attention(1, TOKENS)
            layernorm(4, TOKENS)
            affine(4, 1, "n2_w", "n2_b")

            act.wait_ge(gchain, 8)
            nc.scalar.activation(gates[:], logit[:], ACT.Exp).then_inc(gexp, 1)

            def hi1(s, u):
                act.wait_ge(w1_loaded, 16 * (u + 1))
                nc.scalar.copy(w1h[s][:], w1f[:]).then_inc(w1_hi, 1)

            def hi2(s, u):
                act.wait_ge(w2_loaded, 16 * (u + 1))
                nc.scalar.copy(w2h[s][:], w2f[:]).then_inc(w2_hi, 1)

            def iteration(u, s, last=False):
                for m in range(FC):
                    t = FC * u + m
                    act.wait_ge(e1_ready, t + 1)
                    p = 2 * (m % 2)
                    i = sum(w for _, w in COLS128[:7])
                    act_b = cols128[:, bass.ds(i + t, 1)]
                    nc.scalar.activation(hg[:].rearrange("p (g t) -> p g t", g=GROUPS), ps[:, p:p + 2, 0:NG],
                                         ACT.Gelu, bias=act_b).then_inc(e1_gelu, 1)
                    act.wait_ge(gated, t + 1)
                    nc.scalar.copy(hh[s][:, m, :], gh[:]).then_inc(h_hi, 1)
                    if m == 1 and not last:
                        hi1(1 - s, u + 1)
                    if m == 3:
                        hi2(s, u)

            iteration(0, 0)
            with act.Fori(0, (EXPERTS - 2) // 2) as i:
                iteration(2 * i + 1, 1)
                iteration(2 * i + 2, 0)
            iteration(EXPERTS - 1, 1, last=True)

        @block.vector
        def _(dve):
            def layernorm(n, T, src, wait_src, dst=None):
                for g in range(GROUPS):
                    c, v = cols(g, T), GROUPS * n + g + 1
                    wait_src(g)
                    dve.wait_ge(ln_mean, v)
                    mean = ps[0:CH, MEAN[g], 0:GI * T].unsqueeze(1).to_broadcast([CH, KC, GI * T])
                    nc.vector.tensor_tensor(xc[:, :, c], src[:, :, c], mean, ALU.subtract).then_inc(ln_xc, 1)
                for g in range(GROUPS):
                    c, v = cols(g, T), GROUPS * n + g + 1
                    dve.wait_ge(ln_rstd, v)
                    dve.wait_ge(ln_xc, v)
                    r = rstd[:, c].unsqueeze(1).to_broadcast([CH, KC, GI * T])
                    nc.vector.tensor_tensor((dst or z)[:, :, c], xc[:, :, c], r, ALU.mult).then_inc(ln_z, 1)

            def take_k(a, T, bias):
                for g in range(GROUPS):
                    for c in range(HC):
                        t = (a * GROUPS + g) * HC + c
                        dve.wait_ge(k_ready, t + 1)
                        nc.vector.scalar_tensor_tensor(
                            kbd[:, c, :, cols(g, T)],
                            ps[:, 2 + t % 2, 0:GI * T].unsqueeze(1).to_broadcast([128, HPC, GI * T]),
                            col(bias, c),
                            headmask[:].unsqueeze(2).to_broadcast([128, HPC, GI * T]),
                            ALU.add, ALU.mult).then_inc(k_taken, 1)

            shuffle = [HD + i % HD for i in range(PAD)]

            def attention(a, T):
                def centre(b):
                    n = IMAGES * a + b
                    dve.wait_ge(s_ready, n + 1)
                    sc = ps[0:T, 0:HC, 0:HPC * T].rearrange("p c (h t) -> p c h t", t=T)
                    nc.vector.tensor_reduce(rowmax[0:T, :].rearrange("p (c h) -> p c h", c=HC), sc,
                                            AXX, ALU.max).then_inc(max_ready, 1)
                    dve.wait_ge(max_ready, n + 1)
                    dve.wait_ge(exp_done, n)
                    m = rowmax[0:T, :].rearrange("p (c h) -> p c h", c=HC).unsqueeze(3).to_broadcast(
                        [T, HC, HPC, T])
                    nc.vector.tensor_tensor(
                        prob[0:T, :, 0:T].rearrange("p (c h) t -> p c h t", c=HC), sc, m,
                        ALU.subtract).then_inc(sub_done, 1)

                def normalise(b):
                    n = IMAGES * a + b
                    dve.wait_ge(consts_set, 2)
                    dve.wait_ge(o_ready, n + 1)
                    o = ps[:, OB, 0:HC * T].rearrange("p (c t) -> p c t", t=T)
                    nc.vector.stream_shuffle(den[:, :, 0:T], o, shuffle).then_inc(den_ready, 1)
                    dve.wait_ge(rden_ready, n + 1)
                    nc.vector.tensor_tensor(oT[:, :, bass.ds(b * T, T)], o, rden[:, :, 0:T],
                                            ALU.mult).then_inc(o_done, 1)

                centre(0)
                with dve.Fori(0, IMAGES - 1) as b:
                    centre(b + 1)
                    normalise(b)
                normalise(IMAGES - 1)

            def take_proj(p, T, fn):
                for g in range(GROUPS):
                    for m in range(KC):
                        dve.wait_ge(proj_ready, 4 * p + 2 * g + m + 1)
                        fn(m, cols(g, T), ps[0:CH, 4 + 2 * g + m, 0:GI * T]).then_inc(proj_taken, 1)

            def proj_bias(i, name):
                dve.wait_ge(pbe_ready, i + 1)
                nc.vector.tensor_tensor(proj_b_eff[:, i, :], ps[0:CH, 7, 0:KC], vec(name),
                                        ALU.add).then_inc(pbe_done, 1)
                dve.wait_ge(pbe_done, i + 1)

            nc.vector.memset(vpad[:], 1.0).then_inc(consts_set, 1)
            nc.vector.memset(eps_col[:], EPS).then_inc(consts_set, 1)
            dve.wait_ge(loaded["pos"], 16)
            dve.wait_ge(loaded["cols96"], 16)
            for c in range(KC):
                last = nc.vector.tensor_scalar(pos_b[:, c, :], pos[:, c, :], vec("tok_ln_b", c), None, ALU.add)
            last.then_inc(posb_ready, 1)

            layernorm(0, PATCHES, tokx, lambda g: dve.wait_ge(tokx_ready, g + 1))
            dve.wait_ge(posb_ready, 1)
            for g in range(GROUPS):
                c = cols(g, PATCHES)
                dve.wait_ge(ln_z, g + 1)
                for k in range(KC):
                    last = nc.vector.scalar_tensor_tensor(
                        id0[:, k, c].rearrange("p (b t) -> p b t", t=PATCHES),
                        z[:, k, c].rearrange("p (b t) -> p b t", t=PATCHES), vec("tok_ln_g", k),
                        pos_b[:, k, :].unsqueeze(1).to_broadcast([CH, GI, PATCHES]), ALU.mult, ALU.add)
                last.then_inc(id0_ready, 1)

            def take_ff2(f, fn):
                for g in range(GROUPS):
                    for m in range(KC):
                        dve.wait_ge(ff2_ready, 4 * f + 2 * g + m + 1)
                        fn(g, m, cols(g, PATCHES), ps[0:CH, 4 + 2 * g + m, 0:GI * PATCHES]).then_inc(ff2_taken, 1)

            take_ff2(0, lambda g, m, c, p: nc.vector.tensor_scalar(
                ffo[:, m, c], p, vec("tok_ff2_b", m), None, ALU.add))
            dve.wait_ge(loaded["headmask"], 16)
            take_k(0, PATCHES, "tok_k_b")
            proj_bias(0, "tok_proj_b")
            attention(0, PATCHES)
            take_proj(0, PATCHES, lambda m, c, p: nc.vector.scalar_tensor_tensor(
                x1[:, m, c], p, proj_b_eff[:, 0, m:m + 1], id0[:, m, c], ALU.add, ALU.add))
            h_img = h[:].rearrange("p k (b t) -> p k b t", t=TOKENS)
            nc.vector.tensor_copy(h_img[:, :, :, 0],
                                  vec("cls").unsqueeze(2).to_broadcast([CH, KC, IMAGES])).then_inc(cls_set, 1)
            take_ff2(1, lambda g, m, c, p: nc.vector.scalar_tensor_tensor(
                h_img[:, m, GI * g:GI * (g + 1), 1:TOKENS], p.rearrange("p (b t) -> p b t", t=PATCHES),
                vec("tok_ff2_b", m), x1[:, m, c].rearrange("p (b t) -> p b t", t=PATCHES),
                ALU.add, ALU.add))

            dve.wait_ge(cls_set, 1)
            layernorm(1, TOKENS, h, lambda g: dve.wait_ge(ff2_taken, 4 + 2 * (g + 1)), nrm)
            for g in range(GROUPS):
                for c in range(2 * HC):
                    t = 2 * HC * g + c
                    dve.wait_ge(f_lin, t + 1)
                    dst = fq if c < HC else fk
                    nc.vector.tensor_tensor(dst[:, c % HC, cols(g, TOKENS)], flin[:, t % 2, :],
                                            ps[:, t % 4, 0:NG], ALU.mult).then_inc(f_done, 1)
            dve.wait_ge(loaded["blockmask"], 16)
            with dve.Fori(0, IMAGES) as b:
                dve.wait_ge(kv_ready, b + 1)
                nc.vector.tensor_tensor(
                    kvbd[:], ps[:, KVB, 0:HC * 128].rearrange("p (c n) -> p c n", c=HC),
                    blockmask[:].unsqueeze(1).to_broadcast([128, HC, 128]), ALU.mult).then_inc(kv_taken, 1)
                dve.wait_ge(consts_set, 2)
                dve.wait_ge(perf_oready, b + 1)
                o = ps[:, POB, 0:HC * TOKENS].rearrange("p (c t) -> p c t", t=TOKENS)
                nc.vector.stream_shuffle(den[:], o, shuffle).then_inc(perf_den, 1)
                dve.wait_ge(perf_den, b + 1)
                nc.vector.tensor_scalar(rden[:], den[:], DENOM_EPS, None, ALU.max).then_inc(clamp_done, 1)
                dve.wait_ge(clamp_done, b + 1)
                nc.vector.reciprocal(lden[:], rden[:]).then_inc(perf_rden, 1)
                dve.wait_ge(perf_rden, b + 1)
                nc.vector.tensor_tensor(oT[:, :, bass.ds(b * TOKENS, TOKENS)], o, lden[:],
                                        ALU.mult).then_inc(perf_odone, 1)
            take_proj(1, TOKENS, lambda m, c, p: nc.vector.scalar_tensor_tensor(
                h[:, m, c], p, vec("perf_proj_b", m), h[:, m, c], ALU.add, ALU.add))

            layernorm(2, TOKENS, h, lambda g: dve.wait_ge(proj_taken, 4 + 2 * (g + 1)), x2)
            layernorm(3, TOKENS, x2, lambda g: dve.wait_ge(ln_z, 4 + g + 1))
            take_k(1, TOKENS, "ffn_k_b")
            proj_bias(1, "ffn_proj_b")
            attention(1, TOKENS)
            take_proj(2, TOKENS, lambda m, c, p: nc.vector.scalar_tensor_tensor(
                xp[:, m, c], p, proj_b_eff[:, 1, m:m + 1], x2[:, m, c], ALU.add, ALU.add))
            layernorm(4, TOKENS, xp, lambda g: dve.wait_ge(proj_taken, 8 + 2 * (g + 1)))
            nc.vector.tensor_tensor(h[:], h[:], xp[:], ALU.add).then_inc(base_ready, 1)

            for g in range(GROUPS):
                c = cols(g, TOKENS)
                dve.wait_ge(aff, GROUPS + g + 1)
                nc.vector.tensor_copy(xh[:, :, c], nrm[:, :, c]).then_inc(xh_ready, 1)
                dve.wait_ge(xh_ready, g + 1)
                nc.vector.tensor_tensor(xl[:, :, c], nrm[:, :, c], xh[:, :, c].bitcast(F32),
                                        ALU.subtract).then_inc(xl_ready, 1)

            steps = [0]

            def step(ins):
                steps[0] += 1
                ins.then_inc(gchain, 1)
                dve.wait_ge(gchain, steps[0])

            TT, EE = GATE_TILES, EXPERTS
            dve.wait_ge(gl_ready, 1)
            dve.wait_ge(loaded["earlier"], 16)
            step(nc.vector.tensor_copy(logit[:], ps[0:GATE_ROWS, 0, 0:TT * EE].rearrange("p (t e) -> p t e", e=EE)))
            other = logit[:].unsqueeze(2).to_broadcast([GATE_ROWS, TT, EE, EE])
            own_e = logit[:].unsqueeze(3).to_broadcast([GATE_ROWS, TT, EE, EE])
            step(nc.vector.tensor_tensor(cmp_gt[:], other, own_e, ALU.is_gt))
            step(nc.vector.tensor_tensor(cmp_eq[:], other, own_e, ALU.is_equal))
            step(nc.vector.tensor_tensor(cmp_eq[:], cmp_eq[:],
                                         earlier[0:GATE_ROWS].unsqueeze(1).to_broadcast([GATE_ROWS, TT, EE, EE]),
                                         ALU.mult))
            step(nc.vector.tensor_tensor(cmp_gt[:], cmp_gt[:], cmp_eq[:], ALU.add))
            step(nc.vector.tensor_reduce(rank[:].rearrange("p (t e) -> p t e", e=EE), cmp_gt[:], AXX, ALU.add))
            step(nc.vector.tensor_reduce(gsum[:], logit[:], AXX, ALU.max))
            step(nc.vector.tensor_tensor(logit[:], logit[:],
                                         gsum[:].unsqueeze(2).to_broadcast([GATE_ROWS, TT, EE]), ALU.subtract))
            step(nc.vector.tensor_scalar(rank[:], rank[:], 2.0, None, ALU.is_lt))
            dve.wait_ge(gexp, 1)
            step(nc.vector.tensor_tensor(gates[:], gates[:], rank[:].rearrange("p (t e) -> p t e", e=EE), ALU.mult))
            step(nc.vector.tensor_reduce(gsum[:], gates[:], AXX, ALU.add))
            step(nc.vector.reciprocal(gsum[:], gsum[:]))
            step(nc.vector.tensor_tensor(gates[:], gates[:],
                                         gsum[:].unsqueeze(2).to_broadcast([GATE_ROWS, TT, EE]), ALU.mult))
            dve.wait_ge(gt_ready, 1)
            n = 4 * GATE_ROWS
            nc.vector.tensor_copy(gates_T[:, 0:n], ps[0:EE, 2, 0:n]).then_inc(gt_taken, 1)
            nc.vector.tensor_copy(gates_T[:, n:ALL], ps[0:EE, 3, 0:GATE_ROWS]).then_inc(gt_taken, 1)

            def iteration(u, s, turn):
                dve.wait_ge(g_loaded[s], 16 * (turn + 1))
                for m in range(FC):
                    t = FC * u + m
                    dve.wait_ge(e1_gelu, t + 1)
                    dve.wait_ge(h_lo, t)
                    nc.vector.tensor_tensor(gh[:], hg[:], gate_b[s][:], ALU.mult).then_inc(gated, 1)
                    dve.wait_ge(h_hi, t + 1)
                    nc.vector.tensor_tensor(hl[s][:, m, :], gh[:], hh[s][:, m, :].bitcast(F32),
                                            ALU.subtract).then_inc(h_lo, 1)

            iteration(0, 0, 0)
            with dve.Fori(0, (EXPERTS - 2) // 2) as i:
                iteration(2 * i + 1, 1, i)
                iteration(2 * i + 2, 0, i + 1)
            iteration(EXPERTS - 1, 1, (EXPERTS - 2) // 2)

            dve.wait_ge(base_ready, 1)
            for g in range(GROUPS):
                for m in range(KC):
                    dve.wait_ge(y_ready, 2 * g + m + 1)
                    last = nc.vector.tensor_tensor(outbuf[:, m, cols(g, TOKENS)], h[:, m, cols(g, TOKENS)],
                                                   ps[0:CH, 4 + 2 * g + m, 0:NG], ALU.add)
                last.then_inc(out_ready, 1)

        @block.tensor
        def _(pe):
            def product(dst, pairs):
                for i, (lhsT, rhs) in enumerate(pairs):
                    last = nc.tensor.matmul(dst, lhsT, rhs, start=i == 0, stop=i == len(pairs) - 1)
                return last

            def layernorm(n, T, src, wait_src):
                for g in range(GROUPS):
                    wait_src(g)
                    product(ps[0:CH, MEAN[g], 0:GI * T],
                            [(mean_w[:], src[:, k, cols(g, T)]) for k in range(KC)]).then_inc(ln_mean, 1)
                for g in range(GROUPS):
                    pe.wait_ge(ln_sq, GROUPS * n + g + 1)
                    product(ps[0:CH, VAR[g], 0:GI * T],
                            [(mean_w[:], sq[:, k, cols(g, T)]) for k in range(KC)]).then_inc(ln_var, 1)

            def feed_forward(f, src, wait_src):
                for g in range(GROUPS):
                    wait_src(g)
                    for m in range(FC):
                        t = (f * GROUPS + g) * FC + m
                        if t >= 4:
                            pe.wait_ge(ff1_gelu, t - 3)
                        product(ps[:, t % 4, 0:GI * PATCHES],
                                [(ff1_w[:, k, m * 128:(m + 1) * 128], src[:, k, cols(g, PATCHES)])
                                 for k in range(KC)]).then_inc(ff1_ready, 1)
                for g in range(GROUPS):
                    pe.wait_ge(ff1_gelu, (f * GROUPS + g + 1) * FC)
                    for m in range(KC):
                        product(ps[0:CH, 4 + 2 * g + m, 0:GI * PATCHES],
                                [(ff2_w[:, k, m * CH:(m + 1) * CH], hid[:, k, cols(g, PATCHES)])
                                 for k in range(FC)]).then_inc(ff2_ready, 1)

            def queries_keys(a, blk, T, src, wait_src):
                for g in range(GROUPS):
                    wait_src(g)
                    for c in range(HC):
                        t = (a * GROUPS + g) * HC + c
                        if t >= 2:
                            pe.wait_ge(q_taken, t - 1)
                            pe.wait_ge(k_taken, t - 1)
                        for w, bank, done in ((wq, t % 2, q_ready), (wk, 2 + t % 2, k_ready)):
                            product(ps[:, bank, 0:GI * T],
                                    [(w[blk][:, k, c * 128:(c + 1) * 128], src[:, k, cols(g, T)])
                                     for k in range(KC)]).then_inc(done, 1)

            def value_bias(blk, name):
                for m in range(KC):
                    last = product(ps[0:CH, 7, m:m + 1],
                                   [(wo[blk][:, c, m * CH:(m + 1) * CH], col(name, c)) for c in range(HC)])
                last.then_inc(pbe_ready, 1)

            def values(b, k, T, blk, bank, taken, before, done):
                pe.wait_ge(x_copied, IMAGES * k + b + 1)
                if not (isinstance(b, int) and before + b == 0):
                    pe.wait_ge(taken, before + b)
                product(ps[0:T, bank, 0:D],
                        [(x_img[:, c, 0:T], wv[blk][:, c, :]) for c in range(KC)]).then_inc(done, 1)

            def attention(a, k, T, blk):
                def scores(b):
                    n = IMAGES * a + b
                    pe.wait_ge(q_copied, IMAGES * k + b + 1)
                    pe.wait_ge(sub_done, n)
                    for c in range(HC):
                        last = nc.tensor.matmul(
                            ps[0:T, c, 0:HPC * T].rearrange("p (h t) -> p h t", t=T),
                            q_img[:, c, 0:T], kbd[:, c, :, bass.ds(b * T, T)], start=True, stop=True)
                    last.then_inc(s_ready, 1)

                def transposes(b):
                    n = IMAGES * a + b
                    have("ident")
                    pe.wait_ge(exp_done, n + 1)
                    for i in range(HEADS):
                        j, o = divmod(i, HEADS // 2)
                        last = nc.tensor.transpose(ps[0:T, PT0 + j, o * T:(o + 1) * T], eprob[0:T, i, 0:T],
                                                   ident[0:T, 0:T])
                    last.then_inc(pt_ready, 1)

                def weigh(b):
                    n = IMAGES * a + b
                    pe.wait_ge(consts_set, 1)
                    pe.wait_ge(pt_taken, n + 1)
                    pe.wait_ge(v_taken, n + 1)
                    if not (isinstance(n, int) and n == 0):
                        pe.wait_ge(o_done, n)
                    for i in range(HEADS):
                        c, j = divmod(i, HPC)
                        last = nc.tensor.matmul(ps[PAD * j:PAD * (j + 1), OB, c * T:(c + 1) * T],
                                                vpad[0:T, i, :], probT[0:T, i, 0:T], start=True, stop=True)
                    last.then_inc(o_ready, 1)

                def vals(b):
                    values(b, k, T, blk, VB, v_taken, IMAGES * a, v_ready)

                pe.wait_ge(k_taken, GROUPS * HC * (a + 1))
                def step(b):
                    scores(b + 1)
                    transposes(b)
                    weigh(b)
                    vals(b + 1)

                scores(0)
                vals(0)
                step(0)
                with pe.Fori(1, IMAGES - 1) as b:
                    step(b)
                transposes(IMAGES - 1)
                weigh(IMAGES - 1)

            def project(blk, T, wait_src):
                for g in range(GROUPS):
                    wait_src(g)
                    for m in range(KC):
                        product(ps[0:CH, 4 + 2 * g + m, 0:GI * T],
                                [(wo[blk][:, c, m * CH:(m + 1) * CH], oT[:, c, cols(g, T)])
                                 for c in range(HC)]).then_inc(proj_ready, 1)

            def have(*names):
                for name in names:
                    pe.wait_ge(loaded[name], 16)

            have("patches", "patch_w")
            for g in range(GROUPS):
                for m in range(KC):
                    product(ps[0:CH, 2 * g + m, 0:GI * PATCHES],
                            [(patch_w[:, k, m * CH:(m + 1) * CH], patches[:, k, cols(g, PATCHES)])
                             for k in range(FC)]).then_inc(patch_ready, 1)
            have("mean_w")
            layernorm(0, PATCHES, tokx, lambda g: pe.wait_ge(tokx_ready, g + 1))
            have("ff1_w", "ff2_w")
            feed_forward(0, id0, lambda g: pe.wait_ge(id0_ready, g + 1))
            have("tok_wq", "tok_wk", "tok_wv", "tok_wo", "ident", "cols128")
            queries_keys(0, "tok", PATCHES, ffo, lambda g: pe.wait_ge(ff2_taken, 2 * (g + 1)))
            value_bias("tok", "tok_v_b")
            attention(0, 0, PATCHES, "tok")
            project("tok", PATCHES, lambda g: pe.wait_ge(o_done, GI * (g + 1)))
            feed_forward(1, x1, lambda g: pe.wait_ge(proj_taken, 2 * (g + 1)))

            pe.wait_ge(cls_set, 1)
            layernorm(1, TOKENS, h, lambda g: pe.wait_ge(ff2_taken, 4 + 2 * (g + 1)))
            have("perf_wq", "perf_wk", "rand_w", "perf_wv", "perf_wo")
            for g in range(GROUPS):
                pe.wait_ge(ln_z, GROUPS + g + 1)
                for c in range(2 * HC):
                    t = 2 * HC * g + c
                    if t >= 4:
                        pe.wait_ge(f_done, t - 3)
                    w = wq["perf"] if c < HC else wk["perf"]
                    o = (c % HC) * 128
                    product(ps[:, t % 4, 0:NG], [(w[:, k, o:o + 128], nrm[:, k, cols(g, TOKENS)])
                                                 for k in range(KC)]).then_inc(f_ready, 1)
            for g in range(GROUPS):
                pe.wait_ge(f_done, 2 * HC * g + HC)
                for c in range(HC):
                    t = HC * g + c
                    if t >= 2:
                        pe.wait_ge(qf_done, t - 1)
                    product(ps[:, 4 + t % 2, 0:NG],
                            [(rand_w[:, c, :], fq[:, c, cols(g, TOKENS)])]).then_inc(qf_ready, 1)

            def key_logits(b):
                pe.wait_ge(q_copied, IMAGES + b + 1)
                pe.wait_ge(kf_done, b)
                for c in range(HC):
                    last = nc.tensor.matmul(ps[0:TOKENS, KLB, c * 128:(c + 1) * 128], q_img[:, c, :],
                                            rand_w[:, c, :], start=True, stop=True)
                last.then_inc(kl_ready, 1)

            def perf_values(b):
                values(b, 1, TOKENS, "perf", PVB, perf_vtaken, 0, perf_vready)

            def keys_values(b):
                pe.wait_ge(kf_done, b + 1)
                pe.wait_ge(perf_vtaken, b + 1)
                for c in range(HC):
                    last = nc.tensor.matmul(ps[:, KVB, c * 128:(c + 1) * 128], kfeat[:, c * 128:(c + 1) * 128],
                                            vpad[:, c * HPC:(c + 1) * HPC, :], start=True, stop=True)
                last.then_inc(kv_ready, 1)

            def perf_out(b):
                pe.wait_ge(kv_taken, b + 1)
                if not (isinstance(b, int) and b == 0):
                    pe.wait_ge(perf_odone, b)
                for c in range(HC):
                    last = nc.tensor.matmul(ps[:, POB, c * TOKENS:(c + 1) * TOKENS], kvbd[:, c, :],
                                            qT[:, c, bass.ds(b * TOKENS, TOKENS)], start=True, stop=True)
                last.then_inc(perf_oready, 1)

            pe.wait_ge(f_done, 2 * GROUPS * HC)
            pe.wait_ge(qf_done, GROUPS * HC)
            key_logits(0)
            perf_values(0)
            def perf_step(b):
                keys_values(b)
                key_logits(b + 1)
                perf_values(b + 1)
                perf_out(b)

            perf_step(0)
            with pe.Fori(1, IMAGES - 1) as b:
                perf_step(b)
            keys_values(IMAGES - 1)
            perf_out(IMAGES - 1)
            project("perf", TOKENS, lambda g: pe.wait_ge(perf_odone, GI * (g + 1)))

            layernorm(2, TOKENS, h, lambda g: pe.wait_ge(proj_taken, 4 + 2 * (g + 1)))
            layernorm(3, TOKENS, x2, lambda g: pe.wait_ge(ln_z, 4 + g + 1))
            have("ffn_wq", "ffn_wk", "ffn_wv", "ffn_wo", "w_gate", "b2")
            queries_keys(1, "ffn", TOKENS, nrm, lambda g: pe.wait_ge(aff, g + 1))
            value_bias("ffn", "ffn_v_b")
            attention(1, 2, TOKENS, "ffn")
            project("ffn", TOKENS, lambda g: pe.wait_ge(o_done, IMAGES + GI * (g + 1)))
            layernorm(4, TOKENS, xp, lambda g: pe.wait_ge(proj_taken, 8 + 2 * (g + 1)))

            pe.wait_ge(aff, 2 * GROUPS)
            for t in range(GATE_TILES):
                last = product(ps[0:GATE_ROWS, 0, t * EXPERTS:(t + 1) * EXPERTS],
                               [(nrm[:, k, t * GATE_ROWS:(t + 1) * GATE_ROWS], w_gate[:, k, :])
                                for k in range(KC)])
            last.then_inc(gl_ready, 1)
            pe.wait_ge(gchain, 13)
            for t in range(GATE_TILES):
                bank, o = (2, t * GATE_ROWS) if t < 4 else (3, 0)
                last = nc.tensor.transpose(ps[0:EXPERTS, bank, o:o + GATE_ROWS], gates[:, t, :],
                                           ident[0:GATE_ROWS, 0:GATE_ROWS])
            last.then_inc(gt_ready, 1)

            pe.wait_ge(gt_taken, 2)
            for g in range(GROUPS):
                for m in range(KC):
                    nc.tensor.matmul(ps[0:CH, 4 + 2 * g + m, 0:NG], b2[:, m * CH:(m + 1) * CH],
                                     gates_T[:, cols(g, TOKENS)], start=True, stop=False)

            def first_layer(u, s, m):
                t = FC * u + m
                if not (isinstance(t, int) and t < 2):
                    pe.wait_ge(e1_gelu, t - 1)
                p = 2 * (m % 2)
                w = slice(m * 128, (m + 1) * 128)
                for g in range(GROUPS):
                    c = cols(g, TOKENS)
                    last = product(ps[:, p + g, 0:NG],
                                   [pair for k in range(KC) for pair in
                                    ((w1h[s][:, k, w], xh[:, k, c]), (w1h[s][:, k, w], xl[:, k, c]),
                                     (w1l[s][:, k, w], xh[:, k, c]))])
                last.then_inc(e1_ready, 1)

            def second_layer(u, s, m, last_expert=False):
                pe.wait_ge(h_lo, FC * u + m + 1)
                for g in range(GROUPS):
                    c = cols(g, TOKENS)
                    for o in range(KC):
                        w = slice(o * CH, (o + 1) * CH)
                        dst = ps[0:CH, 4 + 2 * g + o, 0:NG]
                        end = last_expert and m == FC - 1
                        nc.tensor.matmul(dst, w2h[s][:, m, w], hh[s][:, m, c], start=False, stop=False)
                        nc.tensor.matmul(dst, w2h[s][:, m, w], hl[s][:, m, c], start=False, stop=False)
                        last = nc.tensor.matmul(dst, w2l[s][:, m, w], hh[s][:, m, c], start=False, stop=end)
                        if end:
                            last.then_inc(y_ready, 1)

            def iteration(u, s, last=False):
                pe.wait_ge(w1_lo, u + 1)
                for m in range(FC):
                    first_layer(u, s, m)
                    if m == 0:
                        pe.wait_ge(w2_lo, u)
                    second_layer(u - 1, 1 - s, m)

            pe.wait_ge(xl_ready, GROUPS)
            pe.wait_ge(w1_lo, 1)
            for m in range(FC):
                first_layer(0, 0, m)
            with pe.Fori(0, (EXPERTS - 2) // 2) as i:
                iteration(2 * i + 1, 1)
                iteration(2 * i + 2, 0)
            iteration(EXPERTS - 1, 1)
            pe.wait_ge(w2_lo, EXPERTS)
            for m in range(FC):
                second_layer(EXPERTS - 1, 1, m, last_expert=True)


def positions():
    p = np.arange(PATCHES, dtype=np.float32)[:, None]
    i = np.arange(D // 2, dtype=np.float32)[None, :]
    angle = (p / np.power(np.float32(10000.0), np.float32(2.0) * i / np.float32(D))).astype(np.float32)
    table = np.zeros((PATCHES, D), np.float32)
    table[:, 0::2] = np.sin(angle)
    table[:, 1::2] = np.cos(angle)
    return table


def layout(a):
    def rows(w, part):
        return w.reshape(-1, part, w.shape[-1]).transpose(1, 0, 2)

    def pad_cols(w, twice=False):
        out = np.zeros((D, HEADS, PAD), np.float32)
        out[:, :, :HD] = w.reshape(D, HEADS, HD)
        if twice:
            out[:, :, HD:] = w.reshape(D, HEADS, HD)
        return rows(out.reshape(D, HEADS * PAD), CH)

    def pad_rows(w):
        out = np.zeros((HEADS, PAD, D), np.float32)
        out[:, :HD] = w.reshape(HEADS, HD, D)
        return rows(out.reshape(HEADS * PAD, D), 128)

    def pad_vec(v):
        out = np.zeros((HEADS, PAD), np.float32)
        out[:, :HD] = v.reshape(HEADS, HD)
        return out.reshape(HC, 128).T

    o = {}
    x = a["x"].reshape(IMAGES, 3, 8, 16, 8, 16)
    o["patches"] = rows(x.transpose(1, 3, 5, 0, 2, 4).reshape(HIDDEN, IMAGES * PATCHES), 128)
    o["patch_w"] = rows(a["L0_tok_patch_w"].reshape(D, HIDDEN).T, 128)
    o["ff1_w"] = rows(a["L0_tok_ff1_w"], CH)
    o["ff2_w"] = rows(a["L0_tok_ff2_w"], 128)
    for blk, w, p in (("tok", a["L0_tok_qkv_w"], a["L0_tok_proj_w"]),
                      ("perf", a["L0_attn_qkv_w"].T, a["L0_attn_proj_w"].T),
                      ("ffn", a["L0_ffn_qkv_w"].T, a["L0_ffn_proj_w"].T)):
        o[f"{blk}_wq"] = pad_cols(w[:, 0:D], blk == "perf")
        o[f"{blk}_wk"] = pad_cols(w[:, D:2 * D], blk == "perf")
        o[f"{blk}_wv"] = rows(w[:, 2 * D:3 * D], CH)
        o[f"{blk}_wo"] = pad_rows(p)
    r = np.zeros((HC, HPC, PAD, HPC, FEATURES), np.float32)
    for i in range(HEADS):
        c, j = divmod(i, HPC)
        r[c, j, :HD, j] = a["L0_attn_rand_matrix"][i]
        r[c, j, HD:, j] = 1.0
    o["rand_w"] = r.reshape(HC, 128, 128).transpose(1, 0, 2)
    o["w_gate"] = rows(a["L0_ffn_w_gate"], CH)
    o["b2"] = a["L0_ffn_b2"]
    o["w1"] = a["L0_ffn_W1"].reshape(EXPERTS, KC, CH, HIDDEN).transpose(0, 2, 1, 3)
    o["w2"] = a["L0_ffn_W2"].reshape(EXPERTS, FC, 128, D).transpose(0, 2, 1, 3)
    v96 = {"patch_b": a["L0_tok_patch_b"], "tok_ln_g": a["L0_tok_ln_g"], "tok_ln_b": a["L0_tok_ln_b"],
           "tok_ff2_b": a["L0_tok_ff2_b"], "tok_proj_b": a["L0_tok_proj_b"],
           "perf_proj_b": a["L0_attn_proj_b"], "n1_w": a["L0_ffn_norm1_w"], "n1_b": a["L0_ffn_norm1_b"],
           "ffn_proj_b": a["L0_ffn_proj_b"], "n2_w": a["L0_ffn_norm2_w"], "n2_b": a["L0_ffn_norm2_b"],
           "cls": a["cls_tok"]}
    o["cols96"] = np.concatenate([v96[n].reshape(KC, CH).T for n in COLS96], axis=1)
    upper = (np.arange(128) % PAD >= HD)[:, None]
    v128 = {"tok_ff1_b": a["L0_tok_ff1_b"].reshape(FC, 128).T,
            "b1": a["L0_ffn_b1"].reshape(EXPERTS * FC, 128).T,
            "feat_add": np.where(upper, 0.0, SCALE ** 0.5).astype(np.float32),
            "feat_mul": np.where(upper, -0.5 * SCALE, 0.0).astype(np.float32)}
    for blk, bias in (("tok", a["L0_tok_qkv_b"]), ("ffn", a["L0_ffn_qkv_b"])):
        for i, n in enumerate("qkv"):
            v128[f"{blk}_{n}_b"] = pad_vec(bias[i * D:(i + 1) * D])
    o["cols128"] = np.concatenate([v128[n] for n, _ in COLS128], axis=1)
    head = np.arange(128) // PAD
    o["ident"] = np.eye(128, dtype=np.float32)
    o["headmask"] = (head[:, None] == np.arange(HPC)[None, :]).astype(np.float32)
    o["blockmask"] = (head[:, None] == head[None, :]).astype(np.float32) / FEATURES
    e = np.arange(EXPERTS)
    o["earlier"] = np.broadcast_to((e[None, :] < e[:, None]).astype(np.float32), (128, EXPERTS, EXPERTS))
    o["pos"] = rows(positions().T, CH)
    o["mean_w"] = np.full((CH, CH), 1.0 / D, np.float32)
    return {k: np.ascontiguousarray(v, dtype=np.float32) for k, v in o.items()}


def kernel(**inputs):
    import concourse.bacc as _bacc
    from concourse.bass_utils import run_bass_kernel_spmd as _run

    nc = _bacc.Bacc("TRN2", target_bir_lowering=False, num_devices=1)
    arrays, dram = {}, {}
    for name, v in layout({k: np.asarray(v) for k, v in inputs.items()}).items():
        arrays[f"in_{name}"] = v
        dram[name] = nc.dram_tensor(f"in_{name}", v.shape, F32, kind="ExternalInput").ap()
    out = nc.dram_tensor("out_tokens", (CH, KC, ALL), F32, kind="ExternalOutput").ap()
    build_tower(nc, dram, out)
    got = _run(nc, [arrays], core_ids=[0]).results[0]["out_tokens"]
    return np.ascontiguousarray(np.asarray(got).transpose(2, 1, 0).reshape(IMAGES, TOKENS, D))
```

```python
from contextlib import ExitStack

import numpy as np

import concourse.bass as bass
from concourse import mybir

F32 = mybir.dt.float32
F32R = mybir.dt.float32r
ALU = mybir.AluOpType
ACT = mybir.ActivationFunctionType
AXX = mybir.AxisListType.X

IMAGES = 8
PATCHES = 64
TOKENS = PATCHES + 1
D = 192
CH = 96
KC = D // CH
HEADS = 12
HD = D // HEADS
PAD = 32
HPC = 128 // PAD
HC = HEADS // HPC
HQ = HEADS // KC
HIDDEN = 768
FC = HIDDEN // 128
EXPERTS = 8
GROUPS = 2
GI = IMAGES // GROUPS
ALL = IMAGES * TOKENS
NG = GI * TOKENS
GATE_ROWS = 104
GATE_TILES = ALL // GATE_ROWS
EPS = 1e-5
DENOM_EPS = 1e-12
FEATURES = 2 * HD
SCALE = float(HD) ** -0.5

COLS96 = ["patch_b", "tok_ln_g", "tok_ln_b", "tok_ff2_b", "tok_proj_b", "perf_proj_b",
          "n1_w", "n1_b", "ffn_proj_b", "n2_w", "n2_b", "cls", "tok_q_b", "tok_k_b", "ffn_q_b", "ffn_k_b"]
COLS128 = [("tok_ff1_b", FC), ("tok_v_b", HC), ("ffn_v_b", HC), ("b1", EXPERTS * FC),
           ("feat_add", 1), ("feat_mul", 1)]


def build_tower(nc, dram, out):
    ctx = ExitStack()
    with ctx:
        def sem(name):
            return ctx.enter_context(nc.semaphore(name))

        cursor = [-(-nc.sbuf_base // 64) * 64]

        def reserve(nbytes):
            at = cursor[0]
            cursor[0] += -(-nbytes // 64) * 64
            return at

        def place(name, shape, at, dt=F32):
            return nc.alloc_sbuf_tensor_at(name, shape, dt, offset=at)

        def own(name, shape, dt=F32):
            return place(name, shape, reserve(4 * int(np.prod(shape[1:]))), dt)

        ident = own("ident", [128, 128])
        headmask = own("headmask", [CH, HQ])
        earlier = own("earlier", [128, EXPERTS, EXPERTS])
        pos = own("pos", [CH, KC, PATCHES])
        pos_b = own("pos_b", [CH, KC, PATCHES])
        mean_w = own("mean_w", [CH, CH])
        cols96 = own("cols96", [CH, 2 * len(COLS96)])
        cols128 = own("cols128", [128, sum(w for _, w in COLS128)])
        w_gate = own("w_gate", [CH, KC, EXPERTS])
        b2 = own("b2", [EXPERTS, D])
        proj_b_eff = own("proj_b_eff", [CH, 2, KC])
        eps_col = own("eps_col", [CH, 1])
        eps_eps_col = own("eps_eps_col", [CH, 1])

        def vec(name, c=None):
            i = 2 * COLS96.index(name)
            return cols96[:, i:i + KC] if c is None else cols96[:, i + c:i + c + 1]

        def place128(name):
            return sum(w for _, w in COLS128[:[n for n, _ in COLS128].index(name)])

        def col(name, j):
            i = place128(name) + j
            return cols128[:, i:i + 1]

        h = own("h", [CH, KC, ALL])
        x2 = own("x2", [CH, KC, ALL])
        xp = own("xp", [CH, KC, ALL])
        nrm = own("nrm", [CH, KC, ALL])
        at_xc = reserve(4 * KC * ALL)
        at_sq = reserve(4 * KC * ALL)
        at_z = reserve(4 * KC * ALL)
        xc = place("xc", [CH, KC, ALL], at_xc)
        sq = place("sq", [CH, KC, ALL], at_sq)
        z = place("z", [CH, KC, ALL], at_z)
        rstd = own("rstd", [CH, ALL])
        rstd2 = own("rstd2", [CH, ALL])
        tokx = nrm
        id0 = x2
        ffo = nrm
        x1 = xp

        at_s1 = reserve(4 * (2 * KC * HIDDEN + 2 * FC * D))
        tok_off = [at_s1]

        def tok_place(name, shape):
            t = place(name, shape, tok_off[0])
            tok_off[0] += 4 * int(np.prod(shape[1:]))
            return t

        ff1_w = tok_place("ff1_w", [CH, KC, HIDDEN])
        ff2_w = tok_place("ff2_w", [128, FC, D])
        wq = {"tok": tok_place("tok_wq", [CH, KC, D])}
        wk = {"tok": tok_place("tok_wk", [CH, KC, D])}
        wv = {"tok": tok_place("tok_wv", [CH, KC, D])}
        wo = {"tok": tok_place("tok_wo", [128, HC, D])}
        for blk in ("perf", "ffn"):
            width = HC * 128 if blk == "perf" else D
            wq[blk] = own(f"{blk}_wq", [CH, KC, width])
            wk[blk] = own(f"{blk}_wk", [CH, KC, width])
            wv[blk] = own(f"{blk}_wv", [CH, KC, D])
            wo[blk] = own(f"{blk}_wo", [128, HC, D])
        rand_w = own("rand_w", [128, HC, 128])

        at_u = reserve(4 * 4 * FC * ALL)
        patches = place("patches", [128, FC, IMAGES * PATCHES], at_u + 4 * FC * ALL)
        patch_w = place("patch_w", [128, FC, D], at_u + 4 * 2 * FC * ALL)
        hid = place("hid", [128, FC, IMAGES * PATCHES], at_u)
        kbd = place("kbd", [CH, KC, HQ, ALL], at_u + 4 * FC * ALL)
        qS = place("qS", [CH, KC, ALL], at_u + 4 * 3 * FC * ALL)
        qT = place("qT", [128, HC, ALL], at_u + 4 * 3 * FC * ALL)
        oT = place("oT", [128, HC, ALL], at_u + 4 * 3 * FC * ALL + 4 * HC * ALL)
        prob = place("prob", [TOKENS, HEADS, TOKENS], at_u)
        eprob = place("eprob", [TOKENS, HEADS, TOKENS], at_u + 3136)
        probT = place("probT", [TOKENS, HEADS, TOKENS], at_u + 6272)
        fq = place("fq", [128, HC, ALL], at_u + 4 * FC * ALL)
        fk = place("fk", [128, HC, ALL], at_u + 4 * FC * ALL + 4 * HC * ALL)
        flin = place("flin", [128, 2, NG], at_u + 4 * FC * ALL + 8 * HC * ALL)
        hg = place("hg", [128, FC, ALL], at_u)
        hh = place("hh", [128, FC, ALL], at_u + 4 * FC * ALL, F32R)
        hl = place("hl", [128, FC, ALL], at_u + 4 * 2 * FC * ALL, F32R)

        q_img = own("q_img", [128, HC, TOKENS])
        x_img = own("x_img", [CH, KC, TOKENS])
        vpad = own("vpad", [TOKENS, HEADS, PAD])
        rowmax = own("rowmax", [TOKENS, 2, HEADS])
        den = own("den", [128, HC, TOKENS])
        rden = own("rden", [128, HC, TOKENS])
        lden = own("lden", [128, HC, TOKENS])
        o_img = own("o_img", [128, HC, TOKENS])
        kfeat = own("kfeat", [TOKENS, 2, HC * 128])
        kvbd = own("kvbd", [128, HC, 128])

        w1f = own("w1f", [CH, KC, HIDDEN])
        w2f = own("w2f", [128, FC, D])
        n1, n2 = 4 * KC * HIDDEN, 4 * FC * D
        at_s = [reserve(2 * n1 + 2 * n2), at_s1]
        w1h = [place(f"w1h{s}", [CH, KC, HIDDEN], at_s[s], F32R) for s in range(2)]
        w1l = [place(f"w1l{s}", [CH, KC, HIDDEN], at_s[s] + n1, F32R) for s in range(2)]
        w2h = [place(f"w2h{s}", [128, FC, D], at_s[s] + 2 * n1, F32R) for s in range(2)]
        w2l = [place(f"w2l{s}", [128, FC, D], at_s[s] + 2 * n1 + n2, F32R) for s in range(2)]
        gate_b = [own(f"gate_b{s}", [128, ALL]) for s in range(2)]
        gh = [place(f"gh{j}", [128, ALL], at_xc + 4 * ALL * j) for j in range(2)]
        gates_T = place("gates_T", [EXPERTS, ALL], at_sq)
        ones_row = own("ones_row", [1, 128])
        outbuf = z
        xh = own("xh", [CH, KC, ALL], F32R)
        xl = own("xl", [CH, KC, ALL], F32R)
        logit = own("logit", [GATE_ROWS, GATE_TILES, EXPERTS])
        cmp_gt = own("cmp_gt", [GATE_ROWS, GATE_TILES, EXPERTS, EXPERTS])
        cmp_eq = own("cmp_eq", [GATE_ROWS, GATE_TILES, EXPERTS, EXPERTS])
        rank = own("rank", [GATE_ROWS, GATE_TILES * EXPERTS])
        gsum = own("gsum", [GATE_ROWS, GATE_TILES])
        gates = own("gates", [GATE_ROWS, GATE_TILES, EXPERTS])

        ps = ctx.enter_context(nc.psum_tensor("ps", [128, 8, 512], F32))

        gates_dram = nc.dram_tensor("gates_by_expert", [EXPERTS, ALL], F32, kind="Internal").ap()

        PS = FC // 2
        loads = [("cols96", cols96), ("mean_w", mean_w),
                 ("pos", pos), ("ff1_w", ff1_w), ("cols128", cols128), ("tok_wo", wo["tok"]),
                 ("ffn_wo", wo["ffn"]), ("ff2_w", ff2_w),
                 ("tok_wq", wq["tok"]), ("tok_wk", wk["tok"]), ("headmask", headmask), ("ident", ident),
                 ("tok_wv", wv["tok"]),
                 ("perf_wq", wq["perf"]), ("perf_wk", wk["perf"]), ("rand_w", rand_w),
                 ("perf_wv", wv["perf"]), ("perf_wo", wo["perf"]),
                 ("ffn_wq", wq["ffn"]), ("ffn_wk", wk["ffn"]), ("ffn_wv", wv["ffn"]),
                 ("w_gate", w_gate), ("earlier", earlier), ("b2", b2)]
        loaded = {name: sem(f"loaded_{name}") for name, _ in loads}
        loaded |= {name: sem(f"loaded_{name}") for i in range(PS)
                   for name in (f"patch_w{i}", f"patches{i}_0", f"patches{i}_1")}
        patch_ready = sem("patch_ready")
        tokx_ready = sem("tokx_ready")
        posb_ready = sem("posb_ready")
        id0_ready = sem("id0_ready")
        consts_set = sem("consts_set")
        ln_mean = sem("ln_mean")
        ln_xc = sem("ln_xc")
        ln_sq = sem("ln_sq")
        ln_var = sem("ln_var")
        ln_log = sem("ln_log")
        ln_rstd = sem("ln_rstd")
        ln_z = sem("ln_z")
        twice_log = sem("twice_log")
        twice_rstd = sem("twice_rstd")
        x2_ready = sem("x2_ready")
        aff = sem("aff")
        ff1_ready = sem("ff1_ready")
        ff1_gelu = sem("ff1_gelu")
        ff2_ready = sem("ff2_ready")
        ff2_taken = sem("ff2_taken")
        cls_set = sem("cls_set")
        q_ready = sem("q_ready")
        q_taken = sem("q_taken")
        k_ready = sem("k_ready")
        k_taken = sem("k_taken")
        q_copied = sem("q_copied")
        x_copied = sem("x_copied")
        s_ready = sem("s_ready")
        max_ready = sem("max_ready")
        sub_done = sem("sub_done")
        exp_done = sem("exp_done")
        pt_ready = sem("pt_ready")
        pt_taken = sem("pt_taken")
        v_ready = sem("v_ready")
        v_taken = sem("v_taken")
        o_ready = sem("o_ready")
        den_ready = sem("den_ready")
        den_log = sem("den_log")
        rden_ready = sem("rden_ready")
        o_done = sem("o_done")
        pbe_ready = sem("pbe_ready")
        pbe_done = sem("pbe_done")
        proj_ready = sem("proj_ready")
        proj_taken = sem("proj_taken")
        f_ready = sem("f_ready")
        f_lin = sem("f_lin")
        f_done = sem("f_done")
        qf_ready = sem("qf_ready")
        qf_done = sem("qf_done")
        kl_ready = sem("kl_ready")
        kf_done = sem("kf_done")
        kv_ready = sem("kv_ready")
        kv_taken = sem("kv_taken")
        clamp_done = sem("clamp_done")
        perf_vready = sem("perf_vready")
        perf_vtaken = sem("perf_vtaken")
        perf_oready = sem("perf_oready")
        perf_den = sem("perf_den")
        perf_log = sem("perf_log")
        perf_rden = sem("perf_rden")
        perf_prod = sem("perf_prod")
        perf_better = sem("perf_better")
        perf_otaken = sem("perf_otaken")
        perf_odone = sem("perf_odone")
        xh_ready = sem("xh_ready")
        xl_ready = sem("xl_ready")
        gl_ready = sem("gl_ready")
        gchain = sem("gchain")
        gexp = sem("gexp")
        gt_ready = sem("gt_ready")
        gt_taken = sem("gt_taken")
        g0_ready = sem("g0_ready")
        g0_taken = sem("g0_taken")
        g_stored = sem("g_stored")
        g_loaded = [sem(f"g_loaded{s}") for s in range(2)]
        w1_loaded = sem("w1_loaded")
        w2_loaded = sem("w2_loaded")
        w1_hi = sem("w1_hi")
        w1_lo = sem("w1_lo")
        w2_hi = sem("w2_hi")
        w2_lo = sem("w2_lo")
        e1_ready = sem("e1_ready")
        e1_gelu = sem("e1_gelu")
        gated = sem("gated")
        h_hi = sem("h_hi")
        h_lo = sem("h_lo")
        hidden_read = sem("hidden_read")
        y_ready = sem("y_ready")
        base_ready = sem("base_ready")
        out_ready = sem("out_ready")
        stored = sem("stored")

        block = ctx.enter_context(nc.Block())

        def cols(g, tokens):
            return slice(g * GI * tokens, (g + 1) * GI * tokens)

        def mean_bank(n, g):
            return 4 * (n % 2) + 2 * g

        def var_bank(n, g):
            return 4 * (n % 2) + 2 * g + 1

        def proj_bank(p, g, m):
            return 4 * (p % 2) + 2 * g + m

        PATCH0, FF1_0, BIAS, Q0, K0, PT0, VB, OB = 4, 4, 7, 4, 6, 4, 6, 7
        KLB, PVB, KVB, POB = (0, 7), 1, 2, 3

        @block.sync
        def _(sp):
            def load_patches(i, g):
                k, c = slice(2 * i, 2 * i + 2), cols(g, PATCHES)
                sp.dma_start(patches[:, k, c], dram["patches"][:, k, c]).then_inc(loaded[f"patches{i}_{g}"], 16)

            for i in range(PS):
                k = slice(2 * i, 2 * i + 2)
                sp.dma_start(patch_w[:, k], dram["patch_w"][:, k]).then_inc(loaded[f"patch_w{i}"], 16)
                load_patches(i, 0)
            for name, dst in loads:
                if name == "ff1_w":
                    for i in range(PS):
                        load_patches(i, 1)
                sp.dma_start(dst[:], dram[name]).then_inc(loaded[name], 16)
                if name == "tok_wv":
                    sp.dma_start(w1f[:], dram["w1"][0]).then_inc(w1_loaded, 16)
                    sp.dma_start(w2f[:], dram["w2"][0]).then_inc(w2_loaded, 16)

            def first_weights(u, row):
                sp.wait_ge(w1_lo, u)
                sp.dma_start(w1f[:], row(dram["w1"])).then_inc(w1_loaded, 16)

            def second_weights(u, row):
                sp.wait_ge(w2_lo, u)
                sp.dma_start(w2f[:], row(dram["w2"])).then_inc(w2_loaded, 16)

            def next_gates(u, s):
                sp.dma_start(gate_b[s][:], gates_dram[bass.ds(u, 1), :].partition_broadcast(128)
                             ).then_inc(g_loaded[s], 16)

            first_weights(1, lambda w: w[1])
            sp.wait_ge(gt_taken, 2)
            sp.dma_start(gates_dram, gates_T[:]).then_inc(g_stored, 16)
            sp.wait_ge(g_stored, 16)
            sp.dma_start(gate_b[1][:], gates_dram[1:2, :].partition_broadcast(128)).then_inc(g_loaded[1], 16)
            second_weights(1, lambda w: w[1])
            with sp.Fori(0, (EXPERTS - 2) // 2) as i:
                for s in range(2):
                    u = 2 * i + (2 + s)
                    first_weights(u, lambda w: w[bass.ds(u, 1)].rearrange("o p k n -> (o p) k n"))
                    second_weights(u, lambda w: w[bass.ds(u, 1)].rearrange("o p k n -> (o p) k n"))
                    sp.wait_ge(gated, FC * (u - 1))
                    next_gates(u, s)

            for g in range(GROUPS):
                sp.wait_ge(out_ready, g + 1)
                sp.dma_start(out[:, :, cols(g, TOKENS)], outbuf[:, :, cols(g, TOKENS)]).then_inc(stored, 16)
            sp.wait_ge(stored, 16 * GROUPS)

        @block.gpsimd
        def _(pool):
            def copies(T, q_dst, q_src, x_src, q_read, x_read, before, rest):
                def one(b):
                    n = before + b
                    if not (isinstance(n, int) and n == 0):
                        pool.wait_ge(q_read, n)
                    nc.gpsimd.tensor_copy(q_dst[:, :, 0:T], q_src[:, :, bass.ds(b * T, T)]).then_inc(q_copied, 1)
                    if not (isinstance(n, int) and n == 0):
                        pool.wait_ge(x_read, n)
                    nc.gpsimd.tensor_copy(x_img[:, :, 0:T], x_src[:, :, bass.ds(b * T, T)]).then_inc(x_copied, 1)
                one(0)
                rest()
                with pool.Fori(1, IMAGES) as b:
                    one(b)

            def lo1(s, u):
                pool.wait_ge(w1_hi, u + 1)
                nc.gpsimd.tensor_tensor(w1l[s][:], w1f[:], w1h[s][:].bitcast(F32), ALU.subtract).then_inc(w1_lo, 1)

            def lo2(s, u):
                pool.wait_ge(w2_hi, u + 1)
                nc.gpsimd.tensor_tensor(w2l[s][:], w2f[:], w2h[s][:].bitcast(F32), ALU.subtract).then_inc(w2_lo, 1)

            q_half = q_img[0:CH, 0:KC, :]
            pool.wait_ge(q_taken, KC)
            copies(PATCHES, q_half, qS, ffo, s_ready, v_ready, 0, lambda: pool.wait_ge(q_taken, GROUPS * KC))
            lo1(0, 0)
            pool.wait_ge(f_done, 2 * HC)
            copies(TOKENS, q_img[:], fk, nrm, kl_ready, perf_vready, 0, lambda: pool.wait_ge(f_done, 2 * GROUPS * HC))
            for g in range(GROUPS):
                c = cols(g, TOKENS)
                pool.wait_ge(ln_rstd, 2 * GROUPS + g + 1)
                nc.gpsimd.tensor_tensor(x2[:, :, c], xc[:, :, c],
                                        rstd[:, c].unsqueeze(1).to_broadcast([CH, KC, NG]),
                                        ALU.mult).then_inc(x2_ready, 1)
            pool.wait_ge(q_taken, GROUPS * KC + KC)
            copies(TOKENS, q_half, qS, nrm, s_ready, v_ready, IMAGES,
                   lambda: pool.wait_ge(q_taken, 2 * GROUPS * KC))

            for g in range(GROUPS):
                c = cols(g, TOKENS)
                pool.wait_ge(xh_ready, g + 1)
                nc.gpsimd.tensor_tensor(xl[:, :, c], nrm[:, :, c], xh[:, :, c].bitcast(F32),
                                        ALU.subtract).then_inc(xl_ready, 1)

            def iteration(u, s, last=False):
                if not last:
                    lo1(1 - s, u + 1)
                lo2(s, u)

            iteration(0, 0)
            with pool.Fori(0, (EXPERTS - 2) // 2) as i:
                iteration(2 * i + 1, 1)
                iteration(2 * i + 2, 0)
            iteration(EXPERTS - 1, 1, last=True)

        @block.scalar
        def _(act):
            def squares(n, T, g):
                c = cols(g, T)
                act.wait_ge(ln_xc, GROUPS * n + g + 1)
                if n:
                    act.wait_ge(ln_var, GROUPS * n)
                nc.scalar.activation(sq[:, :, c], xc[:, :, c], ACT.Square).then_inc(ln_sq, 1)

            def twice_scale(n, T, g):
                c = cols(g, T)
                act.wait_ge(ln_var, GROUPS * n + g + 1)
                nc.scalar.activation(rstd2[:, c], ps[0:CH, var_bank(n, g), 0:GI * T], ACT.Ln,
                                     scale=1.0 + EPS, bias=eps_eps_col[:, 0:1]).then_inc(twice_log, 1)
                act.wait_ge(twice_log, g + 1)
                nc.scalar.activation(rstd2[:, c], rstd2[:, c], ACT.Exp, scale=-0.5).then_inc(twice_rstd, 1)

            def scale(n, T, g):
                c, v = cols(g, T), GROUPS * n + g + 1
                act.wait_ge(ln_var, v)
                nc.scalar.activation(rstd[:, c], ps[0:CH, var_bank(n, g), 0:GI * T], ACT.Ln,
                                     bias=eps_col[:, 0:1]).then_inc(ln_log, 1)
                act.wait_ge(ln_log, v)
                nc.scalar.activation(rstd[:, c], rstd[:, c], ACT.Exp, scale=-0.5).then_inc(ln_rstd, 1)

            def gelus(f):
                for g in range(GROUPS):
                    for m in range(FC):
                        t = (f * GROUPS + g) * FC + m
                        act.wait_ge(ff1_ready, t + 1)
                        nc.scalar.activation(hid[:, m, cols(g, PATCHES)], ps[:, FF1_0 + t % 4, 0:GI * PATCHES],
                                             ACT.Gelu_apprx_tanh, bias=col("tok_ff1_b", m)).then_inc(ff1_gelu, 1)

            def take_q(a, T, bias, tiles):
                for i in tiles:
                    g, c = divmod(i, KC)
                    t = a * GROUPS * KC + i
                    act.wait_ge(q_ready, t + 1)
                    nc.scalar.activation(qS[:, c, cols(g, T)], ps[0:CH, Q0 + t % 2, 0:GI * T], ACT.Identity,
                                         bias=vec(bias, c)).then_inc(q_taken, 1)

            def attention(a, T):
                def exp(b):
                    n = IMAGES * a + b
                    act.wait_ge(sub_done, n + 1)
                    act.wait_ge(pt_ready, n)
                    nc.scalar.activation(eprob[0:T, :, 0:T], prob[0:T, :, 0:T], ACT.Exp,
                                         scale=SCALE).then_inc(exp_done, 1)

                def take_v(b):
                    n = IMAGES * a + b
                    act.wait_ge(v_ready, n + 1)
                    nc.scalar.copy(vpad[0:T, :, 0:HD],
                                   ps[0:T, VB, 0:D].rearrange("p (h d) -> p h d", d=HD)).then_inc(v_taken, 1)

                def take_pt(b):
                    n = IMAGES * a + b
                    act.wait_ge(pt_ready, n + 1)
                    half = HEADS // 2
                    for j in range(2):
                        last = nc.scalar.copy(
                            probT[0:T, half * j:half * (j + 1), 0:T],
                            ps[0:T, PT0 + j, 0:half * T].rearrange("p (h t) -> p h t", t=T))
                    last.then_inc(pt_taken, 1)

                def reciprocal(b):
                    n = IMAGES * a + b
                    act.wait_ge(den_ready, n + 1)
                    nc.scalar.activation(lden[:, :, 0:T], den[:, :, 0:T], ACT.Ln).then_inc(den_log, 1)
                    act.wait_ge(den_log, n + 1)
                    nc.scalar.activation(rden[:, :, 0:T], lden[:, :, 0:T], ACT.Exp,
                                         scale=-1.0).then_inc(rden_ready, 1)

                exp(0)
                take_v(0)
                take_pt(0)
                with act.Fori(1, IMAGES) as b:
                    exp(b)
                    reciprocal(b - 1)
                    take_v(b)
                    take_pt(b)
                reciprocal(IMAGES - 1)

            def exp_and_log():
                nc.scalar.preload_act_table_set("natural_log_exp_and_others")

            exp_and_log()
            act.wait_ge(loaded["cols96"], 16)
            for g in range(GROUPS):
                for m in range(KC):
                    act.wait_ge(patch_ready, 2 * g + m + 1)
                    last = nc.scalar.activation(tokx[:, m, cols(g, PATCHES)],
                                                ps[0:CH, PATCH0 + 2 * g + m, 0:GI * PATCHES],
                                                ACT.Identity, bias=vec("patch_b", m))
                last.then_inc(tokx_ready, 1)
                if g == 0:
                    act.wait_ge(consts_set, 2)
                    squares(0, PATCHES, 0)
                    scale(0, PATCHES, 0)
            squares(0, PATCHES, 1)
            scale(0, PATCHES, 1)
            act.wait_ge(loaded["cols128"], 16)
            gelus(0)
            exp_and_log()
            take_q(0, PATCHES, "tok_q_b", range(GROUPS * KC))
            attention(0, PATCHES)
            gelus(1)
            exp_and_log()
            act.wait_ge(w1_loaded, 16)
            nc.scalar.copy(w1h[0][:], w1f[:]).then_inc(w1_hi, 1)
            def feature_input(t):
                act.wait_ge(f_ready, t + 1)
                if t >= 2:
                    act.wait_ge(f_done, t - 1)
                nc.scalar.activation(flin[:, t % 2, :], ps[:, t % 4, 0:NG], ACT.Identity,
                                     scale=col("feat_mul", 0), bias=col("feat_add", 0)).then_inc(f_lin, 1)

            squares(1, TOKENS, 0)
            scale(1, TOKENS, 0)
            squares(1, TOKENS, 1)
            feature_input(0)
            feature_input(1)
            scale(1, TOKENS, 1)
            for t in range(2, 2 * GROUPS * HC):
                feature_input(t)
            for g in range(GROUPS):
                for c in range(HC):
                    t = HC * g + c
                    act.wait_ge(qf_ready, t + 1)
                    nc.scalar.activation(qT[:, c, cols(g, TOKENS)], ps[:, 4 + t % 2, 0:NG],
                                         ACT.Exp).then_inc(qf_done, 1)

            def take_kv(b):
                act.wait_ge(kv_ready, b + 1)
                for j in range(HPC):
                    r = slice(PAD * j, PAD * (j + 1))
                    last = nc.scalar.activation(
                        kvbd[r, :, r], ps[r, KVB, 0:HC * 128].rearrange("p (c n) -> p c n", c=HC)[:, :, r],
                        ACT.Copy, scale=1.0 / FEATURES)
                last.then_inc(kv_taken, 1)

            def key_features(b, half):
                act.wait_ge(kl_ready, b + 1)
                nc.scalar.activation(kfeat[:, half], ps[0:TOKENS, KLB[half], 0:HC * 128],
                                     ACT.Exp).then_inc(kf_done, 1)

            def take_values(b):
                act.wait_ge(perf_vready, b + 1)
                if not (isinstance(b, int) and b == 0):
                    act.wait_ge(kv_ready, b)
                nc.scalar.copy(vpad[:, :, 0:HD],
                               ps[0:TOKENS, PVB, 0:D].rearrange("p (h d) -> p h d", d=HD)
                               ).then_inc(perf_vtaken, 1)

            def take_out(n):
                act.wait_ge(perf_oready, n)
                if not (isinstance(n, int) and n == 1):
                    act.wait_ge(perf_odone, n - 1)
                nc.scalar.copy(o_img[:], ps[:, POB, 0:HC * TOKENS].rearrange("p (c t) -> p c t", t=TOKENS)
                               ).then_inc(perf_otaken, 1)

            def sums_reciprocal(n):
                act.wait_ge(clamp_done, n)
                nc.scalar.activation(rden[:], lden[:], ACT.Ln).then_inc(perf_log, 1)
                act.wait_ge(perf_log, n)
                nc.scalar.activation(rden[:], rden[:], ACT.Exp, scale=-1.0).then_inc(perf_rden, 1)

            def perf_step(b, half):
                key_features(b + 1, half)
                if not (isinstance(b, int) and b == 0):
                    take_out(b)
                take_values(b + 1)
                take_kv(b)
                if not (isinstance(b, int) and b == 0):
                    sums_reciprocal(b)

            key_features(0, 0)
            take_values(0)
            perf_step(0, 1)
            perf_step(1, 0)
            perf_step(2, 1)
            with act.Fori(3, IMAGES - 1, 2) as b:
                perf_step(b, 0)
                perf_step(b + 1, 1)
            take_out(IMAGES - 1)
            take_kv(IMAGES - 1)
            sums_reciprocal(IMAGES - 1)
            take_out(IMAGES)
            sums_reciprocal(IMAGES)

            squares(2, TOKENS, 0)
            twice_scale(2, TOKENS, 0)
            scale(2, TOKENS, 0)
            squares(2, TOKENS, 1)
            take_q(1, TOKENS, "ffn_q_b", [0])
            twice_scale(2, TOKENS, 1)
            scale(2, TOKENS, 1)
            take_q(1, TOKENS, "ffn_q_b", range(1, GROUPS * KC))
            attention(1, TOKENS)
            for g in range(GROUPS):
                squares(3, TOKENS, g)
                scale(3, TOKENS, g)

            act.wait_ge(gchain, 8)
            nc.scalar.activation(gates[:], logit[:], ACT.Exp).then_inc(gexp, 1)

            def hi1(s, u):
                act.wait_ge(w1_loaded, 16 * (u + 1))
                nc.scalar.copy(w1h[s][:], w1f[:]).then_inc(w1_hi, 1)

            def hi2(s, u):
                act.wait_ge(w2_loaded, 16 * (u + 1))
                nc.scalar.copy(w2h[s][:], w2f[:]).then_inc(w2_hi, 1)

            def rounded(u, m):
                t = FC * u + m
                act.wait_ge(gated, t + 1)
                nc.scalar.copy(hh[:, m, :], gh[m % 2][:]).then_inc(h_hi, 1)

            def gelu(u, m):
                t = FC * u + m
                act.wait_ge(e1_ready, t + 1)
                p = 2 * (m % 2)
                nc.scalar.activation(hg[:, m, :].rearrange("p (g t) -> p g t", g=GROUPS), ps[:, p:p + 2, 0:NG],
                                     ACT.Gelu, bias=cols128[:, bass.ds(place128("b1") + t, 1)]).then_inc(e1_gelu, 1)

            def iteration(u, s, first=False, last=False):
                for m in range(FC):
                    if not first:
                        rounded(u - 1, m)
                    gelu(u, m)
                    if m == 1 and not last:
                        hi1(1 - s, u + 1)
                    if m == 3:
                        hi2(s, u)

            iteration(0, 0, first=True)
            with act.Fori(0, (EXPERTS - 2) // 2) as i:
                iteration(2 * i + 1, 1)
                iteration(2 * i + 2, 0)
            iteration(EXPERTS - 1, 1, last=True)
            for m in range(FC):
                if m >= FC - 2:
                    act.wait_ge(hidden_read, EXPERTS // 2 - 1 + m - (FC - 2))
                rounded(EXPERTS - 1, m)

        @block.vector
        def _(dve):
            def centre_tokens(n, T, src, g):
                dve.wait_ge(ln_mean, GROUPS * n + g + 1)
                mean = ps[0:CH, mean_bank(n, g), 0:GI * T].unsqueeze(1).to_broadcast([CH, KC, GI * T])
                c = cols(g, T)
                nc.vector.tensor_tensor(xc[:, :, c], src[:, :, c], mean, ALU.subtract).then_inc(ln_xc, 1)

            def scale_tokens(n, T, g, dst=z, by=rstd, ready=ln_rstd, turn=None):
                dve.wait_ge(ready, GROUPS * n + g + 1 if turn is None else turn)
                dve.wait_ge(ln_xc, GROUPS * n + g + 1)
                c = cols(g, T)
                nc.vector.tensor_tensor(dst[:, :, c], xc[:, :, c], by[:, c].unsqueeze(1).to_broadcast(
                    [CH, KC, GI * T]), ALU.mult).then_inc(ln_z, 1)

            def affine(n, g, w, b, dst, done):
                dve.wait_ge(ln_z, GROUPS * n + g + 1)
                for c in range(KC):
                    last = nc.vector.tensor_scalar(dst[:, c, cols(g, TOKENS)], z[:, c, cols(g, TOKENS)],
                                                   vec(w, c), vec(b, c), ALU.mult, ALU.add)
                last.then_inc(done, 1)

            def take_k(a, T, bias, tiles):
                for i in tiles:
                    g, c = divmod(i, KC)
                    t = a * GROUPS * KC + i
                    dve.wait_ge(k_ready, t + 1)
                    nc.vector.scalar_tensor_tensor(
                        kbd[:, c, :, cols(g, T)],
                        ps[0:CH, K0 + t % 2, 0:GI * T].unsqueeze(1).to_broadcast([CH, HQ, GI * T]),
                        vec(bias, c),
                        headmask[:].unsqueeze(2).to_broadcast([CH, HQ, GI * T]),
                        ALU.add, ALU.mult).then_inc(k_taken, 1)

            shuffle = [HD + i % HD for i in range(PAD)]

            def attention(a, T, between):
                first = IMAGES * a

                def centre(n, half):
                    dve.wait_ge(s_ready, n + 1)
                    sc = ps[0:T, 2 * half:2 * half + KC, 0:HQ * T].rearrange("p c (h t) -> p c h t", t=T)
                    nc.vector.tensor_reduce(rowmax[0:T, half].rearrange("p (c h) -> p c h", c=KC), sc,
                                            AXX, ALU.max).then_inc(max_ready, 1)
                    dve.wait_ge(max_ready, n + 1)
                    if not (isinstance(n, int) and n == 0):
                        dve.wait_ge(exp_done, n)
                    m = rowmax[0:T, half].rearrange("p (c h) -> p c h", c=KC).unsqueeze(3).to_broadcast(
                        [T, KC, HQ, T])
                    nc.vector.tensor_tensor(
                        prob[0:T, :, 0:T].rearrange("p (c h) t -> p c h t", c=KC), sc, m,
                        ALU.subtract).then_inc(sub_done, 1)

                def normalise(n1):
                    dve.wait_ge(consts_set, 4)
                    dve.wait_ge(o_ready, n1)
                    o = ps[:, OB, 0:HC * T].rearrange("p (c t) -> p c t", t=T)
                    nc.vector.stream_shuffle(den[:, :, 0:T], o, shuffle).then_inc(den_ready, 1)
                    dve.wait_ge(rden_ready, n1)
                    nc.vector.tensor_tensor(oT[:, :, bass.ds((n1 - first - 1) * T, T)], o, rden[:, :, 0:T],
                                            ALU.mult).then_inc(o_done, 1)

                centre(first, 0)
                centre(first + 1, 1)
                with dve.Fori(first + 1, first + IMAGES - 1, 2) as n:
                    centre(n + 1, 0)
                    normalise(n)
                    centre(n + 2, 1)
                    normalise(n + 1)
                normalise(first + IMAGES - 1)
                between()
                normalise(first + IMAGES)

            def take_proj(p, T, g, m, fn):
                dve.wait_ge(proj_ready, 4 * p + 2 * g + m + 1)
                fn(m, cols(g, T), ps[0:CH, proj_bank(p, g, m), 0:GI * T]).then_inc(proj_taken, 1)

            def proj_bias(i, name):
                dve.wait_ge(pbe_ready, i + 1)
                nc.vector.tensor_tensor(proj_b_eff[:, i, :], ps[0:CH, BIAS, 0:KC], vec(name),
                                        ALU.add).then_inc(pbe_done, 1)

            nc.vector.memset(vpad[:], 1.0).then_inc(consts_set, 1)
            nc.vector.memset(eps_eps_col[:], EPS * EPS)
            nc.vector.memset(eps_col[:], EPS).then_inc(consts_set, 1)
            nc.vector.memset(ones_row[:], 1.0).then_inc(consts_set, 1)
            nc.vector.memset(kvbd[:], 0.0).then_inc(consts_set, 1)
            dve.wait_ge(loaded["pos"], 16)
            dve.wait_ge(loaded["cols96"], 16)
            for c in range(KC):
                last = nc.vector.tensor_scalar(pos_b[:, c, :], pos[:, c, :], vec("tok_ln_b", c), None, ALU.add)
            last.then_inc(posb_ready, 1)

            def positioned(g):
                c = cols(g, PATCHES)
                dve.wait_ge(ln_z, g + 1)
                for k in range(KC):
                    last = nc.vector.scalar_tensor_tensor(
                        id0[:, k, c].rearrange("p (b t) -> p b t", t=PATCHES),
                        z[:, k, c].rearrange("p (b t) -> p b t", t=PATCHES), vec("tok_ln_g", k),
                        pos_b[:, k, :].unsqueeze(1).to_broadcast([CH, GI, PATCHES]), ALU.mult, ALU.add)
                last.then_inc(id0_ready, 1)

            centre_tokens(0, PATCHES, tokx, 0)
            scale_tokens(0, PATCHES, 0)
            dve.wait_ge(posb_ready, 1)
            positioned(0)
            centre_tokens(0, PATCHES, tokx, 1)
            scale_tokens(0, PATCHES, 1)
            positioned(1)
            def take_ff2(f, g, m, fn):
                dve.wait_ge(ff2_ready, 4 * f + 2 * g + m + 1)
                fn(g, m, cols(g, PATCHES), ps[0:CH, 2 * g + m, 0:GI * PATCHES]).then_inc(ff2_taken, 1)

            for g in range(GROUPS):
                for m in range(KC):
                    take_ff2(0, g, m, lambda g, m, c, p: nc.vector.tensor_scalar(
                        ffo[:, m, c], p, vec("tok_ff2_b", m), None, ALU.add))
            dve.wait_ge(loaded["headmask"], 16)
            take_k(0, PATCHES, "tok_k_b", range(GROUPS * KC))

            def take_tok_proj(g, m):
                take_proj(0, PATCHES, g, m, lambda m, c, p: nc.vector.scalar_tensor_tensor(
                    x1[:, m, c], p, proj_b_eff[:, 0, m:m + 1], id0[:, m, c], ALU.add, ALU.add))

            def first_half(take):
                take(0, 0)
                take(0, 1)

            proj_bias(0, "tok_proj_b")
            dve.wait_ge(pbe_done, 1)
            attention(0, PATCHES, lambda: first_half(take_tok_proj))
            take_tok_proj(1, 0)
            take_tok_proj(1, 1)
            proj_bias(1, "ffn_proj_b")
            h_img = h[:].rearrange("p k (b t) -> p k b t", t=TOKENS)
            nc.vector.tensor_copy(h_img[:, :, :, 0],
                                  vec("cls").unsqueeze(2).to_broadcast([CH, KC, IMAGES])).then_inc(cls_set, 1)

            def take_tokens(g, m):
                take_ff2(1, g, m, lambda g, m, c, p: nc.vector.scalar_tensor_tensor(
                    h_img[:, m, GI * g:GI * (g + 1), 1:TOKENS], p.rearrange("p (b t) -> p b t", t=PATCHES),
                    vec("tok_ff2_b", m), x1[:, m, c].rearrange("p (b t) -> p b t", t=PATCHES),
                    ALU.add, ALU.add))

            def feature(t):
                g, c = divmod(t, 2 * HC)
                dve.wait_ge(f_lin, t + 1)
                dst = fq if c < HC else fk
                nc.vector.tensor_tensor(dst[:, c % HC, cols(g, TOKENS)], flin[:, t % 2, :],
                                        ps[:, t % 4, 0:NG], ALU.mult).then_inc(f_done, 1)

            first_half(take_tokens)
            take_tokens(1, 0)
            dve.wait_ge(cls_set, 1)
            centre_tokens(1, TOKENS, h, 0)
            take_tokens(1, 1)
            scale_tokens(1, TOKENS, 0, nrm)
            centre_tokens(1, TOKENS, h, 1)
            feature(0)
            feature(1)
            scale_tokens(1, TOKENS, 1, nrm)
            for t in range(2, 2 * GROUPS * HC):
                feature(t)

            def normalise(n):
                dve.wait_ge(consts_set, 4)
                dve.wait_ge(perf_otaken, n)
                nc.vector.stream_shuffle(den[:], o_img[:], shuffle).then_inc(perf_den, 1)
                dve.wait_ge(perf_den, n)
                nc.vector.tensor_scalar(lden[:], den[:], DENOM_EPS, None, ALU.max).then_inc(clamp_done, 1)
                dve.wait_ge(perf_rden, n)
                nc.vector.tensor_tensor(den[:], lden[:], rden[:], ALU.mult).then_inc(perf_prod, 1)
                dve.wait_ge(perf_prod, n)
                nc.vector.scalar_tensor_tensor(den[:], den[:], 2.0, rden[:], ALU.subtract, ALU.mult
                                               ).then_inc(perf_better, 1)
                dve.wait_ge(perf_better, n)
                nc.vector.scalar_tensor_tensor(oT[:, :, bass.ds((n - 1) * TOKENS, TOKENS)], den[:], -1.0,
                                               o_img[:], ALU.mult, ALU.mult).then_inc(perf_odone, 1)

            def take_perf_proj(g, m):
                take_proj(1, TOKENS, g, m, lambda m, c, p: nc.vector.scalar_tensor_tensor(
                    h[:, m, c], p, vec("perf_proj_b", m), h[:, m, c], ALU.add, ALU.add))

            with dve.Fori(1, IMAGES) as n:
                normalise(n)
            first_half(take_perf_proj)
            normalise(IMAGES)

            def scale_twice(g):
                scale_tokens(2, TOKENS, g, z, rstd2, twice_rstd, g + 1)
                affine(2, g, "n1_w", "n1_b", nrm, aff)

            centre_tokens(2, TOKENS, h, 0)
            take_perf_proj(1, 0)
            take_perf_proj(1, 1)
            scale_twice(0)
            centre_tokens(2, TOKENS, h, 1)
            take_k(1, TOKENS, "ffn_k_b", [0])
            scale_twice(1)
            take_k(1, TOKENS, "ffn_k_b", range(1, GROUPS * KC))

            def take_ffn_proj(g, m):
                if g == m == 0:
                    dve.wait_ge(x2_ready, GROUPS)
                take_proj(2, TOKENS, g, m, lambda m, c, p: nc.vector.scalar_tensor_tensor(
                    xp[:, m, c], p, proj_b_eff[:, 1, m:m + 1], x2[:, m, c], ALU.add, ALU.add))

            dve.wait_ge(pbe_done, 2)
            attention(1, TOKENS, lambda: first_half(take_ffn_proj))
            centre_tokens(3, TOKENS, xp, 0)
            take_ffn_proj(1, 0)
            take_ffn_proj(1, 1)
            for g in range(GROUPS):
                scale_tokens(3, TOKENS, g)
                affine(3, g, "n2_w", "n2_b", nrm, aff)
                affine(3, g, "n2_w", "n2_b", xh, xh_ready)
                if g == 0:
                    centre_tokens(3, TOKENS, xp, 1)
            nc.vector.tensor_tensor(h[:], h[:], xp[:], ALU.add).then_inc(base_ready, 1)

            steps = [0]

            def step(ins):
                steps[0] += 1
                ins.then_inc(gchain, 1)
                dve.wait_ge(gchain, steps[0])

            TT, EE = GATE_TILES, EXPERTS
            dve.wait_ge(gl_ready, 1)
            dve.wait_ge(loaded["earlier"], 16)
            step(nc.vector.tensor_copy(logit[:], ps[0:GATE_ROWS, 4, 0:TT * EE].rearrange("p (t e) -> p t e", e=EE)))
            other = logit[:].unsqueeze(2).to_broadcast([GATE_ROWS, TT, EE, EE])
            own_e = logit[:].unsqueeze(3).to_broadcast([GATE_ROWS, TT, EE, EE])
            step(nc.vector.tensor_tensor(cmp_gt[:], other, own_e, ALU.is_gt))
            step(nc.vector.tensor_tensor(cmp_eq[:], other, own_e, ALU.is_equal))
            step(nc.vector.tensor_tensor(cmp_eq[:], cmp_eq[:],
                                         earlier[0:GATE_ROWS].unsqueeze(1).to_broadcast([GATE_ROWS, TT, EE, EE]),
                                         ALU.mult))
            step(nc.vector.tensor_tensor(cmp_gt[:], cmp_gt[:], cmp_eq[:], ALU.add))
            step(nc.vector.tensor_reduce(rank[:].rearrange("p (t e) -> p t e", e=EE), cmp_gt[:], AXX, ALU.add))
            step(nc.vector.tensor_reduce(gsum[:], logit[:], AXX, ALU.max))
            step(nc.vector.tensor_tensor(logit[:], logit[:],
                                         gsum[:].unsqueeze(2).to_broadcast([GATE_ROWS, TT, EE]), ALU.subtract))
            step(nc.vector.tensor_scalar(rank[:], rank[:], 2.0, None, ALU.is_lt))
            dve.wait_ge(gexp, 1)
            step(nc.vector.tensor_tensor(gates[:], gates[:], rank[:].rearrange("p (t e) -> p t e", e=EE), ALU.mult))
            step(nc.vector.tensor_reduce(gsum[:], gates[:], AXX, ALU.add))
            step(nc.vector.reciprocal(gsum[:], gsum[:]))
            step(nc.vector.tensor_tensor(gates[:], gates[:],
                                         gsum[:].unsqueeze(2).to_broadcast([GATE_ROWS, TT, EE]), ALU.mult))
            dve.wait_ge(gt_ready, 1)
            n = 4 * GATE_ROWS
            nc.vector.tensor_copy(gates_T[:, 0:n], ps[0:EE, 5, 0:n]).then_inc(gt_taken, 1)
            nc.vector.tensor_copy(gates_T[:, n:ALL], ps[0:EE, 6, 0:GATE_ROWS]).then_inc(gt_taken, 1)

            for g in range(GROUPS):
                dve.wait_ge(g0_ready, g + 1)
                nc.vector.tensor_copy(gate_b[0][:, cols(g, TOKENS)], ps[:, 4 + 3 * g, 0:NG]).then_inc(g0_taken, 1)

            def gate(t, m, s):
                dve.wait_ge(e1_gelu, t + 1)
                nc.vector.tensor_tensor(gh[m % 2][:], hg[:, m, :], gate_b[s][:], ALU.mult).then_inc(gated, 1)

            def iteration(u, s, turn, last=False):
                for m in range(FC):
                    t = FC * u + m
                    if not (isinstance(t, int) and t == 0):
                        dve.wait_ge(h_lo, t)
                    if m < FC - 1:
                        gate(t + 1, m + 1, s)
                    elif not last:
                        dve.wait_ge(g_loaded[1 - s], 16 * (turn + 1))
                        gate(t + 1, 0, 1 - s)
                    dve.wait_ge(h_hi, t + 1)
                    nc.vector.tensor_tensor(hl[:, m, :], gh[m % 2][:], hh[:, m, :].bitcast(F32),
                                            ALU.subtract).then_inc(h_lo, 1)

            dve.wait_ge(g0_taken, GROUPS)
            gate(0, 0, 0)
            iteration(0, 0, 0)
            with dve.Fori(0, (EXPERTS - 2) // 2) as i:
                iteration(2 * i + 1, 1, i)
                iteration(2 * i + 2, 0, i + 1)
            iteration(EXPERTS - 1, 1, 0, last=True)

            dve.wait_ge(base_ready, 1)
            for g in range(GROUPS):
                for m in range(KC):
                    dve.wait_ge(y_ready, 2 * g + m + 1)
                    last = nc.vector.tensor_tensor(outbuf[:, m, cols(g, TOKENS)], h[:, m, cols(g, TOKENS)],
                                                   ps[0:CH, 4 + 2 * g + m, 0:NG], ALU.add)
                last.then_inc(out_ready, 1)

        @block.tensor
        def _(pe):
            def product(dst, pairs):
                for i, (lhsT, rhs) in enumerate(pairs):
                    last = nc.tensor.matmul(dst, lhsT, rhs, start=i == 0, stop=i == len(pairs) - 1)
                return last

            def means(n, T, src, g):
                product(ps[0:CH, mean_bank(n, g), 0:GI * T],
                        [(mean_w[:], src[:, k, cols(g, T)]) for k in range(KC)]).then_inc(ln_mean, 1)

            def variances(n, T, g):
                pe.wait_ge(ln_sq, GROUPS * n + g + 1)
                product(ps[0:CH, var_bank(n, g), 0:GI * T],
                        [(mean_w[:], sq[:, k, cols(g, T)]) for k in range(KC)]).then_inc(ln_var, 1)

            def then_layernorm(n, T, src, tile, taken, turns, early=False, filler=None):
                def first_means():
                    pe.wait_ge(taken, turns[0])
                    means(n, T, src, 0)

                if early:
                    first_means()
                    tile(1, 0)
                    variances(n, T, 0)
                    tile(1, 1)
                else:
                    tile(1, 0)
                    first_means()
                    tile(1, 1)
                    variances(n, T, 0)
                pe.wait_ge(taken, turns[1])
                means(n, T, src, 1)
                if filler:
                    filler()
                variances(n, T, 1)

            def ff1_tile(f, src, g, m):
                i = g * FC + m
                t = f * GROUPS * FC + i
                if i >= 4:
                    pe.wait_ge(ff1_gelu, t - 3)
                product(ps[:, FF1_0 + t % 4, 0:GI * PATCHES],
                        [(ff1_w[:, k, m * 128:(m + 1) * 128], src[:, k, cols(g, PATCHES)])
                         for k in range(KC)]).then_inc(ff1_ready, 1)

            def ff2_tile(f, g, m):
                pe.wait_ge(ff1_gelu, (f * GROUPS + g + 1) * FC)
                product(ps[0:CH, 2 * g + m, 0:GI * PATCHES],
                        [(ff2_w[:, k, m * CH:(m + 1) * CH], hid[:, k, cols(g, PATCHES)])
                         for k in range(FC)]).then_inc(ff2_ready, 1)

            def queries_keys(a, blk, T, src, tiles):
                for i in tiles:
                    g, c = divmod(i, KC)
                    t = a * GROUPS * KC + i
                    if i >= 2:
                        pe.wait_ge(q_taken, t - 1)
                        pe.wait_ge(k_taken, t - 1)
                    for w, bank, done in ((wq, Q0 + t % 2, q_ready), (wk, K0 + t % 2, k_ready)):
                        product(ps[0:CH, bank, 0:GI * T],
                                [(w[blk][:, k, c * CH:(c + 1) * CH], src[:, k, cols(g, T)])
                                 for k in range(KC)]).then_inc(done, 1)

            def value_bias(blk, name):
                for m in range(KC):
                    last = product(ps[0:CH, BIAS, m:m + 1],
                                   [(wo[blk][:, c, m * CH:(m + 1) * CH], col(name, c)) for c in range(HC)])
                last.then_inc(pbe_ready, 1)

            def attention(a, k, T, blk):
                first = IMAGES * a

                def scores(n, half):
                    pe.wait_ge(q_copied, n + IMAGES * (k - a) + 1)
                    if not (isinstance(n, int) and n < first + 2):
                        pe.wait_ge(sub_done, n - 1)
                    for c in range(KC):
                        last = nc.tensor.matmul(
                            ps[0:T, 2 * half + c, 0:HQ * T].rearrange("p (h t) -> p h t", t=T),
                            q_img[0:CH, c, 0:T], kbd[:, c, :, bass.ds((n - first) * T, T)],
                            start=True, stop=True)
                    last.then_inc(s_ready, 1)

                def vals(n):
                    pe.wait_ge(x_copied, n + IMAGES * (k - a) + 1)
                    if not (isinstance(n, int) and n == 0):
                        pe.wait_ge(v_taken, n)
                    product(ps[0:T, VB, 0:D],
                            [(x_img[:, c, 0:T], wv[blk][:, c, :]) for c in range(KC)]).then_inc(v_ready, 1)

                def transposes(n):
                    have("ident")
                    pe.wait_ge(exp_done, n + 1)
                    if not (isinstance(n, int) and n == 0):
                        pe.wait_ge(pt_taken, n)
                    for i in range(HEADS):
                        j, o = divmod(i, HEADS // 2)
                        last = nc.tensor.transpose(ps[0:T, PT0 + j, o * T:(o + 1) * T], eprob[0:T, i, 0:T],
                                                   ident[0:T, 0:T])
                    last.then_inc(pt_ready, 1)

                def output_free(n1):
                    if not (isinstance(n1, int) and n1 == 1):
                        pe.wait_ge(o_done, n1 - 1)

                def weigh(n1):
                    pe.wait_ge(consts_set, 1)
                    pe.wait_ge(pt_taken, n1)
                    pe.wait_ge(v_taken, n1)
                    for i in range(HEADS):
                        c, j = divmod(i, HPC)
                        last = nc.tensor.matmul(ps[PAD * j:PAD * (j + 1), OB, c * T:(c + 1) * T],
                                                vpad[0:T, i, :], probT[0:T, i, 0:T], start=True, stop=True)
                    last.then_inc(o_ready, 1)

                def step(n, half, last=False):
                    if not last:
                        scores(n + 1, half)
                    output_free(n)
                    vals(n)
                    weigh(n)
                    transposes(n)

                pe.wait_ge(k_taken, KC * (GROUPS * a + 1))
                scores(first, 0)
                pe.wait_ge(k_taken, KC * GROUPS * (a + 1))
                if blk == "tok":
                    value_bias("tok", "tok_v_b")
                scores(first + 1, 1)
                vals(first)
                transposes(first)
                if blk == "tok":
                    pe.wait_ge(pbe_done, 1)
                step(first + 1, 0)
                with pe.Fori(first + 2, first + IMAGES - 2, 2) as n:
                    step(n, 1)
                    step(n + 1, 0)
                step(first + IMAGES - 2, 1)
                step(first + IMAGES - 1, 0, last=True)
                pe.wait_ge(o_done, first + GI)
                project(k, blk, T, 0, 0)
                project(k, blk, T, 0, 1)
                output_free(first + IMAGES)
                weigh(first + IMAGES)

            def project(p, blk, T, g, m):
                product(ps[0:CH, proj_bank(p, g, m), 0:GI * T],
                        [(wo[blk][:, c, m * CH:(m + 1) * CH], oT[:, c, cols(g, T)])
                         for c in range(HC)]).then_inc(proj_ready, 1)

            def have(*names):
                for name in names:
                    pe.wait_ge(loaded[name], 16)

            def patch_sums(i, g):
                for m in range(KC):
                    for k in range(2 * i, 2 * i + 2):
                        last = nc.tensor.matmul(ps[0:CH, PATCH0 + 2 * g + m, 0:GI * PATCHES],
                                                patch_w[:, k, m * CH:(m + 1) * CH],
                                                patches[:, k, cols(g, PATCHES)], start=k == 0, stop=k == FC - 1)
                    if i == PS - 1:
                        last.then_inc(patch_ready, 1)

            for i in range(PS):
                have(f"patch_w{i}", f"patches{i}_0")
                patch_sums(i, 0)
            for i in range(PS):
                have(f"patches{i}_1")
                patch_sums(i, 1)
                if i == 0:
                    have("mean_w")
                    pe.wait_ge(tokx_ready, 1)
                    means(0, PATCHES, tokx, 0)
                elif i == 1:
                    variances(0, PATCHES, 0)
            pe.wait_ge(tokx_ready, 2)
            means(0, PATCHES, tokx, 1)
            have("ff1_w")
            pe.wait_ge(id0_ready, 1)
            for m in range(FC):
                if m == 2:
                    variances(0, PATCHES, 1)
                ff1_tile(0, id0, 0, m)
            pe.wait_ge(id0_ready, 2)
            for m in range(FC):
                ff1_tile(0, id0, 1, m)
            have("ff2_w")
            for g in range(GROUPS):
                for m in range(KC):
                    ff2_tile(0, g, m)
            have("tok_wq", "tok_wk", "tok_wv", "tok_wo", "ident", "cols128")
            for g in range(GROUPS):
                pe.wait_ge(ff2_taken, 2 * (g + 1))
                queries_keys(0, "tok", PATCHES, ffo, range(KC * g, KC * (g + 1)))
            attention(0, 0, PATCHES, "tok")
            pe.wait_ge(o_done, IMAGES)
            project(0, "tok", PATCHES, 1, 0)
            project(0, "tok", PATCHES, 1, 1)
            have("ffn_wo")
            value_bias("ffn", "ffn_v_b")
            for g in range(GROUPS):
                pe.wait_ge(proj_taken, 2 * (g + 1))
                for m in range(FC):
                    if g == 0 and m == BIAS - FF1_0:
                        pe.wait_ge(pbe_done, 2)
                    ff1_tile(1, x1, g, m)
            ff2_tile(1, 0, 0)
            ff2_tile(1, 0, 1)

            have("perf_wq", "perf_wk", "rand_w", "perf_wv", "perf_wo")

            def feature_product(t):
                g, c = divmod(t, 2 * HC)
                if t >= 4:
                    pe.wait_ge(f_done, t - 3)
                w = wq["perf"] if c < HC else wk["perf"]
                o = (c % HC) * 128
                product(ps[:, t % 4, 0:NG], [(w[:, k, o:o + 128], nrm[:, k, cols(g, TOKENS)])
                                             for k in range(KC)]).then_inc(f_ready, 1)

            def first_features():
                pe.wait_ge(ln_z, GROUPS + 1)
                feature_product(0)
                feature_product(1)

            pe.wait_ge(cls_set, 1)
            then_layernorm(1, TOKENS, h, lambda g, m: ff2_tile(1, g, m), ff2_taken, (6, 8),
                           filler=first_features)
            for t in range(2, 2 * GROUPS * HC):
                if t == 2 * HC:
                    pe.wait_ge(ln_z, 2 * GROUPS)
                feature_product(t)
            for g in range(GROUPS):
                pe.wait_ge(f_done, 2 * HC * g + HC)
                for c in range(HC):
                    t = HC * g + c
                    if t >= 2:
                        pe.wait_ge(qf_done, t - 1)
                    product(ps[:, 4 + t % 2, 0:NG],
                            [(rand_w[:, c, :], fq[:, c, cols(g, TOKENS)])]).then_inc(qf_ready, 1)

            def key_logits(b, half):
                pe.wait_ge(q_copied, IMAGES + b + 1)
                if not (isinstance(b, int) and b < 2):
                    pe.wait_ge(kf_done, b - 1)
                for c in range(HC):
                    last = nc.tensor.matmul(ps[0:TOKENS, KLB[half], c * 128:(c + 1) * 128], q_img[:, c, :],
                                            rand_w[:, c, :], start=True, stop=True)
                last.then_inc(kl_ready, 1)

            def perf_values(b):
                pe.wait_ge(x_copied, IMAGES + b + 1)
                if not (isinstance(b, int) and b == 0):
                    pe.wait_ge(perf_vtaken, b)
                product(ps[0:TOKENS, PVB, 0:D],
                        [(x_img[:, c], wv["perf"][:, c, :]) for c in range(KC)]).then_inc(perf_vready, 1)

            def keys_values(b, half):
                pe.wait_ge(kf_done, b + 1)
                pe.wait_ge(perf_vtaken, b + 1)
                for c in range(HC):
                    last = nc.tensor.matmul(ps[:, KVB, c * 128:(c + 1) * 128],
                                            kfeat[:, half, c * 128:(c + 1) * 128],
                                            vpad[:, c * HPC:(c + 1) * HPC, :], start=True, stop=True)
                last.then_inc(kv_ready, 1)

            def perf_out(n):
                pe.wait_ge(kv_taken, n)
                if not (isinstance(n, int) and n == 1):
                    pe.wait_ge(perf_otaken, n - 1)
                for c in range(HC):
                    last = nc.tensor.matmul(ps[:, POB, c * TOKENS:(c + 1) * TOKENS], kvbd[:, c, :],
                                            qT[:, c, bass.ds((n - 1) * TOKENS, TOKENS)],
                                            start=True, stop=True)
                last.then_inc(perf_oready, 1)

            pe.wait_ge(f_done, 2 * GROUPS * HC)
            key_logits(0, 0)
            perf_values(0)

            def perf_step(b, half, last=False):
                if not last:
                    key_logits(b + 1, 1 - half)
                    perf_values(b + 1)
                if not (isinstance(b, int) and b == 0):
                    perf_out(b)
                keys_values(b, half)

            perf_step(0, 0)
            pe.wait_ge(qf_done, GROUPS * HC)
            perf_step(1, 1)
            with pe.Fori(2, IMAGES - 2, 2) as b:
                perf_step(b, 0)
                perf_step(b + 1, 1)
            perf_step(IMAGES - 2, 0)
            perf_step(IMAGES - 1, 1, last=True)
            pe.wait_ge(perf_odone, GI)
            project(1, "perf", TOKENS, 0, 0)
            project(1, "perf", TOKENS, 0, 1)
            perf_out(IMAGES)

            have("ffn_wq", "ffn_wk", "ffn_wv", "ffn_wo", "w_gate", "b2")
            def first_queries_keys():
                pe.wait_ge(aff, 1)
                queries_keys(1, "ffn", TOKENS, nrm, [0])

            def last_perf_proj(g, m):
                pe.wait_ge(perf_odone, IMAGES)
                project(1, "perf", TOKENS, g, m)

            then_layernorm(2, TOKENS, h, last_perf_proj, proj_taken, (6, 8), early=True,
                           filler=first_queries_keys)
            queries_keys(1, "ffn", TOKENS, nrm, range(1, KC))
            pe.wait_ge(aff, GROUPS)
            queries_keys(1, "ffn", TOKENS, nrm, range(KC, GROUPS * KC))
            attention(1, 2, TOKENS, "ffn")

            def logits(tiles):
                for t in tiles:
                    last = product(ps[0:GATE_ROWS, 4, t * EXPERTS:(t + 1) * EXPERTS],
                                   [(nrm[:, k, t * GATE_ROWS:(t + 1) * GATE_ROWS], w_gate[:, k, :])
                                    for k in range(KC)])
                return last

            def first_logits():
                pe.wait_ge(aff, GROUPS + 1)
                logits(range(NG // GATE_ROWS))

            def last_ffn_proj(g, m):
                pe.wait_ge(o_done, 2 * IMAGES)
                project(2, "ffn", TOKENS, g, m)

            then_layernorm(3, TOKENS, xp, last_ffn_proj, proj_taken, (10, 12), early=True,
                           filler=first_logits)
            pe.wait_ge(aff, 2 * GROUPS)
            logits(range(NG // GATE_ROWS, GATE_TILES)).then_inc(gl_ready, 1)

            def gates_by_expert():
                pe.wait_ge(gchain, 13)
                for t in range(GATE_TILES):
                    bank, o = (5, t * GATE_ROWS) if t < 4 else (6, 0)
                    last = nc.tensor.transpose(ps[0:EXPERTS, bank, o:o + GATE_ROWS], gates[:, t, :],
                                               ident[0:GATE_ROWS, 0:GATE_ROWS])
                last.then_inc(gt_ready, 1)

            def first_gates():
                pe.wait_ge(gt_taken, 2)
                for g in range(GROUPS):
                    nc.tensor.matmul(ps[:, 4 + 3 * g, 0:NG], ones_row[:], gates_T[0:1, cols(g, TOKENS)],
                                     start=True, stop=True).then_inc(g0_ready, 1)

            def second_biases():
                pe.wait_ge(g0_taken, GROUPS)
                for g in range(GROUPS):
                    for m in range(KC):
                        nc.tensor.matmul(ps[0:CH, 4 + 2 * g + m, 0:NG], b2[:, m * CH:(m + 1) * CH],
                                         gates_T[:, cols(g, TOKENS)], start=True, stop=False)

            def first_layer(u, s, m):
                t = FC * u + m
                if not (isinstance(t, int) and t < 2):
                    pe.wait_ge(e1_gelu, t - 1)
                p = 2 * (m % 2)
                w = slice(m * 128, (m + 1) * 128)
                for g in range(GROUPS):
                    c = cols(g, TOKENS)
                    last = product(ps[:, p + g, 0:NG],
                                   [pair for k in range(KC) for pair in
                                    ((w1h[s][:, k, w], xh[:, k, c]), (w1h[s][:, k, w], xl[:, k, c]),
                                     (w1l[s][:, k, w], xh[:, k, c]))])
                last.then_inc(e1_ready, 1)

            def second_layer(u, s, m, last_expert=False):
                pe.wait_ge(h_lo, FC * u + m + 1)
                for g in range(GROUPS):
                    c = cols(g, TOKENS)
                    for o in range(KC):
                        w = slice(o * CH, (o + 1) * CH)
                        dst = ps[0:CH, 4 + 2 * g + o, 0:NG]
                        end = last_expert and m == FC - 1
                        nc.tensor.matmul(dst, w2h[s][:, m, w], hh[:, m, c], start=False, stop=False)
                        nc.tensor.matmul(dst, w2h[s][:, m, w], hl[:, m, c], start=False, stop=False)
                        last = nc.tensor.matmul(dst, w2l[s][:, m, w], hh[:, m, c], start=False, stop=end)
                        if end:
                            last.then_inc(y_ready, 1)
                return last

            def iteration(u, s):
                pe.wait_ge(w1_lo, u + 1)
                for m in range(FC):
                    first_layer(u, s, m)
                    if m == 0:
                        if not isinstance(u, int):
                            second_layer(u - 2, s, FC - 1)
                        continue
                    if m == 1:
                        pe.wait_ge(w2_lo, u)
                        if isinstance(u, int):
                            second_biases()
                    last = second_layer(u - 1, 1 - s, m - 1)
                return last

            pe.wait_ge(xl_ready, GROUPS)
            pe.wait_ge(w1_lo, 1)
            for m in range(FC):
                first_layer(0, 0, m)
                if m == FC - 2:
                    gates_by_expert()
            first_gates()
            iteration(1, 1)
            with pe.Fori(1, EXPERTS // 2) as i:
                iteration(2 * i, 0)
                iteration(2 * i + 1, 1).then_inc(hidden_read, 1)
            second_layer(EXPERTS - 2, 0, FC - 1).then_inc(hidden_read, 1)
            pe.wait_ge(w2_lo, EXPERTS)
            for m in range(FC):
                second_layer(EXPERTS - 1, 1, m, last_expert=True)


def positions():
    p = np.arange(PATCHES, dtype=np.float32)[:, None]
    i = np.arange(D // 2, dtype=np.float32)[None, :]
    angle = (p / np.power(np.float32(10000.0), np.float32(2.0) * i / np.float32(D))).astype(np.float32)
    table = np.zeros((PATCHES, D), np.float32)
    table[:, 0::2] = np.sin(angle)
    table[:, 1::2] = np.cos(angle)
    return table


def layout(a):
    def rows(w, part):
        return w.reshape(-1, part, w.shape[-1]).transpose(1, 0, 2)

    def twice(w):
        w = w.reshape(D, HEADS, HD)
        return rows(np.concatenate([w, w], axis=2).reshape(D, HEADS * PAD), CH)

    def pad_rows(w):
        out = np.zeros((HEADS, PAD, D), np.float32)
        out[:, :HD] = w.reshape(HEADS, HD, D)
        return rows(out.reshape(HEADS * PAD, D), 128)

    def pad_vec(v):
        out = np.zeros((HEADS, PAD), np.float32)
        out[:, :HD] = v.reshape(HEADS, HD)
        return out.reshape(HC, 128).T

    o = {}
    x = a["x"].reshape(IMAGES, 3, 8, 16, 8, 16)
    o["patches"] = rows(x.transpose(1, 3, 5, 0, 2, 4).reshape(HIDDEN, IMAGES * PATCHES), 128)
    o["patch_w"] = rows(a["L0_tok_patch_w"].reshape(D, HIDDEN).T, 128)
    o["ff1_w"] = rows(a["L0_tok_ff1_w"], CH)
    o["ff2_w"] = rows(a["L0_tok_ff2_w"], 128)
    for blk, w, p in (("tok", a["L0_tok_qkv_w"], a["L0_tok_proj_w"]),
                      ("perf", a["L0_attn_qkv_w"].T, a["L0_attn_proj_w"].T),
                      ("ffn", a["L0_ffn_qkv_w"].T, a["L0_ffn_proj_w"].T)):
        cut = twice if blk == "perf" else (lambda m: rows(m, CH))
        o[f"{blk}_wq"] = cut(w[:, 0:D])
        o[f"{blk}_wk"] = cut(w[:, D:2 * D])
        o[f"{blk}_wv"] = rows(w[:, 2 * D:3 * D], CH)
        o[f"{blk}_wo"] = pad_rows(p)
    r = np.zeros((HC, HPC, PAD, HPC, FEATURES), np.float32)
    for i in range(HEADS):
        c, j = divmod(i, HPC)
        r[c, j, :HD, j] = a["L0_attn_rand_matrix"][i]
        r[c, j, HD:, j] = 1.0
    o["rand_w"] = r.reshape(HC, 128, 128).transpose(1, 0, 2)
    o["w_gate"] = rows(a["L0_ffn_w_gate"], CH)
    o["b2"] = a["L0_ffn_b2"]
    o["w1"] = a["L0_ffn_W1"].reshape(EXPERTS, KC, CH, HIDDEN).transpose(0, 2, 1, 3)
    o["w2"] = a["L0_ffn_W2"].reshape(EXPERTS, FC, 128, D).transpose(0, 2, 1, 3)
    v96 = {"patch_b": a["L0_tok_patch_b"], "tok_ln_g": a["L0_tok_ln_g"], "tok_ln_b": a["L0_tok_ln_b"],
           "tok_ff2_b": a["L0_tok_ff2_b"], "tok_proj_b": a["L0_tok_proj_b"],
           "perf_proj_b": a["L0_attn_proj_b"], "n1_w": a["L0_ffn_norm1_w"], "n1_b": a["L0_ffn_norm1_b"],
           "ffn_proj_b": a["L0_ffn_proj_b"], "n2_w": a["L0_ffn_norm2_w"], "n2_b": a["L0_ffn_norm2_b"],
           "cls": a["cls_tok"]}
    for blk, bias in (("tok", a["L0_tok_qkv_b"]), ("ffn", a["L0_ffn_qkv_b"])):
        v96[f"{blk}_q_b"], v96[f"{blk}_k_b"] = bias[0:D], bias[D:2 * D]
    o["cols96"] = np.concatenate([v96[n].reshape(KC, CH).T for n in COLS96], axis=1)
    upper = (np.arange(128) % PAD >= HD)[:, None]
    v128 = {"tok_ff1_b": a["L0_tok_ff1_b"].reshape(FC, 128).T,
            "b1": a["L0_ffn_b1"].reshape(EXPERTS * FC, 128).T,
            "feat_add": np.where(upper, 0.0, SCALE ** 0.5).astype(np.float32),
            "feat_mul": np.where(upper, -0.5 * SCALE, 0.0).astype(np.float32)}
    for blk, bias in (("tok", a["L0_tok_qkv_b"]), ("ffn", a["L0_ffn_qkv_b"])):
        v128[f"{blk}_v_b"] = pad_vec(bias[2 * D:])
    o["cols128"] = np.concatenate([v128[n] for n, _ in COLS128], axis=1)
    head = np.arange(CH) // HD
    o["ident"] = np.eye(128, dtype=np.float32)
    o["headmask"] = (head[:, None] == np.arange(HQ)[None, :]).astype(np.float32)
    e = np.arange(EXPERTS)
    o["earlier"] = np.broadcast_to((e[None, :] < e[:, None]).astype(np.float32), (128, EXPERTS, EXPERTS))
    o["pos"] = rows(positions().T, CH)
    o["mean_w"] = np.full((CH, CH), 1.0 / D, np.float32)
    return {k: np.ascontiguousarray(v, dtype=np.float32) for k, v in o.items()}


def kernel(**inputs):
    import concourse.bacc as _bacc
    from concourse.bass_utils import run_bass_kernel_spmd as _run

    nc = _bacc.Bacc("TRN2", target_bir_lowering=False, num_devices=1)
    arrays, dram = {}, {}
    for name, v in layout({k: np.asarray(v) for k, v in inputs.items()}).items():
        arrays[f"in_{name}"] = v
        dram[name] = nc.dram_tensor(f"in_{name}", v.shape, F32, kind="ExternalInput").ap()
    out = nc.dram_tensor("out_tokens", (CH, KC, ALL), F32, kind="ExternalOutput").ap()
    build_tower(nc, dram, out)
    got = _run(nc, [arrays], core_ids=[0]).results[0]["out_tokens"]
    return np.ascontiguousarray(np.asarray(got).transpose(2, 1, 0).reshape(IMAGES, TOKENS, D))
```

```python
from contextlib import ExitStack

import numpy as np

import concourse.bass as bass
from concourse import mybir

F32 = mybir.dt.float32
F32R = mybir.dt.float32r
ALU = mybir.AluOpType
ACT = mybir.ActivationFunctionType
AXX = mybir.AxisListType.X

IMAGES = 8
PATCHES = 64
TOKENS = PATCHES + 1
D = 192
CH = 96
KC = D // CH
HEADS = 12
HD = D // HEADS
PAD = 32
HPC = 128 // PAD
HC = HEADS // HPC
HQ = HEADS // KC
HIDDEN = 768
FC = HIDDEN // 128
EXPERTS = 8
GROUPS = 2
GI = IMAGES // GROUPS
ALL = IMAGES * TOKENS
NG = GI * TOKENS
GATE_ROWS = 104
GATE_TILES = ALL // GATE_ROWS
TAIL = D - 128
ROWS0 = [*range(CH), *range(CH + TAIL, D)]
ROWS1 = [*range(CH, CH + TAIL)]
WT = 2
XT = 3
EPS = 1e-5
DENOM_EPS = 1e-12
FEATURES = 2 * HD
SCALE = float(HD) ** -0.5

COLS96 = ["patch_b", "tok_ln_g", "tok_ln_b", "tok_ff2_b", "tok_proj_b", "perf_proj_b",
          "n1_w", "n1_b", "ffn_proj_b", "n2_w", "n2_b", "cls", "tok_q_b", "tok_k_b", "ffn_q_b", "ffn_k_b"]
COLS128 = [("tok_ff1_b", FC), ("b1", EXPERTS * FC),
           ("feat_add", 1), ("feat_mul", 1)]


def build_tower(nc, dram, out):
    ctx = ExitStack()
    with ctx:
        def sem(name):
            return ctx.enter_context(nc.semaphore(name))

        cursor = [-(-nc.sbuf_base // 64) * 64]

        def reserve(nbytes):
            at = cursor[0]
            cursor[0] += -(-nbytes // 64) * 64
            return at

        def place(name, shape, at, dt=F32):
            return nc.alloc_sbuf_tensor_at(name, shape, dt, offset=at)

        def own(name, shape, dt=F32):
            return place(name, shape, reserve(4 * int(np.prod(shape[1:]))), dt)

        ident = own("ident", [128, 128])
        headmask = own("headmask", [CH, HQ])
        earlier = own("earlier", [128, EXPERTS, EXPERTS])
        pos = own("pos", [CH, KC, PATCHES])
        pos_b = own("pos_b", [CH, KC, PATCHES])
        mean_w = own("mean_w", [CH, CH])
        cols96 = own("cols96", [CH, 2 * len(COLS96)])
        cols128 = own("cols128", [128, sum(w for _, w in COLS128)])
        w_gate = own("w_gate", [128, WT, EXPERTS])
        b2 = own("b2", [EXPERTS, D])
        v_bias = {blk: own(f"{blk}_v_bias", [TOKENS, HEADS, HD]) for blk in ("tok", "ffn")}
        eps_col = own("eps_col", [CH, 1])
        eps_eps_col = own("eps_eps_col", [CH, 1])

        def vec(name, c=None):
            i = 2 * COLS96.index(name)
            return cols96[:, i:i + KC] if c is None else cols96[:, i + c:i + c + 1]

        def place128(name):
            return sum(w for _, w in COLS128[:[n for n, _ in COLS128].index(name)])

        def col(name, j):
            i = place128(name) + j
            return cols128[:, i:i + 1]

        h = own("h", [CH, KC, ALL])
        x2 = own("x2", [CH, KC, ALL])
        xp = own("xp", [CH, KC, ALL])
        nrm = own("nrm", [CH, KC, ALL])
        at_xc = reserve(4 * KC * ALL)
        at_sq = reserve(4 * KC * ALL)
        at_z = reserve(4 * KC * ALL)
        xc = place("xc", [CH, KC, ALL], at_xc)
        sq = place("sq", [CH, KC, ALL], at_sq)
        z = place("z", [CH, KC, ALL], at_z)
        rstd = own("rstd", [CH, ALL])
        rstd2 = own("rstd2", [CH, ALL])
        tokx = nrm
        id0 = x2
        ffo = nrm
        x1 = xp

        n1, n2 = 4 * WT * HIDDEN, 4 * FC * D
        at_s1 = reserve(2 * n1 + 2 * n2)
        tok_off = [at_s1]

        def tok_place(name, shape):
            t = place(name, shape, tok_off[0])
            tok_off[0] += 4 * int(np.prod(shape[1:]))
            return t

        ff1_w = tok_place("ff1_w", [CH, KC, HIDDEN])
        ff2_w = tok_place("ff2_w", [128, FC, D])
        wq = {"tok": tok_place("tok_wq", [CH, KC, D])}
        wk = {"tok": tok_place("tok_wk", [CH, KC, D])}
        wv = {"tok": tok_place("tok_wv", [CH, KC, D])}
        wo = {"tok": tok_place("tok_wo", [128, HC, D])}
        for blk in ("perf", "ffn"):
            width = HC * 128 if blk == "perf" else D
            wq[blk] = own(f"{blk}_wq", [CH, KC, width])
            wk[blk] = own(f"{blk}_wk", [CH, KC, width])
            wv[blk] = own(f"{blk}_wv", [CH, KC, D])
            wo[blk] = own(f"{blk}_wo", [128, HC, D])
        rand_w = own("rand_w", [128, HC, 128])

        at_u = reserve(4 * 4 * FC * ALL)
        patches = place("patches", [128, FC, IMAGES * PATCHES], at_u + 4 * FC * ALL)
        patch_w = place("patch_w", [128, FC, D], at_u + 4 * 2 * FC * ALL)
        hid = place("hid", [128, FC, IMAGES * PATCHES], at_u)
        kbd = place("kbd", [CH, KC, HQ, ALL], at_u + 4 * FC * ALL)
        qS = place("qS", [CH, KC, ALL], at_u + 4 * 3 * FC * ALL)
        qT = place("qT", [128, HC, ALL], at_u + 4 * 3 * FC * ALL)
        oT = place("oT", [128, HC, ALL], at_u + 4 * 3 * FC * ALL + 4 * HC * ALL)
        prob = place("prob", [TOKENS, HEADS, TOKENS], at_u)
        eprob = place("eprob", [TOKENS, HEADS, TOKENS], at_u + 3136)
        probT = place("probT", [TOKENS, HEADS, TOKENS], at_u + 6272)
        fq = place("fq", [128, HC, ALL], at_u + 4 * FC * ALL)
        fk = place("fk", [128, HC, ALL], at_u + 4 * FC * ALL + 4 * HC * ALL)
        flin = place("flin", [128, 2, NG], at_u + 4 * FC * ALL + 8 * HC * ALL)
        hg = place("hg", [128, FC, ALL], at_u)
        hh = place("hh", [128, FC, ALL], at_u + 4 * FC * ALL, F32R)
        hl = place("hl", [128, FC, ALL], at_u + 4 * 2 * FC * ALL, F32R)

        x3f = place("x3f", [128, WT, ALL], at_u + 4 * 3 * FC * ALL)
        x3 = place("x3", [128, XT, ALL], at_u + 4 * 3 * FC * ALL + 4 * WT * ALL, F32R)

        q_img = own("q_img", [128, HC, TOKENS])
        x_img = own("x_img", [CH, KC, TOKENS])
        vpad = own("vpad", [TOKENS, HEADS, PAD])
        rowmax = own("rowmax", [TOKENS, 2, HEADS])
        den = own("den", [128, HC, TOKENS])
        rden = own("rden", [128, HC, TOKENS])
        lden = own("lden", [128, HC, TOKENS])
        o_img = own("o_img", [128, 2, HC, TOKENS])
        clamped = own("clamped", [128, HC, TOKENS])
        sums = own("sums", [128, 2, HC, TOKENS])
        rsums = own("rsums", [128, 2, HC, TOKENS])
        better = own("better", [128, HC, TOKENS])
        kfeat = own("kfeat", [TOKENS, 2, HC * 128])
        kvbd = own("kvbd", [128, HC, 128])

        w1f = own("w1f", [128, WT, HIDDEN])
        w2f = own("w2f", [128, FC, D])
        at_s = [reserve(2 * n1 + 2 * n2), at_s1]
        w1h = [place(f"w1h{s}", [128, WT, HIDDEN], at_s[s], F32R) for s in range(2)]
        w1l = [place(f"w1l{s}", [128, WT, HIDDEN], at_s[s] + n1, F32R) for s in range(2)]
        w2h = [place(f"w2h{s}", [128, FC, D], at_s[s] + 2 * n1, F32R) for s in range(2)]
        w2l = [place(f"w2l{s}", [128, FC, D], at_s[s] + 2 * n1 + n2, F32R) for s in range(2)]
        gate_b = [own(f"gate_b{s}", [128, ALL]) for s in range(2)]
        gh = [place(f"gh{j}", [128, ALL], at_xc + 4 * ALL * j) for j in range(2)]
        gates_T = place("gates_T", [EXPERTS, ALL], at_sq)
        ones_row = own("ones_row", [1, 128])
        outbuf = z
        xh = own("xh", [CH, KC, ALL], F32R)
        xl = own("xl", [CH, KC, ALL], F32R)
        logit = own("logit", [GATE_ROWS, GATE_TILES, EXPERTS])
        cmp_gt = own("cmp_gt", [GATE_ROWS, GATE_TILES, EXPERTS, EXPERTS])
        cmp_eq = own("cmp_eq", [GATE_ROWS, GATE_TILES, EXPERTS, EXPERTS])
        rank = own("rank", [GATE_ROWS, GATE_TILES * EXPERTS])
        gsum = own("gsum", [GATE_ROWS, GATE_TILES])
        gates = own("gates", [GATE_ROWS, GATE_TILES, EXPERTS])

        ps = ctx.enter_context(nc.psum_tensor("ps", [128, 8, 512], F32))

        gates_dram = nc.dram_tensor("gates_by_expert", [EXPERTS, ALL], F32, kind="Internal").ap()

        PS = FC // 2
        loads = [("cols96", cols96), ("mean_w", mean_w),
                 ("pos", pos), ("ff1_w", ff1_w), ("cols128", cols128), ("tok_wo", wo["tok"]),
                 ("ffn_wo", wo["ffn"]), ("ff2_w", ff2_w),
                 ("tok_wq", wq["tok"]), ("tok_wk", wk["tok"]), ("headmask", headmask), ("ident", ident),
                 ("tok_wv", wv["tok"]),
                 ("perf_wq", wq["perf"]), ("perf_wk", wk["perf"]), ("rand_w", rand_w),
                 ("perf_wv", wv["perf"]), ("perf_wo", wo["perf"]),
                 ("ffn_wq", wq["ffn"]), ("ffn_wk", wk["ffn"]), ("ffn_wv", wv["ffn"]),
                 ("w_gate", w_gate), ("earlier", earlier), ("b2", b2)]
        loaded = {name: sem(f"loaded_{name}") for name, _ in loads}
        loaded |= {f"{blk}_v_bias": sem(f"loaded_{blk}_v_bias") for blk in v_bias}
        loaded |= {name: sem(f"loaded_{name}") for i in range(PS)
                   for name in (f"patch_w{i}", f"patches{i}_0", f"patches{i}_1")}
        patch_ready = sem("patch_ready")
        tokx_ready = sem("tokx_ready")
        posb_ready = sem("posb_ready")
        id0_ready = sem("id0_ready")
        consts_set = sem("consts_set")
        ln_mean = sem("ln_mean")
        ln_xc = sem("ln_xc")
        ln_sq = sem("ln_sq")
        ln_var = sem("ln_var")
        ln_log = sem("ln_log")
        ln_rstd = sem("ln_rstd")
        ln_z = sem("ln_z")
        twice_log = sem("twice_log")
        twice_rstd = sem("twice_rstd")
        x2_ready = sem("x2_ready")
        aff = sem("aff")
        ff1_ready = sem("ff1_ready")
        ff1_gelu = sem("ff1_gelu")
        ffw1_hi = sem("ffw1_hi")
        ffw1_lo = sem("ffw1_lo")
        ffw2_hi = sem("ffw2_hi")
        ffw2_lo = sem("ffw2_lo")
        hid_hi = sem("hid_hi")
        hid_lo = sem("hid_lo")
        x1_hi = sem("x1_hi")
        x1_lo = sem("x1_lo")
        ff2_ready = sem("ff2_ready")
        ff2_taken = sem("ff2_taken")
        cls_set = sem("cls_set")
        q_ready = sem("q_ready")
        q_taken = sem("q_taken")
        k_ready = sem("k_ready")
        k_taken = sem("k_taken")
        q_copied = sem("q_copied")
        x_copied = sem("x_copied")
        s_ready = sem("s_ready")
        max_ready = sem("max_ready")
        sub_done = sem("sub_done")
        exp_done = sem("exp_done")
        pt_ready = sem("pt_ready")
        pt_taken = sem("pt_taken")
        v_ready = sem("v_ready")
        v_taken = sem("v_taken")
        o_ready = sem("o_ready")
        den_ready = sem("den_ready")
        den_log = sem("den_log")
        rden_ready = sem("rden_ready")
        o_done = sem("o_done")
        proj_ready = sem("proj_ready")
        proj_taken = sem("proj_taken")
        f_ready = sem("f_ready")
        f_lin = sem("f_lin")
        f_done = sem("f_done")
        qf_ready = sem("qf_ready")
        qf_done = sem("qf_done")
        kl_ready = sem("kl_ready")
        kf_done = sem("kf_done")
        kv_ready = sem("kv_ready")
        kv_taken = sem("kv_taken")
        clamp_done = sem("clamp_done")
        perf_vready = sem("perf_vready")
        perf_vtaken = sem("perf_vtaken")
        perf_oready = sem("perf_oready")
        perf_den = sem("perf_den")
        perf_log = sem("perf_log")
        perf_rden = sem("perf_rden")
        perf_prod = sem("perf_prod")
        perf_better = sem("perf_better")
        perf_otaken = sem("perf_otaken")
        perf_odone = sem("perf_odone")
        xh_ready = sem("xh_ready")
        xl_ready = sem("xl_ready")
        gl_ready = sem("gl_ready")
        gchain = sem("gchain")
        gexp = sem("gexp")
        gt_ready = sem("gt_ready")
        gt_taken = sem("gt_taken")
        g0_ready = sem("g0_ready")
        g0_taken = sem("g0_taken")
        g_stored = sem("g_stored")
        g_loaded = [sem(f"g_loaded{s}") for s in range(2)]
        w1_loaded = [sem(f"w1_loaded{k}") for k in range(WT)]
        w2_loaded = sem("w2_loaded")
        w1_hi = [sem(f"w1_hi{k}") for k in range(WT)]
        w1_lo = [sem(f"w1_lo{k}") for k in range(WT)]
        w2_hi = sem("w2_hi")
        w2_lo = sem("w2_lo")
        e1_ready = sem("e1_ready")
        e1_gelu = sem("e1_gelu")
        gated = sem("gated")
        h_hi = sem("h_hi")
        h_lo = sem("h_lo")
        hidden_read = sem("hidden_read")
        y_ready = sem("y_ready")
        base_ready = sem("base_ready")
        out_ready = sem("out_ready")
        stored = sem("stored")

        block = ctx.enter_context(nc.Block())

        def cols(g, tokens):
            return slice(g * GI * tokens, (g + 1) * GI * tokens)

        def mean_bank(n, g):
            return (0, 2, 4, 6, 0, 2, 2, 6)[GROUPS * n + g]

        def var_bank(n, g):
            return mean_bank(n, g) + 1

        def proj_bank(p, g, m):
            return (0, 2, 4, 6, 0, 4)[GROUPS * p + g] + m

        PATCH0, FF1_0, Q0, K0, PT0, VB, OB = 4, 4, 4, 6, 4, 6, 7
        KLB, PVB, KVB, POB = (0, 7), 1, 2, 3

        @block.sync
        def _(sp):
            def load_patches(i, g):
                k, c = slice(2 * i, 2 * i + 2), cols(g, PATCHES)
                sp.dma_start(patches[:, k, c], dram["patches"][:, k, c]).then_inc(loaded[f"patches{i}_{g}"], 16)

            for i in range(PS):
                k = slice(2 * i, 2 * i + 2)
                sp.dma_start(patch_w[:, k], dram["patch_w"][:, k]).then_inc(loaded[f"patch_w{i}"], 16)
                load_patches(i, 0)
            for name, dst in loads:
                if name == "ff1_w":
                    for i in range(PS):
                        load_patches(i, 1)
                sp.dma_start(dst[:], dram[name]).then_inc(loaded[name], 16)
                if name in ("tok_wv", "ffn_wv"):
                    blk = name[:3]
                    sp.dma_start(v_bias[blk][:], dram[f"{blk}_v_bias"].partition_broadcast(TOKENS)
                                 ).then_inc(loaded[f"{blk}_v_bias"], 16)
                if name == "tok_wv":
                    for k in range(WT):
                        sp.dma_start(w1f[:, k], dram["w1"][0, :, k]).then_inc(w1_loaded[k], 16)
                    sp.dma_start(w2f[:], dram["w2"][0]).then_inc(w2_loaded, 16)

            def first_weights(u, row):
                for k in range(WT):
                    sp.wait_ge(w1_lo[k], u)
                    sp.dma_start(w1f[:, k], row(dram["w1"], k)).then_inc(w1_loaded[k], 16)

            def second_weights(u, row):
                sp.wait_ge(w2_lo, u)
                sp.dma_start(w2f[:], row(dram["w2"])).then_inc(w2_loaded, 16)

            def next_gates(u, s):
                sp.dma_start(gate_b[s][:], gates_dram[bass.ds(u, 1), :].partition_broadcast(128)
                             ).then_inc(g_loaded[s], 16)

            first_weights(1, lambda w, k: w[1, :, k])
            first_weights(2, lambda w, k: w[2, :, k])
            sp.wait_ge(gt_taken, 2)
            sp.dma_start(gates_dram, gates_T[:]).then_inc(g_stored, 16)
            sp.wait_ge(g_stored, 16)
            sp.dma_start(gate_b[1][:], gates_dram[1:2, :].partition_broadcast(128)).then_inc(g_loaded[1], 16)
            second_weights(1, lambda w: w[1])

            def loads_of(u, s, last=False):
                sp.wait_ge(gated, FC * (u - 1))
                next_gates(u, s)
                if not last:
                    first_weights(u + 1, lambda w, k: w[bass.ds(u + 1, 1), :, k].rearrange("o p n -> (o p) n"))
                second_weights(u, lambda w: w[bass.ds(u, 1)].rearrange("o p k n -> (o p) k n"))

            with sp.Fori(0, (EXPERTS - 4) // 2) as i:
                loads_of(2 * i + 2, 0)
                loads_of(2 * i + 3, 1)
            loads_of(EXPERTS - 2, 0)
            loads_of(EXPERTS - 1, 1, last=True)

            for g in range(GROUPS):
                sp.wait_ge(out_ready, g + 1)
                sp.dma_start(out[:, :, cols(g, TOKENS)], outbuf[:, :, cols(g, TOKENS)]).then_inc(stored, 16)
            sp.wait_ge(stored, 16 * GROUPS)

        @block.gpsimd
        def _(pool):
            def copies(T, q_dst, q_src, x_src, q_read, x_read, before, rest):
                def one(b):
                    n = before + b
                    if not (isinstance(n, int) and n == 0):
                        pool.wait_ge(q_read, n)
                    nc.gpsimd.tensor_copy(q_dst[:, :, 0:T], q_src[:, :, bass.ds(b * T, T)]).then_inc(q_copied, 1)
                    if not (isinstance(n, int) and n == 0):
                        pool.wait_ge(x_read, n)
                    nc.gpsimd.tensor_copy(x_img[:, :, 0:T], x_src[:, :, bass.ds(b * T, T)]).then_inc(x_copied, 1)
                one(0)
                rest()
                with pool.Fori(1, IMAGES) as b:
                    one(b)

            def lo1(s, u):
                for k in range(2):
                    pool.wait_ge(w1_hi[k], u + 1)
                    nc.gpsimd.tensor_tensor(w1l[s][:, k], w1f[:, k], w1h[s][:, k].bitcast(F32),
                                            ALU.subtract).then_inc(w1_lo[k], 1)

            def lo2(s, u):
                pool.wait_ge(w2_hi, u + 1)
                nc.gpsimd.tensor_tensor(w2l[s][:], w2f[:], w2h[s][:].bitcast(F32), ALU.subtract).then_inc(w2_lo, 1)

            pool.wait_ge(ffw2_hi, 1)
            nc.gpsimd.tensor_tensor(w2l[0][:], ff2_w[:], w2h[0][:].bitcast(F32), ALU.subtract).then_inc(ffw2_lo, 1)
            pool.wait_ge(ffw1_hi, 1)
            nc.gpsimd.tensor_tensor(w1l[0][0:CH], ff1_w[:], w1h[0][0:CH, 0:KC].bitcast(F32),
                                    ALU.subtract).then_inc(ffw1_lo, 1)
            q_half = q_img[0:CH, 0:KC, :]
            pool.wait_ge(q_taken, KC)
            copies(PATCHES, q_half, qS, ffo, s_ready, v_ready, 0, lambda: pool.wait_ge(q_taken, GROUPS * KC))
            lo1(0, 0)
            pool.wait_ge(f_done, 2 * HC)
            copies(TOKENS, q_img[:], fk, nrm, kl_ready, perf_vready, 0, lambda: pool.wait_ge(f_done, 2 * GROUPS * HC))
            for g in range(GROUPS):
                c = cols(g, TOKENS)
                pool.wait_ge(ln_rstd, 2 * GROUPS + g + 1)
                nc.gpsimd.tensor_tensor(x2[:, :, c], xc[:, :, c],
                                        rstd[:, c].unsqueeze(1).to_broadcast([CH, KC, NG]),
                                        ALU.mult).then_inc(x2_ready, 1)
            pool.wait_ge(q_taken, GROUPS * KC + KC)
            copies(TOKENS, q_half, qS, nrm, s_ready, v_ready, IMAGES,
                   lambda: pool.wait_ge(q_taken, 2 * GROUPS * KC))

            pool.wait_ge(proj_taken, 12)
            nc.gpsimd.tensor_tensor(h[:], h[:], xp[:], ALU.add).then_inc(base_ready, 1)

            def iteration(u, s, last=False):
                if not last:
                    lo1(1 - s, u + 1)
                lo2(s, u)

            iteration(0, 0)
            with pool.Fori(0, (EXPERTS - 2) // 2) as i:
                iteration(2 * i + 1, 1)
                iteration(2 * i + 2, 0)
            iteration(EXPERTS - 1, 1, last=True)

        @block.scalar
        def _(act):
            def squares(n, T, g):
                c = cols(g, T)
                act.wait_ge(ln_xc, GROUPS * n + g + 1)
                if n:
                    act.wait_ge(ln_var, GROUPS * n)
                nc.scalar.activation(sq[:, :, c], xc[:, :, c], ACT.Square).then_inc(ln_sq, 1)

            def twice_scale(n, T, g):
                c = cols(g, T)
                act.wait_ge(ln_var, GROUPS * n + g + 1)
                nc.scalar.activation(rstd2[:, c], ps[0:CH, var_bank(n, g), 0:GI * T], ACT.Ln,
                                     scale=1.0 + EPS, bias=eps_eps_col[:, 0:1]).then_inc(twice_log, 1)
                act.wait_ge(twice_log, g + 1)
                nc.scalar.activation(rstd2[:, c], rstd2[:, c], ACT.Exp, scale=-0.5).then_inc(twice_rstd, 1)

            def scale(n, T, g):
                c, v = cols(g, T), GROUPS * n + g + 1
                act.wait_ge(ln_var, v)
                nc.scalar.activation(rstd[:, c], ps[0:CH, var_bank(n, g), 0:GI * T], ACT.Ln,
                                     bias=eps_col[:, 0:1]).then_inc(ln_log, 1)
                act.wait_ge(ln_log, v)
                nc.scalar.activation(rstd[:, c], rstd[:, c], ACT.Exp, scale=-0.5).then_inc(ln_rstd, 1)

            def gelus(f, g):
                for m in range(FC):
                    t = (f * GROUPS + g) * FC + m
                    act.wait_ge(ff1_ready, t + 1)
                    nc.scalar.activation(hid[:, m, cols(g, PATCHES)], ps[:, FF1_0 + t % 4, 0:GI * PATCHES],
                                         ACT.Gelu_apprx_tanh, bias=col("tok_ff1_b", m)).then_inc(ff1_gelu, 1)

            def take_q(a, T, bias, tiles):
                for i in tiles:
                    g, c = divmod(i, KC)
                    t = a * GROUPS * KC + i
                    act.wait_ge(q_ready, t + 1)
                    nc.scalar.activation(qS[:, c, cols(g, T)], ps[0:CH, Q0 + t % 2, 0:GI * T], ACT.Identity,
                                         bias=vec(bias, c)).then_inc(q_taken, 1)

            def attention(a, T, between=None):
                def exp(b):
                    n = IMAGES * a + b
                    act.wait_ge(sub_done, n + 1)
                    act.wait_ge(pt_ready, n)
                    nc.scalar.activation(eprob[0:T, :, 0:T], prob[0:T, :, 0:T], ACT.Exp,
                                         scale=SCALE).then_inc(exp_done, 1)

                def take_pt(b):
                    n = IMAGES * a + b
                    act.wait_ge(pt_ready, n + 1)
                    half = HEADS // 2
                    for j in range(2):
                        last = nc.scalar.copy(
                            probT[0:T, half * j:half * (j + 1), 0:T],
                            ps[0:T, PT0 + j, 0:half * T].rearrange("p (h t) -> p h t", t=T))
                    last.then_inc(pt_taken, 1)

                def reciprocal(b):
                    n = IMAGES * a + b
                    act.wait_ge(den_ready, n + 1)
                    nc.scalar.activation(lden[:, :, 0:T], den[:, :, 0:T], ACT.Ln).then_inc(den_log, 1)
                    act.wait_ge(den_log, n + 1)
                    nc.scalar.activation(rden[:, :, 0:T], lden[:, :, 0:T], ACT.Exp,
                                         scale=-1.0).then_inc(rden_ready, 1)

                exp(0)
                take_pt(0)
                with act.Fori(1, IMAGES) as b:
                    exp(b)
                    reciprocal(b - 1)
                    take_pt(b)
                if between:
                    between()
                reciprocal(IMAGES - 1)

            def exp_and_log():
                nc.scalar.preload_act_table_set("natural_log_exp_and_others")

            exp_and_log()
            act.wait_ge(loaded["cols96"], 16)
            for g in range(GROUPS):
                for m in range(KC):
                    act.wait_ge(patch_ready, 2 * g + m + 1)
                    last = nc.scalar.activation(tokx[:, m, cols(g, PATCHES)],
                                                ps[0:CH, PATCH0 + 2 * g + m, 0:GI * PATCHES],
                                                ACT.Identity, bias=vec("patch_b", m))
                last.then_inc(tokx_ready, 1)
                if g == 0:
                    act.wait_ge(consts_set, 2)
                    squares(0, PATCHES, 0)
                    scale(0, PATCHES, 0)
            squares(0, PATCHES, 1)
            scale(0, PATCHES, 1)
            act.wait_ge(loaded["cols128"], 16)
            for g in range(GROUPS):
                gelus(0, g)
            exp_and_log()
            take_q(0, PATCHES, "tok_q_b", range(GROUPS * KC))

            attention(0, PATCHES)
            gelus(1, 0)
            gelus(1, 1)
            exp_and_log()
            for k in range(WT):
                act.wait_ge(w1_loaded[k], 16)
                nc.scalar.copy(w1h[0][:, k], w1f[:, k]).then_inc(w1_hi[k], 1)
            def feature_input(t):
                act.wait_ge(f_ready, t + 1)
                if t >= 2:
                    act.wait_ge(f_done, t - 1)
                nc.scalar.activation(flin[:, t % 2, :], ps[:, t % 4, 0:NG], ACT.Identity,
                                     scale=col("feat_mul", 0), bias=col("feat_add", 0)).then_inc(f_lin, 1)

            squares(1, TOKENS, 0)
            scale(1, TOKENS, 0)
            squares(1, TOKENS, 1)
            feature_input(0)
            feature_input(1)
            scale(1, TOKENS, 1)
            for t in range(2, 2 * GROUPS * HC):
                feature_input(t)
            for g in range(GROUPS):
                for c in range(HC):
                    t = HC * g + c
                    act.wait_ge(qf_ready, t + 1)
                    nc.scalar.activation(qT[:, c, cols(g, TOKENS)], ps[:, 4 + t % 2, 0:NG],
                                         ACT.Exp).then_inc(qf_done, 1)

            def take_kv(b):
                act.wait_ge(kv_ready, b + 1)
                for j in range(HPC):
                    r = slice(PAD * j, PAD * (j + 1))
                    last = nc.scalar.activation(
                        kvbd[r, :, r], ps[r, KVB, 0:HC * 128].rearrange("p (c n) -> p c n", c=HC)[:, :, r],
                        ACT.Copy, scale=1.0 / FEATURES)
                last.then_inc(kv_taken, 1)

            def key_features(b, half):
                act.wait_ge(kl_ready, b + 1)
                nc.scalar.activation(kfeat[:, half], ps[0:TOKENS, KLB[half], 0:HC * 128],
                                     ACT.Exp).then_inc(kf_done, 1)

            def take_values(b):
                act.wait_ge(perf_vready, b + 1)
                if not (isinstance(b, int) and b == 0):
                    act.wait_ge(kv_ready, b)
                nc.scalar.copy(vpad[:, :, 0:HD],
                               ps[0:TOKENS, PVB, 0:D].rearrange("p (h d) -> p h d", d=HD)
                               ).then_inc(perf_vtaken, 1)

            def take_out(n, half):
                act.wait_ge(perf_oready, n)
                if not (isinstance(n, int) and n < 3):
                    act.wait_ge(perf_odone, n - 2)
                nc.scalar.copy(o_img[:, half], ps[:, POB, 0:HC * TOKENS].rearrange(
                    "p (c t) -> p c t", t=TOKENS)).then_inc(perf_otaken, 1)

            def sums_reciprocal(n, half):
                act.wait_ge(perf_den, n)
                nc.scalar.activation(rsums[:, half], sums[:, half], ACT.Ln).then_inc(perf_log, 1)
                act.wait_ge(perf_log, n)
                nc.scalar.activation(rsums[:, half], rsums[:, half], ACT.Exp, scale=-1.0).then_inc(perf_rden, 1)

            def perf_step(b, half):
                key_features(b + 1, 1 - half)
                if not (isinstance(b, int) and b == 0):
                    take_out(b, 1 - half)
                take_values(b + 1)
                take_kv(b)
                if not (isinstance(b, int) and b == 0):
                    sums_reciprocal(b, 1 - half)

            key_features(0, 0)
            take_values(0)
            perf_step(0, 0)
            perf_step(1, 1)
            perf_step(2, 0)
            with act.Fori(3, IMAGES - 1, 2) as b:
                perf_step(b, 1)
                perf_step(b + 1, 0)
            take_out(IMAGES - 1, 0)
            take_kv(IMAGES - 1)
            sums_reciprocal(IMAGES - 1, 0)
            take_out(IMAGES, 1)
            sums_reciprocal(IMAGES, 1)

            squares(2, TOKENS, 0)
            twice_scale(2, TOKENS, 0)
            scale(2, TOKENS, 0)
            squares(2, TOKENS, 1)
            take_q(1, TOKENS, "ffn_q_b", [0])
            twice_scale(2, TOKENS, 1)
            scale(2, TOKENS, 1)
            take_q(1, TOKENS, "ffn_q_b", range(1, GROUPS * KC))
            attention(1, TOKENS, lambda: squares(3, TOKENS, 0))
            scale(3, TOKENS, 0)
            squares(3, TOKENS, 1)
            def rounded_input(g):
                c = cols(g, TOKENS)
                act.wait_ge(aff, GROUPS + g + 1)
                nc.scalar.copy(x3[:, 0, c], x3f[:, 0, c])
                nc.scalar.copy(x3[0:TAIL, 1, c], x3f[0:TAIL, 1, c]).then_inc(xh_ready, 1)

            rounded_input(0)
            scale(3, TOKENS, 1)
            rounded_input(1)

            act.wait_ge(gchain, 3)
            nc.scalar.activation(gates[:], gates[:], ACT.Exp).then_inc(gexp, 1)

            def hi1(s, u, k):
                act.wait_ge(w1_loaded[k], 16 * (u + 1))
                nc.scalar.copy(w1h[s][:, k], w1f[:, k]).then_inc(w1_hi[k], 1)

            def hi2(s, u):
                act.wait_ge(w2_loaded, 16 * (u + 1))
                nc.scalar.copy(w2h[s][:], w2f[:]).then_inc(w2_hi, 1)

            def rounded(u, m):
                t = FC * u + m
                act.wait_ge(gated, t + 1)
                nc.scalar.copy(hh[:, m, :], gh[m % 2][:]).then_inc(h_hi, 1)

            def gelu(u, m):
                t = FC * u + m
                act.wait_ge(e1_ready, t + 1)
                p = 2 * (m % 2)
                nc.scalar.activation(hg[:, m, :].rearrange("p (g t) -> p g t", g=GROUPS), ps[:, p:p + 2, 0:NG],
                                     ACT.Gelu, bias=cols128[:, bass.ds(place128("b1") + t, 1)]).then_inc(e1_gelu, 1)

            def iteration(u, s, first=False, last=False):
                for m in range(FC):
                    if not first:
                        rounded(u - 1, m)
                    gelu(u, m)
                    if m < WT and not last:
                        hi1(1 - s, u + 1, m)
                    if m == 3:
                        hi2(s, u)

            iteration(0, 0, first=True)
            with act.Fori(0, (EXPERTS - 2) // 2) as i:
                iteration(2 * i + 1, 1)
                iteration(2 * i + 2, 0)
            iteration(EXPERTS - 1, 1, last=True)
            for m in range(FC):
                if m >= FC - 2:
                    act.wait_ge(hidden_read, EXPERTS // 2 - 1 + m - (FC - 2))
                rounded(EXPERTS - 1, m)

        @block.vector
        def _(dve):
            def centre_tokens(n, T, src, g):
                dve.wait_ge(ln_mean, GROUPS * n + g + 1)
                mean = ps[0:CH, mean_bank(n, g), 0:GI * T].unsqueeze(1).to_broadcast([CH, KC, GI * T])
                c = cols(g, T)
                nc.vector.tensor_tensor(xc[:, :, c], src[:, :, c], mean, ALU.subtract).then_inc(ln_xc, 1)

            def scale_tokens(n, T, g, dst=z, by=rstd, ready=ln_rstd, turn=None):
                dve.wait_ge(ready, GROUPS * n + g + 1 if turn is None else turn)
                dve.wait_ge(ln_xc, GROUPS * n + g + 1)
                c = cols(g, T)
                nc.vector.tensor_tensor(dst[:, :, c], xc[:, :, c], by[:, c].unsqueeze(1).to_broadcast(
                    [CH, KC, GI * T]), ALU.mult).then_inc(ln_z, 1)

            def affine(n, g, w, b, dst, done):
                dve.wait_ge(ln_z, GROUPS * n + g + 1)
                for c in range(KC):
                    last = nc.vector.tensor_scalar(dst[:, c, cols(g, TOKENS)], z[:, c, cols(g, TOKENS)],
                                                   vec(w, c), vec(b, c), ALU.mult, ALU.add)
                last.then_inc(done, 1)

            def take_k(a, T, bias, tiles):
                for i in tiles:
                    g, c = divmod(i, KC)
                    t = a * GROUPS * KC + i
                    dve.wait_ge(k_ready, t + 1)
                    nc.vector.scalar_tensor_tensor(
                        kbd[:, c, :, cols(g, T)],
                        ps[0:CH, K0 + t % 2, 0:GI * T].unsqueeze(1).to_broadcast([CH, HQ, GI * T]),
                        vec(bias, c),
                        headmask[:].unsqueeze(2).to_broadcast([CH, HQ, GI * T]),
                        ALU.add, ALU.mult).then_inc(k_taken, 1)

            shuffle = [HD + i % HD for i in range(PAD)]

            def attention(a, T, blk, first_outputs, between):
                first = IMAGES * a

                def take_v(n):
                    dve.wait_ge(v_ready, n + 1)
                    nc.vector.tensor_tensor(vpad[0:T, :, 0:HD],
                                            ps[0:T, VB, 0:D].rearrange("p (h d) -> p h d", d=HD),
                                            v_bias[blk][0:T], ALU.add).then_inc(v_taken, 1)

                def centre(n, half):
                    dve.wait_ge(s_ready, n + 1)
                    sc = ps[0:T, 2 * half:2 * half + KC, 0:HQ * T].rearrange("p c (h t) -> p c h t", t=T)
                    nc.vector.tensor_reduce(rowmax[0:T, half].rearrange("p (c h) -> p c h", c=KC), sc,
                                            AXX, ALU.max).then_inc(max_ready, 1)
                    dve.wait_ge(max_ready, n + 1)
                    if not (isinstance(n, int) and n == 0):
                        dve.wait_ge(exp_done, n)
                    m = rowmax[0:T, half].rearrange("p (c h) -> p c h", c=KC).unsqueeze(3).to_broadcast(
                        [T, KC, HQ, T])
                    nc.vector.tensor_tensor(
                        prob[0:T, :, 0:T].rearrange("p (c h) t -> p c h t", c=KC), sc, m,
                        ALU.subtract).then_inc(sub_done, 1)

                def normalise(n1):
                    dve.wait_ge(consts_set, 4)
                    dve.wait_ge(o_ready, n1)
                    o = ps[:, OB, 0:HC * T].rearrange("p (c t) -> p c t", t=T)
                    nc.vector.stream_shuffle(den[:, :, 0:T], o, shuffle).then_inc(den_ready, 1)
                    dve.wait_ge(rden_ready, n1)
                    nc.vector.tensor_tensor(oT[:, :, bass.ds((n1 - first - 1) * T, T)], o, rden[:, :, 0:T],
                                            ALU.mult).then_inc(o_done, 1)

                centre(first, 0)
                centre(first + 1, 1)
                take_v(first)
                with dve.Fori(first + 1, first + IMAGES - 1, 2) as n:
                    centre(n + 1, 0)
                    normalise(n)
                    take_v(n)
                    centre(n + 2, 1)
                    normalise(n + 1)
                    take_v(n + 1)
                first_outputs()
                normalise(first + IMAGES - 1)
                take_v(first + IMAGES - 1)
                between()
                normalise(first + IMAGES)

            def take_proj(p, T, g, m, fn):
                dve.wait_ge(proj_ready, 4 * p + 2 * g + m + 1)
                fn(m, cols(g, T), ps[0:CH, proj_bank(p, g, m), 0:GI * T]).then_inc(proj_taken, 1)

            nc.vector.memset(vpad[:], 1.0).then_inc(consts_set, 1)
            nc.vector.memset(eps_eps_col[:], EPS * EPS)
            nc.vector.memset(eps_col[:], EPS).then_inc(consts_set, 1)
            nc.vector.memset(ones_row[:], 1.0).then_inc(consts_set, 1)
            nc.vector.memset(kvbd[:], 0.0).then_inc(consts_set, 1)
            dve.wait_ge(loaded["pos"], 16)
            dve.wait_ge(loaded["cols96"], 16)
            for c in range(KC):
                last = nc.vector.tensor_scalar(pos_b[:, c, :], pos[:, c, :], vec("tok_ln_b", c), None, ALU.add)
            last.then_inc(posb_ready, 1)

            def positioned(g):
                c = cols(g, PATCHES)
                dve.wait_ge(ln_z, g + 1)
                for k in range(KC):
                    last = nc.vector.scalar_tensor_tensor(
                        id0[:, k, c].rearrange("p (b t) -> p b t", t=PATCHES),
                        z[:, k, c].rearrange("p (b t) -> p b t", t=PATCHES), vec("tok_ln_g", k),
                        pos_b[:, k, :].unsqueeze(1).to_broadcast([CH, GI, PATCHES]), ALU.mult, ALU.add)
                last.then_inc(id0_ready, 1)

            centre_tokens(0, PATCHES, tokx, 0)
            scale_tokens(0, PATCHES, 0)
            dve.wait_ge(posb_ready, 1)
            positioned(0)
            centre_tokens(0, PATCHES, tokx, 1)
            scale_tokens(0, PATCHES, 1)
            positioned(1)
            def take_ff2(f, g, m, fn):
                dve.wait_ge(ff2_ready, 4 * f + 2 * g + m + 1)
                fn(g, m, cols(g, PATCHES), ps[0:CH, 2 * g + m, 0:GI * PATCHES]).then_inc(ff2_taken, 1)

            def split_hidden(f, g):
                for m in range(FC):
                    t, c = (f * GROUPS + g) * FC + m, cols(g, PATCHES)
                    dve.wait_ge(ff1_gelu, t + 1)
                    nc.vector.tensor_copy(hh[:, m, c], hid[:, m, c]).then_inc(hid_hi, 1)
                    dve.wait_ge(hid_hi, t + 1)
                    nc.vector.tensor_tensor(hl[:, m, c], hid[:, m, c], hh[:, m, c].bitcast(F32),
                                            ALU.subtract).then_inc(hid_lo, 1)

            dve.wait_ge(loaded["ff2_w"], 16)
            nc.vector.tensor_copy(w2h[0][:], ff2_w[:]).then_inc(ffw2_hi, 1)
            split_hidden(0, 0)
            nc.vector.tensor_copy(w1h[0][0:CH, 0:KC], ff1_w[:]).then_inc(ffw1_hi, 1)
            split_hidden(0, 1)
            for g in range(GROUPS):
                for m in range(KC):
                    take_ff2(0, g, m, lambda g, m, c, p: nc.vector.tensor_scalar(
                        ffo[:, m, c], p, vec("tok_ff2_b", m), None, ALU.add))
            dve.wait_ge(loaded["headmask"], 16)
            take_k(0, PATCHES, "tok_k_b", range(GROUPS * KC))

            def take_tok_proj(g, m):
                v, c = 2 * g + m + 1, cols(g, PATCHES)
                take_proj(0, PATCHES, g, m, lambda m, c, p: nc.vector.scalar_tensor_tensor(
                    x1[:, m, c], p, vec("tok_proj_b", m), id0[:, m, c], ALU.add, ALU.add))
                nc.vector.scalar_tensor_tensor(
                    xh[:, m, c], ps[0:CH, proj_bank(0, g, m), 0:GI * PATCHES], vec("tok_proj_b", m),
                    id0[:, m, c], ALU.add, ALU.add).then_inc(x1_hi, 1)
                dve.wait_ge(proj_taken, v)
                dve.wait_ge(x1_hi, v)
                nc.vector.tensor_tensor(xl[:, m, c], x1[:, m, c], xh[:, m, c].bitcast(F32),
                                        ALU.subtract).then_inc(x1_lo, 1)

            def first_half(take):
                take(0, 0)
                take(0, 1)

            dve.wait_ge(loaded["tok_v_bias"], 16)
            attention(0, PATCHES, "tok", lambda: first_half(take_tok_proj), lambda: None)
            take_tok_proj(1, 0)
            take_tok_proj(1, 1)
            h_img = h[:].rearrange("p k (b t) -> p k b t", t=TOKENS)
            nc.vector.tensor_copy(h_img[:, :, :, 0],
                                  vec("cls").unsqueeze(2).to_broadcast([CH, KC, IMAGES])).then_inc(cls_set, 1)

            def take_tokens(g, m):
                take_ff2(1, g, m, lambda g, m, c, p: nc.vector.scalar_tensor_tensor(
                    h_img[:, m, GI * g:GI * (g + 1), 1:TOKENS], p.rearrange("p (b t) -> p b t", t=PATCHES),
                    vec("tok_ff2_b", m), x1[:, m, c].rearrange("p (b t) -> p b t", t=PATCHES),
                    ALU.add, ALU.add))

            def feature(t):
                g, c = divmod(t, 2 * HC)
                dve.wait_ge(f_lin, t + 1)
                dst = fq if c < HC else fk
                nc.vector.tensor_tensor(dst[:, c % HC, cols(g, TOKENS)], flin[:, t % 2, :],
                                        ps[:, t % 4, 0:NG], ALU.mult).then_inc(f_done, 1)

            split_hidden(1, 0)
            split_hidden(1, 1)
            first_half(take_tokens)
            take_tokens(1, 0)
            dve.wait_ge(cls_set, 1)
            centre_tokens(1, TOKENS, h, 0)
            take_tokens(1, 1)
            scale_tokens(1, TOKENS, 0, nrm)
            centre_tokens(1, TOKENS, h, 1)
            feature(0)
            feature(1)
            scale_tokens(1, TOKENS, 1, nrm)
            for t in range(2, 2 * GROUPS * HC):
                feature(t)

            def spread_sums(n, half):
                dve.wait_ge(perf_otaken, n)
                if not (isinstance(n, int) and n == 1):
                    dve.wait_ge(perf_den, n - 1)
                if not (isinstance(n, int) and n < 3):
                    dve.wait_ge(perf_odone, n - 2)
                nc.vector.tensor_scalar(clamped[:], o_img[:, half], DENOM_EPS, None, ALU.max
                                        ).then_inc(clamp_done, 1)
                dve.wait_ge(consts_set, 4)
                dve.wait_ge(clamp_done, n)
                nc.vector.stream_shuffle(sums[:, half], clamped[:], shuffle).then_inc(perf_den, 1)

            def normalise(n, half):
                dve.wait_ge(perf_rden, n)
                if not (isinstance(n, int) and n == 1):
                    dve.wait_ge(perf_odone, n - 1)
                nc.vector.tensor_tensor(better[:], sums[:, half], rsums[:, half], ALU.mult).then_inc(perf_prod, 1)
                dve.wait_ge(perf_prod, n)
                nc.vector.scalar_tensor_tensor(better[:], better[:], 2.0, rsums[:, half], ALU.subtract,
                                               ALU.mult).then_inc(perf_better, 1)
                dve.wait_ge(perf_better, n)
                nc.vector.scalar_tensor_tensor(oT[:, :, bass.ds((n - 1) * TOKENS, TOKENS)], better[:], -1.0,
                                               o_img[:, half], ALU.mult, ALU.mult).then_inc(perf_odone, 1)

            def take_perf_proj(g, m):
                take_proj(1, TOKENS, g, m, lambda m, c, p: nc.vector.scalar_tensor_tensor(
                    h[:, m, c], p, vec("perf_proj_b", m), h[:, m, c], ALU.add, ALU.add))

            spread_sums(1, 0)
            spread_sums(2, 1)
            normalise(1, 0)
            with dve.Fori(2, IMAGES - 2, 2) as n:
                spread_sums(n + 1, 0)
                normalise(n, 1)
                spread_sums(n + 2, 1)
                normalise(n + 1, 0)
            spread_sums(IMAGES - 1, 0)
            normalise(IMAGES - 2, 1)
            first_half(take_perf_proj)
            normalise(IMAGES - 1, 0)
            spread_sums(IMAGES, 1)
            centre_tokens(2, TOKENS, h, 0)
            normalise(IMAGES, 1)

            def scale_twice(g):
                scale_tokens(2, TOKENS, g, z, rstd2, twice_rstd, g + 1)
                affine(2, g, "n1_w", "n1_b", nrm, aff)

            take_perf_proj(1, 0)
            take_perf_proj(1, 1)
            scale_twice(0)
            centre_tokens(2, TOKENS, h, 1)
            take_k(1, TOKENS, "ffn_k_b", [0])
            scale_twice(1)
            take_k(1, TOKENS, "ffn_k_b", range(1, GROUPS * KC))

            def take_ffn_proj(g, m):
                if g == m == 0:
                    dve.wait_ge(x2_ready, GROUPS)
                take_proj(2, TOKENS, g, m, lambda m, c, p: nc.vector.scalar_tensor_tensor(
                    xp[:, m, c], p, vec("ffn_proj_b", m), x2[:, m, c], ALU.add, ALU.add))

            dve.wait_ge(loaded["ffn_v_bias"], 16)
            attention(1, TOKENS, "ffn", lambda: first_half(take_ffn_proj),
                      lambda: centre_tokens(3, TOKENS, xp, 0))
            take_ffn_proj(1, 0)
            take_ffn_proj(1, 1)
            def rest_of_input(g):
                dve.wait_ge(xh_ready, g + 1)
                c = cols(g, TOKENS)
                nc.vector.tensor_tensor(x3[:, 2, c], x3f[:, 0, c], x3[:, 0, c].bitcast(F32), ALU.subtract)
                nc.vector.tensor_tensor(x3[TAIL:128, 1, c], x3f[0:TAIL, 1, c], x3[0:TAIL, 1, c].bitcast(F32),
                                        ALU.subtract).then_inc(xl_ready, 1)

            scale_tokens(3, TOKENS, 0)
            def experts_input(g):
                dve.wait_ge(ln_z, GROUPS * 3 + g + 1)
                c = cols(g, TOKENS)
                for dst, m, rows in ((x3f[0:CH, 0, c], 0, slice(0, CH)), (x3f[CH:128, 0, c], 1, slice(TAIL, CH)),
                                     (x3f[0:TAIL, 1, c], 1, slice(0, TAIL))):
                    last = nc.vector.tensor_scalar(dst, z[rows, m, c], vec("n2_w", m)[rows], vec("n2_b", m)[rows],
                                                   ALU.mult, ALU.add)
                last.then_inc(aff, 1)

            centre_tokens(3, TOKENS, xp, 1)
            experts_input(0)
            rest_of_input(0)
            scale_tokens(3, TOKENS, 1)
            experts_input(1)
            rest_of_input(1)

            steps = [0]

            def step(ins):
                steps[0] += 1
                ins.then_inc(gchain, 1)
                dve.wait_ge(gchain, steps[0])

            TT, EE = GATE_TILES, EXPERTS
            dve.wait_ge(gl_ready, 1)
            dve.wait_ge(loaded["earlier"], 16)
            step(nc.vector.tensor_copy(logit[:], ps[0:GATE_ROWS, 4, 0:TT * EE].rearrange("p (t e) -> p t e", e=EE)))
            other = logit[:].unsqueeze(2).to_broadcast([GATE_ROWS, TT, EE, EE])
            own_e = logit[:].unsqueeze(3).to_broadcast([GATE_ROWS, TT, EE, EE])
            step(nc.vector.tensor_reduce(gsum[:], logit[:], AXX, ALU.max))
            step(nc.vector.tensor_tensor(gates[:], logit[:],
                                         gsum[:].unsqueeze(2).to_broadcast([GATE_ROWS, TT, EE]), ALU.subtract))
            step(nc.vector.tensor_tensor(cmp_gt[:], other, own_e, ALU.is_gt))
            step(nc.vector.tensor_tensor(cmp_eq[:], other, own_e, ALU.is_equal))
            step(nc.vector.tensor_tensor(cmp_eq[:], cmp_eq[:],
                                         earlier[0:GATE_ROWS].unsqueeze(1).to_broadcast([GATE_ROWS, TT, EE, EE]),
                                         ALU.mult))
            step(nc.vector.tensor_tensor(cmp_gt[:], cmp_gt[:], cmp_eq[:], ALU.add))
            step(nc.vector.tensor_reduce(rank[:].rearrange("p (t e) -> p t e", e=EE), cmp_gt[:], AXX, ALU.add))
            step(nc.vector.tensor_scalar(rank[:], rank[:], 2.0, None, ALU.is_lt))
            dve.wait_ge(gexp, 1)
            step(nc.vector.tensor_tensor(gates[:], gates[:], rank[:].rearrange("p (t e) -> p t e", e=EE), ALU.mult))
            step(nc.vector.tensor_reduce(gsum[:], gates[:], AXX, ALU.add))
            step(nc.vector.reciprocal(gsum[:], gsum[:]))
            step(nc.vector.tensor_tensor(gates[:], gates[:],
                                         gsum[:].unsqueeze(2).to_broadcast([GATE_ROWS, TT, EE]), ALU.mult))
            dve.wait_ge(gt_ready, 1)
            n = 4 * GATE_ROWS
            nc.vector.tensor_copy(gates_T[:, 0:n], ps[0:EE, 5, 0:n]).then_inc(gt_taken, 1)
            nc.vector.tensor_copy(gates_T[:, n:ALL], ps[0:EE, 6, 0:GATE_ROWS]).then_inc(gt_taken, 1)

            for g in range(GROUPS):
                dve.wait_ge(g0_ready, g + 1)
                nc.vector.tensor_copy(gate_b[0][:, cols(g, TOKENS)], ps[:, 4 + 3 * g, 0:NG]).then_inc(g0_taken, 1)

            def gate(t, m, s):
                dve.wait_ge(e1_gelu, t + 1)
                nc.vector.tensor_tensor(gh[m % 2][:], hg[:, m, :], gate_b[s][:], ALU.mult).then_inc(gated, 1)

            def iteration(u, s, turn, last=False):
                for m in range(FC):
                    t = FC * u + m
                    if not (isinstance(t, int) and t == 0):
                        dve.wait_ge(h_lo, t)
                    if m < FC - 1:
                        gate(t + 1, m + 1, s)
                    elif not last:
                        dve.wait_ge(g_loaded[1 - s], 16 * (turn + 1))
                        gate(t + 1, 0, 1 - s)
                    dve.wait_ge(h_hi, t + 1)
                    nc.vector.tensor_tensor(hl[:, m, :], gh[m % 2][:], hh[:, m, :].bitcast(F32),
                                            ALU.subtract).then_inc(h_lo, 1)

            dve.wait_ge(g0_taken, GROUPS)
            gate(0, 0, 0)
            iteration(0, 0, 0)
            with dve.Fori(0, (EXPERTS - 2) // 2) as i:
                iteration(2 * i + 1, 1, i)
                iteration(2 * i + 2, 0, i + 1)
            iteration(EXPERTS - 1, 1, 0, last=True)

            dve.wait_ge(base_ready, 1)
            for g in range(GROUPS):
                for m in range(KC):
                    dve.wait_ge(y_ready, 2 * g + m + 1)
                    last = nc.vector.tensor_tensor(outbuf[:, m, cols(g, TOKENS)], h[:, m, cols(g, TOKENS)],
                                                   ps[0:CH, 4 + 2 * g + m, 0:NG], ALU.add)
                last.then_inc(out_ready, 1)

        @block.tensor
        def _(pe):
            def product(dst, pairs):
                for i, (lhsT, rhs) in enumerate(pairs):
                    last = nc.tensor.matmul(dst, lhsT, rhs, start=i == 0, stop=i == len(pairs) - 1)
                return last

            def keep_clock(bank, n):
                for _ in range(n):
                    nc.tensor.matmul(ps[0:CH, bank, 0:CH], mean_w[:], mean_w[:], start=True, stop=True)

            def means(n, T, src, g):
                product(ps[0:CH, mean_bank(n, g), 0:GI * T],
                        [(mean_w[:], src[:, k, cols(g, T)]) for k in range(KC)]).then_inc(ln_mean, 1)

            def variances(n, T, g):
                pe.wait_ge(ln_sq, GROUPS * n + g + 1)
                product(ps[0:CH, var_bank(n, g), 0:GI * T],
                        [(mean_w[:], sq[:, k, cols(g, T)]) for k in range(KC)]).then_inc(ln_var, 1)

            def then_layernorm(n, T, src, tile, taken, turns, begun=False, filler=None):
                if begun:
                    variances(n, T, 0)
                    tile(1, 0)
                    tile(1, 1)
                else:
                    tile(1, 0)
                    pe.wait_ge(taken, turns[0])
                    means(n, T, src, 0)
                    tile(1, 1)
                    variances(n, T, 0)
                pe.wait_ge(taken, turns[1])
                means(n, T, src, 1)
                if filler:
                    filler()
                variances(n, T, 1)

            def split_pairs(wh, wl, w, src, c):
                return [pair for k in range(src[0].shape[1]) for pair in
                        ((wh[:, k, w], src[0][:, k, c]), (wh[:, k, w], src[1][:, k, c]),
                         (wl[:, k, w], src[0][:, k, c]))]

            def ff1_tile(f, g, m, pairs):
                i = g * FC + m
                t = f * GROUPS * FC + i
                if i >= 4:
                    pe.wait_ge(ff1_gelu, t - 3)
                product(ps[:, FF1_0 + t % 4, 0:GI * PATCHES], pairs).then_inc(ff1_ready, 1)

            def first_ff1_tile(g, m):
                ff1_tile(0, g, m, [(ff1_w[:, k, m * 128:(m + 1) * 128], id0[:, k, cols(g, PATCHES)])
                                   for k in range(KC)])

            def second_ff1_tile(g, m):
                ff1_tile(1, g, m, split_pairs(w1h[0][0:CH], w1l[0][0:CH], slice(m * 128, (m + 1) * 128), (xh, xl),
                                              cols(g, PATCHES)))

            def ff2_tile(f, g, m):
                pe.wait_ge(hid_lo, (f * GROUPS + g + 1) * FC)
                product(ps[0:CH, 2 * g + m, 0:GI * PATCHES],
                        split_pairs(w2h[0], w2l[0], slice(m * CH, (m + 1) * CH), (hh, hl),
                                    cols(g, PATCHES))).then_inc(ff2_ready, 1)

            def queries_keys(a, blk, T, src, tiles):
                for i in tiles:
                    g, c = divmod(i, KC)
                    t = a * GROUPS * KC + i
                    if i >= 2:
                        pe.wait_ge(q_taken, t - 1)
                        pe.wait_ge(k_taken, t - 1)
                    for w, bank, done in ((wq, Q0 + t % 2, q_ready), (wk, K0 + t % 2, k_ready)):
                        product(ps[0:CH, bank, 0:GI * T],
                                [(w[blk][:, k, c * CH:(c + 1) * CH], src[:, k, cols(g, T)])
                                 for k in range(KC)]).then_inc(done, 1)

            def attention(a, k, T, blk, between=None):
                first = IMAGES * a

                def scores(n, half):
                    pe.wait_ge(q_copied, n + IMAGES * (k - a) + 1)
                    if not (isinstance(n, int) and n < first + 2):
                        pe.wait_ge(sub_done, n - 1)
                    for c in range(KC):
                        last = nc.tensor.matmul(
                            ps[0:T, 2 * half + c, 0:HQ * T].rearrange("p (h t) -> p h t", t=T),
                            q_img[0:CH, c, 0:T], kbd[:, c, :, bass.ds((n - first) * T, T)],
                            start=True, stop=True)
                    last.then_inc(s_ready, 1)

                def vals(n):
                    pe.wait_ge(x_copied, n + IMAGES * (k - a) + 1)
                    if not (isinstance(n, int) and n == 0):
                        pe.wait_ge(v_taken, n)
                    product(ps[0:T, VB, 0:D],
                            [(x_img[:, c, 0:T], wv[blk][:, c, :]) for c in range(KC)]).then_inc(v_ready, 1)

                def transposes(n):
                    have("ident")
                    pe.wait_ge(exp_done, n + 1)
                    if not (isinstance(n, int) and n == 0):
                        pe.wait_ge(pt_taken, n)
                    for i in range(HEADS):
                        j, o = divmod(i, HEADS // 2)
                        last = nc.tensor.transpose(ps[0:T, PT0 + j, o * T:(o + 1) * T], eprob[0:T, i, 0:T],
                                                   ident[0:T, 0:T])
                    last.then_inc(pt_ready, 1)

                def output_free(n1):
                    if not (isinstance(n1, int) and n1 == 1):
                        pe.wait_ge(o_done, n1 - 1)

                def weigh(n1):
                    pe.wait_ge(consts_set, 1)
                    pe.wait_ge(pt_taken, n1)
                    pe.wait_ge(v_taken, n1)
                    for i in range(HEADS):
                        c, j = divmod(i, HPC)
                        last = nc.tensor.matmul(ps[PAD * j:PAD * (j + 1), OB, c * T:(c + 1) * T],
                                                vpad[0:T, i, :], probT[0:T, i, 0:T], start=True, stop=True)
                    last.then_inc(o_ready, 1)

                def step(n, half, last=False):
                    if not last:
                        scores(n + 1, half)
                    output_free(n)
                    vals(n)
                    weigh(n)
                    transposes(n)

                pe.wait_ge(k_taken, KC * (GROUPS * a + 1))
                scores(first, 0)
                pe.wait_ge(k_taken, KC * GROUPS * (a + 1))
                scores(first + 1, 1)
                vals(first)
                transposes(first)
                step(first + 1, 0)
                with pe.Fori(first + 2, first + IMAGES - 2, 2) as n:
                    step(n, 1)
                    step(n + 1, 0)
                step(first + IMAGES - 2, 1)
                pe.wait_ge(o_done, first + GI)
                project(k, blk, T, 0, 0)
                project(k, blk, T, 0, 1)
                step(first + IMAGES - 1, 0, last=True)
                if between:
                    between()
                output_free(first + IMAGES)
                weigh(first + IMAGES)

            def project(p, blk, T, g, m):
                product(ps[0:CH, proj_bank(p, g, m), 0:GI * T],
                        [(wo[blk][:, c, m * CH:(m + 1) * CH], oT[:, c, cols(g, T)])
                         for c in range(HC)]).then_inc(proj_ready, 1)

            def have(*names):
                for name in names:
                    pe.wait_ge(loaded[name], 16)

            def patch_sums(i, g):
                for m in range(KC):
                    for k in range(2 * i, 2 * i + 2):
                        last = nc.tensor.matmul(ps[0:CH, PATCH0 + 2 * g + m, 0:GI * PATCHES],
                                                patch_w[:, k, m * CH:(m + 1) * CH],
                                                patches[:, k, cols(g, PATCHES)], start=k == 0, stop=k == FC - 1)
                    if i == PS - 1:
                        last.then_inc(patch_ready, 1)

            for i in range(PS):
                have(f"patch_w{i}", f"patches{i}_0")
                patch_sums(i, 0)
            for i in range(PS):
                have(f"patches{i}_1")
                patch_sums(i, 1)
                if i == 0:
                    have("mean_w")
                    pe.wait_ge(tokx_ready, 1)
                    means(0, PATCHES, tokx, 0)
                elif i == 1:
                    variances(0, PATCHES, 0)
            pe.wait_ge(tokx_ready, 2)
            means(0, PATCHES, tokx, 1)
            have("ff1_w")
            pe.wait_ge(id0_ready, 1)
            for m in range(FC):
                if m == 2:
                    variances(0, PATCHES, 1)
                first_ff1_tile(0, m)
            pe.wait_ge(id0_ready, 2)
            for m in range(FC):
                first_ff1_tile(1, m)
            pe.wait_ge(ffw2_lo, 1)
            for g in range(GROUPS):
                for m in range(KC):
                    ff2_tile(0, g, m)
            have("tok_wq", "tok_wk", "tok_wv", "tok_wo", "ident", "cols128")
            for g in range(GROUPS):
                pe.wait_ge(ff2_taken, 2 * (g + 1))
                queries_keys(0, "tok", PATCHES, ffo, range(KC * g, KC * (g + 1)))
            attention(0, 0, PATCHES, "tok")
            pe.wait_ge(ffw1_lo, 1)
            pe.wait_ge(x1_lo, KC)
            for m in range(3):
                second_ff1_tile(0, m)
            pe.wait_ge(o_done, IMAGES)
            project(0, "tok", PATCHES, 1, 0)
            project(0, "tok", PATCHES, 1, 1)
            for m in range(3, FC):
                second_ff1_tile(0, m)
            pe.wait_ge(x1_lo, 2 * KC)
            for m in range(FC):
                second_ff1_tile(1, m)
            ff2_tile(1, 0, 0)
            ff2_tile(1, 0, 1)

            have("perf_wq", "perf_wk", "rand_w", "perf_wv", "perf_wo")

            def feature_product(t):
                g, c = divmod(t, 2 * HC)
                if t >= 4:
                    pe.wait_ge(f_done, t - 3)
                w = wq["perf"] if c < HC else wk["perf"]
                o = (c % HC) * 128
                product(ps[:, t % 4, 0:NG], [(w[:, k, o:o + 128], nrm[:, k, cols(g, TOKENS)])
                                             for k in range(KC)]).then_inc(f_ready, 1)

            def first_features():
                pe.wait_ge(ln_z, GROUPS + 1)
                feature_product(0)
                feature_product(1)

            pe.wait_ge(cls_set, 1)
            then_layernorm(1, TOKENS, h, lambda g, m: ff2_tile(1, g, m), ff2_taken, (6, 8),
                           filler=first_features)
            for t in range(2, 2 * GROUPS * HC):
                if t == 2 * HC:
                    pe.wait_ge(ln_z, 2 * GROUPS)
                feature_product(t)
            for g in range(GROUPS):
                pe.wait_ge(f_done, 2 * HC * g + HC)
                for c in range(HC):
                    t = HC * g + c
                    if t >= 2:
                        pe.wait_ge(qf_done, t - 1)
                    product(ps[:, 4 + t % 2, 0:NG],
                            [(rand_w[:, c, :], fq[:, c, cols(g, TOKENS)])]).then_inc(qf_ready, 1)

            def key_logits(b, half):
                pe.wait_ge(q_copied, IMAGES + b + 1)
                if not (isinstance(b, int) and b < 2):
                    pe.wait_ge(kf_done, b - 1)
                for c in range(HC):
                    last = nc.tensor.matmul(ps[0:TOKENS, KLB[half], c * 128:(c + 1) * 128], q_img[:, c, :],
                                            rand_w[:, c, :], start=True, stop=True)
                last.then_inc(kl_ready, 1)

            def perf_values(b):
                pe.wait_ge(x_copied, IMAGES + b + 1)
                if not (isinstance(b, int) and b == 0):
                    pe.wait_ge(perf_vtaken, b)
                product(ps[0:TOKENS, PVB, 0:D],
                        [(x_img[:, c], wv["perf"][:, c, :]) for c in range(KC)]).then_inc(perf_vready, 1)

            def keys_values(b, half):
                pe.wait_ge(kf_done, b + 1)
                pe.wait_ge(perf_vtaken, b + 1)
                for c in range(HC):
                    last = nc.tensor.matmul(ps[:, KVB, c * 128:(c + 1) * 128],
                                            kfeat[:, half, c * 128:(c + 1) * 128],
                                            vpad[:, c * HPC:(c + 1) * HPC, :], start=True, stop=True)
                last.then_inc(kv_ready, 1)

            def perf_out(n):
                pe.wait_ge(kv_taken, n)
                if not (isinstance(n, int) and n == 1):
                    pe.wait_ge(perf_otaken, n - 1)
                for c in range(HC):
                    last = nc.tensor.matmul(ps[:, POB, c * TOKENS:(c + 1) * TOKENS], kvbd[:, c, :],
                                            qT[:, c, bass.ds((n - 1) * TOKENS, TOKENS)],
                                            start=True, stop=True)
                last.then_inc(perf_oready, 1)

            pe.wait_ge(f_done, 2 * GROUPS * HC)
            key_logits(0, 0)
            perf_values(0)

            def perf_step(b, half, last=False):
                if not last:
                    key_logits(b + 1, 1 - half)
                    perf_values(b + 1)
                if not (isinstance(b, int) and b == 0):
                    perf_out(b)
                keys_values(b, half)

            perf_step(0, 0)
            pe.wait_ge(qf_done, GROUPS * HC)
            perf_step(1, 1)
            with pe.Fori(2, IMAGES - 2, 2) as b:
                perf_step(b, 0)
                perf_step(b + 1, 1)
            perf_step(IMAGES - 2, 0)
            pe.wait_ge(perf_odone, GI)
            project(1, "perf", TOKENS, 0, 0)
            perf_step(IMAGES - 1, 1, last=True)
            project(1, "perf", TOKENS, 0, 1)
            perf_out(IMAGES)
            pe.wait_ge(proj_taken, 4 + KC)
            means(2, TOKENS, h, 0)
            keep_clock(proj_bank(1, 1, 0), 8)

            have("ffn_wq", "ffn_wk", "ffn_wv", "ffn_wo", "w_gate", "b2")
            def first_queries_keys():
                pe.wait_ge(aff, 1)
                queries_keys(1, "ffn", TOKENS, nrm, [0])

            def last_perf_proj(g, m):
                pe.wait_ge(perf_odone, IMAGES)
                project(1, "perf", TOKENS, g, m)

            then_layernorm(2, TOKENS, h, last_perf_proj, proj_taken, (6, 8), begun=True,
                           filler=first_queries_keys)
            queries_keys(1, "ffn", TOKENS, nrm, range(1, KC))
            pe.wait_ge(aff, GROUPS)
            queries_keys(1, "ffn", TOKENS, nrm, range(KC, GROUPS * KC))
            def first_group_means():
                pe.wait_ge(proj_taken, 8 + KC)
                means(3, TOKENS, xp, 0)

            attention(1, 2, TOKENS, "ffn", first_group_means)

            def logits(tiles):
                for t in tiles:
                    last = product(ps[0:GATE_ROWS, 4, t * EXPERTS:(t + 1) * EXPERTS],
                                   [(x3f[rows, k, t * GATE_ROWS:(t + 1) * GATE_ROWS], w_gate[rows, k, :])
                                    for k, rows in enumerate((slice(0, 128), slice(0, TAIL)))])
                return last

            def last_ffn_proj(g, m):
                pe.wait_ge(o_done, 2 * IMAGES)
                project(2, "ffn", TOKENS, g, m)

            then_layernorm(3, TOKENS, xp, last_ffn_proj, proj_taken, (10, 12), begun=True,
                           filler=lambda: keep_clock(0, 9))
            pe.wait_ge(aff, GROUPS + 1)
            logits(range(NG // GATE_ROWS))
            keep_clock(0, 3)
            def gates_by_expert():
                pe.wait_ge(gchain, 13)
                for t in range(GATE_TILES):
                    bank, o = (5, t * GATE_ROWS) if t < 4 else (6, 0)
                    last = nc.tensor.transpose(ps[0:EXPERTS, bank, o:o + GATE_ROWS], gates[:, t, :],
                                               ident[0:GATE_ROWS, 0:GATE_ROWS])
                last.then_inc(gt_ready, 1)

            def first_gates():
                pe.wait_ge(gt_taken, 2)
                for g in range(GROUPS):
                    nc.tensor.matmul(ps[:, 4 + 3 * g, 0:NG], ones_row[:], gates_T[0:1, cols(g, TOKENS)],
                                     start=True, stop=True).then_inc(g0_ready, 1)

            def second_biases():
                pe.wait_ge(g0_taken, GROUPS)
                for g in range(GROUPS):
                    for m in range(KC):
                        nc.tensor.matmul(ps[0:CH, 4 + 2 * g + m, 0:NG], b2[:, m * CH:(m + 1) * CH],
                                         gates_T[:, cols(g, TOKENS)], start=True, stop=False)

            def first_layer(u, s, m, groups=range(GROUPS)):
                t = FC * u + m
                if not (isinstance(t, int) and t < 2):
                    pe.wait_ge(e1_gelu, t - 1)
                p = 2 * (m % 2)
                w = slice(m * 128, (m + 1) * 128)
                for g in groups:
                    c = cols(g, TOKENS)
                    last = product(ps[:, p + g, 0:NG],
                                   [(w1h[s][:, k % WT, w], x3[:, k, c]) for k in range(XT)] +
                                   [(w1l[s][:, 0, w], x3[:, 0, c]), (w1l[s][0:TAIL, 1, w], x3[0:TAIL, 1, c])])
                if groups[-1] != GROUPS - 1:
                    return
                last.then_inc(e1_ready, 1)

            def second_layer(u, s, m, last_expert=False):
                pe.wait_ge(h_lo, FC * u + m + 1)
                for g in range(GROUPS):
                    c = cols(g, TOKENS)
                    for o in range(KC):
                        w = slice(o * CH, (o + 1) * CH)
                        dst = ps[0:CH, 4 + 2 * g + o, 0:NG]
                        end = last_expert and m == FC - 1
                        nc.tensor.matmul(dst, w2h[s][:, m, w], hh[:, m, c], start=False, stop=False)
                        nc.tensor.matmul(dst, w2h[s][:, m, w], hl[:, m, c], start=False, stop=False)
                        last = nc.tensor.matmul(dst, w2l[s][:, m, w], hh[:, m, c], start=False, stop=end)
                        if end:
                            last.then_inc(y_ready, 1)
                return last

            def iteration(u, s):
                for split in w1_lo:
                    pe.wait_ge(split, u + 1)
                for m in range(FC):
                    first_layer(u, s, m)
                    if m == 0:
                        if not isinstance(u, int):
                            second_layer(u - 2, s, FC - 1)
                        continue
                    if m == 1:
                        pe.wait_ge(w2_lo, u)
                        if isinstance(u, int):
                            second_biases()
                    last = second_layer(u - 1, 1 - s, m - 1)
                return last

            for split in w1_lo:
                pe.wait_ge(split, 1)
            pe.wait_ge(xl_ready, 1)
            first_layer(0, 0, 0, [0])
            first_layer(0, 0, 1, [0])
            keep_clock(2 + 1, 3)
            pe.wait_ge(aff, 2 * GROUPS)
            logits(range(NG // GATE_ROWS, GATE_TILES)).then_inc(gl_ready, 1)

            pe.wait_ge(xl_ready, 2)
            for m in range(FC):
                first_layer(0, 0, m, [1] if m < 2 else range(GROUPS))
                if m == FC - 2:
                    gates_by_expert()
            first_gates()
            iteration(1, 1)
            with pe.Fori(1, EXPERTS // 2) as i:
                iteration(2 * i, 0)
                iteration(2 * i + 1, 1).then_inc(hidden_read, 1)
            second_layer(EXPERTS - 2, 0, FC - 1).then_inc(hidden_read, 1)
            pe.wait_ge(w2_lo, EXPERTS)
            for m in range(FC):
                second_layer(EXPERTS - 1, 1, m, last_expert=True)


def positions():
    p = np.arange(PATCHES, dtype=np.float32)[:, None]
    i = np.arange(D // 2, dtype=np.float32)[None, :]
    angle = (p / np.power(np.float32(10000.0), np.float32(2.0) * i / np.float32(D))).astype(np.float32)
    table = np.zeros((PATCHES, D), np.float32)
    table[:, 0::2] = np.sin(angle)
    table[:, 1::2] = np.cos(angle)
    return table


def layout(a):
    def rows(w, part):
        return w.reshape(-1, part, w.shape[-1]).transpose(1, 0, 2)

    def twice(w):
        w = w.reshape(D, HEADS, HD)
        return rows(np.concatenate([w, w], axis=2).reshape(D, HEADS * PAD), CH)

    def pad_rows(w):
        out = np.zeros((HEADS, PAD, D), np.float32)
        out[:, :HD] = w.reshape(HEADS, HD, D)
        return rows(out.reshape(HEADS * PAD, D), 128)

    o = {}
    x = a["x"].reshape(IMAGES, 3, 8, 16, 8, 16)
    o["patches"] = rows(x.transpose(1, 3, 5, 0, 2, 4).reshape(HIDDEN, IMAGES * PATCHES), 128)
    o["patch_w"] = rows(a["L0_tok_patch_w"].reshape(D, HIDDEN).T, 128)
    o["ff1_w"] = rows(a["L0_tok_ff1_w"], CH)
    o["ff2_w"] = rows(a["L0_tok_ff2_w"], 128)
    for blk, w, p in (("tok", a["L0_tok_qkv_w"], a["L0_tok_proj_w"]),
                      ("perf", a["L0_attn_qkv_w"].T, a["L0_attn_proj_w"].T),
                      ("ffn", a["L0_ffn_qkv_w"].T, a["L0_ffn_proj_w"].T)):
        cut = twice if blk == "perf" else (lambda m: rows(m, CH))
        o[f"{blk}_wq"] = cut(w[:, 0:D])
        o[f"{blk}_wk"] = cut(w[:, D:2 * D])
        o[f"{blk}_wv"] = rows(w[:, 2 * D:3 * D], CH)
        o[f"{blk}_wo"] = pad_rows(p)
    r = np.zeros((HC, HPC, PAD, HPC, FEATURES), np.float32)
    for i in range(HEADS):
        c, j = divmod(i, HPC)
        r[c, j, :HD, j] = a["L0_attn_rand_matrix"][i]
        r[c, j, HD:, j] = 1.0
    o["rand_w"] = r.reshape(HC, 128, 128).transpose(1, 0, 2)
    o["w_gate"] = rows(a["L0_ffn_w_gate"][ROWS0 + ROWS1 + ROWS1], 128)
    o["b2"] = a["L0_ffn_b2"]
    w1 = a["L0_ffn_W1"][:, ROWS0 + ROWS1 + ROWS1]
    o["w1"] = w1.reshape(EXPERTS, WT, 128, HIDDEN).transpose(0, 2, 1, 3)
    o["w2"] = a["L0_ffn_W2"].reshape(EXPERTS, FC, 128, D).transpose(0, 2, 1, 3)
    v96 = {"patch_b": a["L0_tok_patch_b"], "tok_ln_g": a["L0_tok_ln_g"], "tok_ln_b": a["L0_tok_ln_b"],
           "tok_ff2_b": a["L0_tok_ff2_b"], "tok_proj_b": a["L0_tok_proj_b"],
           "perf_proj_b": a["L0_attn_proj_b"], "n1_w": a["L0_ffn_norm1_w"], "n1_b": a["L0_ffn_norm1_b"],
           "ffn_proj_b": a["L0_ffn_proj_b"], "n2_w": a["L0_ffn_norm2_w"], "n2_b": a["L0_ffn_norm2_b"],
           "cls": a["cls_tok"]}
    for blk, bias in (("tok", a["L0_tok_qkv_b"]), ("ffn", a["L0_ffn_qkv_b"])):
        v96[f"{blk}_q_b"], v96[f"{blk}_k_b"] = bias[0:D], bias[D:2 * D]
    o["cols96"] = np.concatenate([v96[n].reshape(KC, CH).T for n in COLS96], axis=1)
    upper = (np.arange(128) % PAD >= HD)[:, None]
    v128 = {"tok_ff1_b": a["L0_tok_ff1_b"].reshape(FC, 128).T,
            "b1": a["L0_ffn_b1"].reshape(EXPERTS * FC, 128).T,
            "feat_add": np.where(upper, 0.0, SCALE ** 0.5).astype(np.float32),
            "feat_mul": np.where(upper, -0.5 * SCALE, 0.0).astype(np.float32)}
    for blk, bias in (("tok", a["L0_tok_qkv_b"]), ("ffn", a["L0_ffn_qkv_b"])):
        o[f"{blk}_v_bias"] = bias[None, 2 * D:].reshape(1, HEADS, HD)
    o["cols128"] = np.concatenate([v128[n] for n, _ in COLS128], axis=1)
    head = np.arange(CH) // HD
    o["ident"] = np.eye(128, dtype=np.float32)
    o["headmask"] = (head[:, None] == np.arange(HQ)[None, :]).astype(np.float32)
    e = np.arange(EXPERTS)
    o["earlier"] = np.broadcast_to((e[None, :] < e[:, None]).astype(np.float32), (128, EXPERTS, EXPERTS))
    o["pos"] = rows(positions().T, CH)
    o["mean_w"] = np.full((CH, CH), 1.0 / D, np.float32)
    return {k: np.ascontiguousarray(v, dtype=np.float32) for k, v in o.items()}


def kernel(**inputs):
    import concourse.bacc as _bacc
    from concourse.bass_utils import run_bass_kernel_spmd as _run

    nc = _bacc.Bacc("TRN2", target_bir_lowering=False, num_devices=1)
    arrays, dram = {}, {}
    for name, v in layout({k: np.asarray(v) for k, v in inputs.items()}).items():
        arrays[f"in_{name}"] = v
        dram[name] = nc.dram_tensor(f"in_{name}", v.shape, F32, kind="ExternalInput").ap()
    out = nc.dram_tensor("out_tokens", (CH, KC, ALL), F32, kind="ExternalOutput").ap()
    build_tower(nc, dram, out)
    got = _run(nc, [arrays], core_ids=[0]).results[0]["out_tokens"]
    return np.ascontiguousarray(np.asarray(got).transpose(2, 1, 0).reshape(IMAGES, TOKENS, D))
```
